# Optimizing a Trainium2 kernel written in Bass

```python
import numpy as np
import jax
import jax.numpy as jnp

def _softmax(x, axis=-1):
    return jax.nn.softmax(x, axis=axis)

def _gelu(x):
    return jax.nn.gelu(x, approximate=True)

def _silu(x):
    return jax.nn.silu(x)

def _sigmoid(x):
    return jax.nn.sigmoid(x)

def _layernorm(x, axis=-1, eps=1e-05):
    m = jnp.mean(x, axis=axis, keepdims=True)
    v = jnp.var(x, axis=axis, keepdims=True)
    return (x - m) / jnp.sqrt(v + eps)

def _scatter_add(tgt, idx, src, axis=0):
    return tgt.at[idx].add(src)

def _segment_sum(src, seg, n):
    return jax.ops.segment_sum(src, seg, n)
kernel_name = 'mk_adj_preln_d4_adj_r2_e1b605'

def setup_inputs(seed: int=0):
    np.random.seed(seed)
    _w = jnp.asarray

    def _rec_inputs():
        import jax
        import jax.numpy as jnp
        _gk = jax.random.key(seed)
        x = -0.000125 + 0.9999 * jax.random.normal(jax.random.fold_in(_gk, 1), (128, 128, 128), jnp.float32)
        _a = jax.random.bernoulli(jax.random.fold_in(_gk, 2), 0.0625, (128, 128))
        _a = jnp.logical_or(_a, jnp.swapaxes(_a, -1, -2))
        _a = jnp.logical_or(_a, jnp.eye(128, dtype=bool))
        _af = _a.astype(jnp.float32)
        _af = _af * jax.random.uniform(jax.random.fold_in(_gk, 3), (128, 128), jnp.float32, 0.05, 0.000488281)
        adj = _af
        return (x, adj)
    x, adj = _rec_inputs()

    def _L0_gnn_setup():
        import jax, jax.numpy as jnp
        import numpy as np
        B, T, D, H = (64, 1024, 128, 128)
        MAX_SKIP = 4

        def _lstm_last(Wih, Whh, bih, bhh, xs):
            N, _, Hd = xs.shape
            bias = bih + bhh

            def step(carry, x_t):
                h, c = carry
                g = x_t @ Wih.T + h @ Whh.T + bias
                i, f, gg, o = jnp.split(g, 4, axis=-1)
                c = jax.nn.sigmoid(f) * c + jax.nn.sigmoid(i) * jnp.tanh(gg)
                h = jax.nn.sigmoid(o) * jnp.tanh(c)
                return ((h, c), None)
            init = (jnp.zeros((N, Hd), xs.dtype), jnp.zeros((N, Hd), xs.dtype))
            (h_last, _), _ = jax.lax.scan(step, init, jnp.swapaxes(xs, 0, 1))
            return h_last
        key = jax.random.key(seed)
        ks = jax.random.split(key, 8)
        s = 0.05
        x = jax.random.normal(ks[0], (B, T, D), jnp.float32)
        adj = jax.random.uniform(ks[1], (T, T), jnp.float32) / T
        Wg0 = jax.random.normal(ks[2], (D, H), jnp.float32) * s
        bg0 = jnp.zeros((H,), jnp.float32)
        Wg1 = jax.random.normal(ks[3], (H, H), jnp.float32) * s
        bg1 = jnp.zeros((H,), jnp.float32)
        Wih = jax.random.normal(ks[4], (MAX_SKIP, 4 * H, H), jnp.float32) * s
        Whh = jax.random.normal(ks[5], (MAX_SKIP, 4 * H, H), jnp.float32) * s
        bih = jax.random.normal(ks[6], (MAX_SKIP, 4 * H), jnp.float32) * s
        bhh = jax.random.normal(ks[7], (MAX_SKIP, 4 * H), jnp.float32) * s
        return dict(x=x, adj=adj, Wg0=Wg0, bg0=bg0, Wg1=Wg1, bg1=bg1, Wih=Wih, Whh=Whh, bih=bih, bhh=bhh)
    _L0_gnn_all = _L0_gnn_setup()
    _L0_gnn_in = {k: v for k, v in _L0_gnn_all.items() if k in ('Wg0', 'bg0', 'Wg1', 'bg1', 'Wih', 'Whh', 'bih', 'bhh')}
    del _L0_gnn_all

    def _L1_gnn_setup():
        import jax, jax.numpy as jnp
        import numpy as np
        NEG = -1e+30
        key = jax.random.key(seed)
        ks = jax.random.split(key, 4)
        B, T, C = (4, 2048, 128)
        x = jax.random.normal(ks[0], (B, T, C), dtype=jnp.float32)
        adj_mask = jax.random.normal(ks[1], (T, T), dtype=jnp.float32)
        Wqkv = jax.random.normal(ks[2], (C, 3 * C), dtype=jnp.float32) * (1.0 / np.sqrt(C))
        Wo = jax.random.normal(ks[3], (C, C), dtype=jnp.float32) * (1.0 / np.sqrt(C))
        return {'x': x, 'adj_mask': adj_mask, 'Wqkv': Wqkv, 'Wo': Wo}
    _L1_gnn_all = _L1_gnn_setup()
    _L1_gnn_in = {k: v for k, v in _L1_gnn_all.items() if k in ('Wqkv', 'Wo')}
    del _L1_gnn_all

    def _L2_gnn_setup():
        import jax, jax.numpy as jnp
        import numpy as np
        B, J, F_IN, F_OUT = (8192, 17, 128, 128)
        key = jax.random.key(seed)
        k1, k2, k3, k4 = jax.random.split(key, 4)
        gain = 1.414
        bound = gain * np.sqrt(6.0 / (F_IN + F_OUT))
        W = jax.random.uniform(k2, (3, F_IN, F_OUT), dtype=jnp.float32, minval=-bound, maxval=bound)
        stdv = 1.0 / np.sqrt(F_OUT)
        bias = jax.random.uniform(k4, (F_OUT,), dtype=jnp.float32, minval=-stdv, maxval=stdv)
        return {'x': jax.random.normal(k1, (B, J, F_IN), dtype=jnp.float32), 'W': W, 'adj': jax.random.uniform(k3, (J, J), dtype=jnp.float32), 'bias': bias}
    _L2_gnn_all = _L2_gnn_setup()
    _L2_gnn_in = {k: v for k, v in _L2_gnn_all.items() if k in ('W', 'bias')}
    del _L2_gnn_all

    def _L3_gnn_setup():
        import jax, jax.numpy as jnp
        import numpy as np
        BT, N, D, HEADS, E = (512, 64, 128, 4, 256)
        LRELU_SLOPE = 0.2
        EPS = 1e-08
        key = jax.random.key(seed)
        ks = jax.random.split(key, 8)
        d = D
        return {'H': jax.random.normal(ks[0], (BT, N, d), jnp.float32), 'W_lin': jax.random.normal(ks[1], (d, d), jnp.float32) / np.sqrt(d).astype(np.float32), 'W_val': jax.random.normal(ks[2], (d, d), jnp.float32) / np.sqrt(d).astype(np.float32), 'a': jax.random.normal(ks[3], (HEADS, d // HEADS), jnp.float32), 'W_out': jax.random.normal(ks[4], (d, d), jnp.float32) / np.sqrt(d).astype(np.float32), 'A0': jax.random.uniform(ks[5], (N, N), jnp.float32), 'src': jax.random.randint(ks[6], (E,), 0, N, jnp.int32), 'dst': jax.random.randint(ks[7], (E,), 0, N, jnp.int32)}
    _L3_gnn_all = _L3_gnn_setup()
    _L3_gnn_in = {k: v for k, v in _L3_gnn_all.items() if k in ('W_lin', 'W_val', 'a', 'W_out', 'src', 'dst')}
    del _L3_gnn_all
    return {'x': x, 'adj': adj, 'L0_gnn_Wg0': _L0_gnn_in['Wg0'], 'L0_gnn_bg0': _L0_gnn_in['bg0'], 'L0_gnn_Wg1': _L0_gnn_in['Wg1'], 'L0_gnn_bg1': _L0_gnn_in['bg1'], 'L0_gnn_Wih': _L0_gnn_in['Wih'], 'L0_gnn_Whh': _L0_gnn_in['Whh'], 'L0_gnn_bih': _L0_gnn_in['bih'], 'L0_gnn_bhh': _L0_gnn_in['bhh'], 'L1_gnn_Wqkv': _L1_gnn_in['Wqkv'], 'L1_gnn_Wo': _L1_gnn_in['Wo'], 'L2_gnn_W': _L2_gnn_in['W'], 'L2_gnn_bias': _L2_gnn_in['bias'], 'L3_gnn_W_lin': _L3_gnn_in['W_lin'], 'L3_gnn_W_val': _L3_gnn_in['W_val'], 'L3_gnn_a': _L3_gnn_in['a'], 'L3_gnn_W_out': _L3_gnn_in['W_out'], 'L3_gnn_src': _L3_gnn_in['src'], 'L3_gnn_dst': _L3_gnn_in['dst']}

def reference(x, adj, L0_gnn_Wg0, L0_gnn_bg0, L0_gnn_Wg1, L0_gnn_bg1, L0_gnn_Wih, L0_gnn_Whh, L0_gnn_bih, L0_gnn_bhh, L1_gnn_Wqkv, L1_gnn_Wo, L2_gnn_W, L2_gnn_bias, L3_gnn_W_lin, L3_gnn_W_val, L3_gnn_a, L3_gnn_W_out, L3_gnn_src, L3_gnn_dst):
    import jax
    import jax.numpy as jnp

    def _L0_gnn_ref(x, adj, Wg0, bg0, Wg1, bg1, Wih, Whh, bih, bhh):
        import jax, jax.numpy as jnp
        import numpy as np
        B, T, D, H = (64, 1024, 128, 128)
        MAX_SKIP = 4

        def _lstm_last(Wih, Whh, bih, bhh, xs):
            N, _, Hd = xs.shape
            bias = bih + bhh

            def step(carry, x_t):
                h, c = carry
                g = x_t @ Wih.T + h @ Whh.T + bias
                i, f, gg, o = jnp.split(g, 4, axis=-1)
                c = jax.nn.sigmoid(f) * c + jax.nn.sigmoid(i) * jnp.tanh(gg)
                h = jax.nn.sigmoid(o) * jnp.tanh(c)
                return ((h, c), None)
            init = (jnp.zeros((N, Hd), xs.dtype), jnp.zeros((N, Hd), xs.dtype))
            (h_last, _), _ = jax.lax.scan(step, init, jnp.swapaxes(xs, 0, 1))
            return h_last
        h = jax.nn.relu(jnp.einsum('ts,bsh->bth', adj, x @ Wg0 + bg0))
        h = jax.nn.relu(jnp.einsum('ts,bsh->bth', adj, h @ Wg1 + bg1))
        Bv, Tv, Hd = h.shape
        for p in range(1, MAX_SKIP + 1):
            nw = Tv // p
            wins = h[:, :nw * p, :].reshape(Bv * nw, p, Hd)
            last = _lstm_last(Wih[p - 1], Whh[p - 1], bih[p - 1], bhh[p - 1], wins)
            idx = jnp.arange(nw) * p + (p - 1)
            h = h.at[:, idx, :].set(last.reshape(Bv, nw, Hd))
        return h

    def _L1_gnn_ref(x, adj_mask, Wqkv, Wo):
        import jax, jax.numpy as jnp
        import numpy as np
        NEG = -1e+30
        B, T, C = x.shape
        qkv = x @ Wqkv
        q, k, v = jnp.split(qkv, 3, axis=-1)
        scale = 1.0 / jnp.sqrt(jnp.asarray(C, dtype=x.dtype))
        scores = jnp.einsum('btd,bsd->bts', q, k) * scale + adj_mask
        causal = jnp.tril(jnp.ones((T, T), dtype=bool))
        scores = jnp.where(causal, scores, NEG)
        attn = jax.nn.softmax(scores, axis=-1)
        y = jnp.einsum('bts,bsd->btd', attn, v)
        return y @ Wo

    def _L2_gnn_ref(x, W, adj, bias):
        import jax, jax.numpy as jnp
        import numpy as np
        B, J, F_IN, F_OUT = (8192, 17, 128, 128)
        adj_0 = jnp.diag(jnp.diagonal(adj))
        adj_1 = jnp.triu(adj, k=1)
        adj_2 = jnp.tril(adj, k=-1)
        h = jnp.einsum('bjf,kfo->kbjo', x, W)
        out = jnp.einsum('ij,bjo->bio', adj_0, h[0]) + jnp.einsum('ij,bjo->bio', adj_1, h[1]) + jnp.einsum('ij,bjo->bio', adj_2, h[2])
        return out + bias[None, None, :]

    def _L3_gnn_ref(H, W_lin, W_val, a, W_out, A0, src, dst):
        import jax, jax.numpy as jnp
        import numpy as np
        BT, N, D, HEADS, E = (512, 64, 128, 4, 256)
        LRELU_SLOPE = 0.2
        EPS = 1e-08
        bt, n, d = H.shape
        h, dh = a.shape
        Xq = (H @ W_lin.T).reshape(bt, n, h, dh)
        Xv = (H @ W_val.T).reshape(bt, n, h, dh)
        Qs = Xq[:, src]
        Kt = Xq[:, dst]
        e = jnp.einsum('behd,hd->beh', jax.nn.leaky_relu(Qs + Kt, LRELU_SLOPE), a)
        e = e + jnp.log(A0[src, dst] + EPS)[None, :, None]
        e_t = e.transpose(1, 0, 2)
        m = jax.ops.segment_max(e_t, src, num_segments=n)
        ex = jnp.exp(e_t - m[src])
        denom = jax.ops.segment_sum(ex, src, num_segments=n)
        attn = ex / denom[src]
        Vt = Xv[:, dst].transpose(1, 0, 2, 3)
        Y = jax.ops.segment_sum(attn[..., None] * Vt, src, num_segments=n)
        Y = Y.transpose(1, 0, 2, 3).reshape(bt, n, d)
        return Y @ W_out.T
    h = jnp.maximum(_layernorm(x, axis=-1), 0.0)
    x = x + _L0_gnn_ref(h, adj, L0_gnn_Wg0, L0_gnn_bg0, L0_gnn_Wg1, L0_gnn_bg1, L0_gnn_Wih, L0_gnn_Whh, L0_gnn_bih, L0_gnn_bhh)
    h = jnp.maximum(_layernorm(x, axis=-1), 0.0)
    x = x + _L1_gnn_ref(h, adj, L1_gnn_Wqkv, L1_gnn_Wo)
    h = jnp.maximum(_layernorm(x, axis=-1), 0.0)
    x = x + _L2_gnn_ref(h, L2_gnn_W, adj, L2_gnn_bias)
    h = jnp.maximum(_layernorm(x, axis=-1), 0.0)
    x = x + _L3_gnn_ref(h, L3_gnn_W_lin, L3_gnn_W_val, L3_gnn_a, L3_gnn_W_out, adj, L3_gnn_src, L3_gnn_dst)
    return x

_drawn_inputs = setup_inputs


def setup_inputs(seed=0):
    import zlib

    import numpy as np

    out = dict(_drawn_inputs(seed))
    spreads = {'L0_gnn_bg0': (0.0, 0.8), 'L0_gnn_bg1': (0.0, 0.8)}
    factors = {'L0_gnn_Wg0': 8.0,
     'L0_gnn_Wg1': 8.0,
     'L0_gnn_Wih': 7.577,
     'L0_gnn_Whh': 8.0,
     'L0_gnn_bih': 2.958,
     'L0_gnn_bhh': 2.983}
    for name, (base, spread) in spreads.items():
        noise = np.random.default_rng([zlib.crc32(name.encode()), seed]).standard_normal(out[name].shape)
        drawn = base * np.exp(spread * noise) if base else spread * noise
        out[name] = jnp.asarray(drawn.astype(out[name].dtype))
    for name, factor in factors.items():
        out[name] = (out[name] * factor).astype(out[name].dtype)
    return out
```

```python
from contextlib import ExitStack

import concourse.bass as bass
from concourse import mybir

F32 = mybir.dt.float32
I32 = mybir.dt.int32
ALU = mybir.AluOpType
ACT = mybir.ActivationFunctionType
AXX = mybir.AxisListType.X

P = 128
EPS = 1e-5
LOG_EPS = 1e-8
NEG = -1e30
CUT = -3e38
SLOPE = 0.2
I, F, G, O = range(4)


def sync_names(nc, ctx, names):
    return {n: ctx.enter_context(nc.semaphore(n)) for n in names.split()}


def four_layers(nc, x_in, adj, adjT, Wg0, bg0, Wg1, bg1, WihT, WhhT, bihT, bhhT, WqkvT, Wo, W2, bias2,
                WlvT, a_col, WoutT, src_row, src_col, dst_row, dst_col, out):
    B = x_in.shape[0]
    T = C = P
    SKIPS = WihT.shape[1] // (4 * P)
    HEADS = a_col.shape[1]
    DH = C // HEADS
    E = src_row.shape[1]
    EC = E // P
    NB = 16
    TURNS = B // NB

    with ExitStack() as ctx:
        def sb(name, shape, dt=F32):
            return ctx.enter_context(nc.sbuf_tensor(name, shape, dt))

        passed = ctx.enter_context(nc.semaphore("passed"))

        def wait_apart(eng, sem, value):
            eng.wait_ge(sem, value)
            eng.sem_inc(passed, 1)

        def scope():
            stack = ctx.enter_context(ExitStack())
            return stack, lambda name, shape, dt=F32: stack.enter_context(nc.sbuf_tensor(name, shape, dt))

        x = sb("x", [P, B, C])
        ps = ctx.enter_context(nc.psum_tensor("ps", [P, 8, 512], F32))

        ident = sb("ident", [P, P])
        ones = sb("ones", [P, P])
        w_g = sb("w_g", [P, 2, P])
        b_g = sb("b_g", [P, 2, P])
        w_ih = sb("w_ih", [P, SKIPS, 4, P])
        w_hh = sb("w_hh", [P, SKIPS, 4, P])
        b_lstm = sb("b_lstm", [P, SKIPS * 4])
        adjT_sb = sb("adjT_sb", [P, P])
        m_qk = sb("m_qk", [P, P])
        w_vo = sb("w_vo", [P, P])
        adj_causal = sb("adj_causal", [P, P])
        adj_ul = sb("adj_ul", [P, 2, P])
        diag_bc = sb("diag_bc", [P, P])
        w2_sb = sb("w2_sb", [P, 3, P])
        bias2_bc = sb("bias2_bc", [P, P])
        w_lv = sb("w_lv", [P, 2, P])
        w_out = sb("w_out", [P, P])
        a_blk = sb("a_blk", [P, HEADS])
        iota_p = sb("iota_p", [P, EC])
        hot_s = sb("hot_s", [P, E])
        hot_d = sb("hot_d", [P, E])
        hot_sd = sb("hot_sd", [P, E])
        hot_sT = sb("hot_sT", [P, EC, P])
        hot_dT = sb("hot_dT", [P, EC, P])
        same = sb("same", [P, EC, E])
        cut_f = sb("cut_f", [P, E])
        cut_b = sb("cut_b", [P, E])
        log_a = sb("log_a", [P, EC])
        half = sb("half", [P, NB])

        stats = sb("stats", [P, NB, 6])
        mv = sb("mv", [P, NB, 2])
        rstd = sb("rstd", [P, NB])
        hn = sb("hn", [P, NB, C])

        part, tmp = scope()
        b_ih = tmp("b_ih", [P, SKIPS * 4])
        b_hh = tmp("b_hh", [P, SKIPS * 4])
        adj_sb = tmp("adj_sb", [P, P])
        wqkvT = tmp("wqkvT", [P, 3, P])
        wo_sb = tmp("wo_sb", [P, P])
        adj_diag = tmp("adj_diag", [P, P])
        a_sb = tmp("a_sb", [P, HEADS])
        iota_e = tmp("iota_e", [P, E])
        ends_row = tmp("ends_row", [P, 2, E], I32)
        ends_rowf = tmp("ends_rowf", [P, 2, E])
        ends_col = tmp("ends_col", [P, 2, EC], I32)
        ends_colf = tmp("ends_colf", [P, EC, 2])
        key_row = tmp("key_row", [P, E])
        key_col = tmp("key_col", [P, EC])
        is_less = tmp("is_less", [P, E])
        rank = tmp("rank", [P, EC])
        perm = tmp("perm", [P, EC, E])
        rep = tmp("rep", [P, 2, EC, P])
        srt = tmp("srt", [P, 2, E])
        srt_col = tmp("srt_col", [P, EC, 2])
        picked = tmp("picked", [P, EC, P])
        S = sync_names(nc, ctx, "ld_x0 ld_x ld_w made pool_link dve_link act_link pe_link")
        with nc.Block() as block:

            @block.sync
            def _(sp):
                sp.dma_start(x[:, 0:NB, :], x_in[0:NB].rearrange("b t c -> t b c")).then_inc(S["ld_x0"], 16)
                for dst, s in ((w_g[:, 0], Wg0), (w_g[:, 1], Wg1), (w_ih[:].rearrange("p a g h -> p (a g h)"), WihT),
                               (w_hh[:].rearrange("p a g h -> p (a g h)"), WhhT), (b_ih[:], bihT), (b_hh[:], bhhT),
                               (adj_sb[:], adj), (adjT_sb[:], adjT),
                               (wqkvT[:], WqkvT.rearrange("(k d) c -> d k c", d=P)), (wo_sb[:], Wo),
                               (w2_sb[:], W2.rearrange("k f o -> f k o")),
                               (w_lv[:].rearrange("p k c -> p (k c)"), WlvT), (w_out[:], WoutT), (a_sb[:], a_col),
                               (b_g[:, 0], bg0.to_broadcast([P, P])), (b_g[:, 1], bg1.to_broadcast([P, P])),
                               (bias2_bc[:], bias2.to_broadcast([P, P])),
                               (ends_row[:, 0], src_row.to_broadcast([P, E])),
                               (ends_row[:, 1], dst_row.to_broadcast([P, E])),
                               (ends_col[:, 0], src_col), (ends_col[:, 1], dst_col)):
                    sp.dma_start(dst, s).then_inc(S["ld_w"], 16)
                for i in range(1, TURNS):
                    sp.dma_start(x[:, i * NB:(i + 1) * NB, :],
                                 x_in[i * NB:(i + 1) * NB].rearrange("b t c -> t b c")).then_inc(S["ld_x"], 16)
            n_w = 21 * 16

            @block.gpsimd
            def _(pool):
                n = [0]

                def link(ins):
                    n[0] += 1
                    ins.then_inc(S["pool_link"], 1)
                    pool.wait_ge(S["pool_link"], n[0])

                link(nc.gpsimd.memset(ident[:], 0.0))
                link(nc.gpsimd.memset(ones[:], 1.0))
                link(nc.gpsimd.memset(half[:], -0.5))
                link(nc.gpsimd.affine_select(out=ident[:], in_=ident[:], compare_op=ALU.not_equal, fill=1.0, base=0,
                                             pattern=[[-1, P]], channel_multiplier=1))
                link(nc.gpsimd.iota(iota_e[:], pattern=[[1, E]], base=0, channel_multiplier=0,
                                    allow_small_or_imprecise_dtypes=True))
                link(nc.gpsimd.iota(iota_p[:], pattern=[[P, EC]], base=0, channel_multiplier=1,
                                    allow_small_or_imprecise_dtypes=True))
                pool.wait_ge(S["ld_w"], n_w)
                link(nc.gpsimd.affine_select(out=adj_causal[:], in_=adj_sb[:], compare_op=ALU.is_ge, fill=NEG,
                                             base=0, pattern=[[-1, P]], channel_multiplier=1))
                link(nc.gpsimd.affine_select(out=adj_ul[:, 0], in_=adjT_sb[:], compare_op=ALU.is_gt, fill=0.0,
                                             base=0, pattern=[[-1, P]], channel_multiplier=1))
                link(nc.gpsimd.affine_select(out=adj_ul[:, 1], in_=adjT_sb[:], compare_op=ALU.is_gt, fill=0.0,
                                             base=0, pattern=[[1, P]], channel_multiplier=-1))
                link(nc.gpsimd.affine_select(out=adj_diag[:], in_=adjT_sb[:], compare_op=ALU.is_equal, fill=0.0,
                                             base=0, pattern=[[1, P]], channel_multiplier=-1))
                link(nc.gpsimd.affine_select(out=a_blk[:], in_=a_sb[:], compare_op=ALU.is_ge, fill=0.0,
                                             base=0, pattern=[[-DH, HEADS]], channel_multiplier=1))
                link(nc.gpsimd.affine_select(out=a_blk[:], in_=a_blk[:], compare_op=ALU.is_ge, fill=0.0,
                                             base=DH - 1, pattern=[[DH, HEADS]], channel_multiplier=-1))
                nc.gpsimd.memset(log_a[:], 0.0).then_inc(S["made"], 1)

            @block.vector
            def _(dve):
                n = [0]

                def link(ins):
                    n[0] += 1
                    ins.then_inc(S["dve_link"], 1)
                    dve.wait_ge(S["dve_link"], n[0])

                dve.wait_ge(S["ld_w"], n_w)
                dve.wait_ge(S["made"], 1)
                link(nc.vector.tensor_tensor(b_lstm[:], b_ih[:], b_hh[:], ALU.add))
                link(nc.vector.tensor_copy(ends_rowf[:], ends_row[:]))
                link(nc.vector.tensor_copy(ends_colf[:].rearrange("p c k -> p k c"), ends_col[:]))
                link(nc.vector.scalar_tensor_tensor(key_row[:], ends_rowf[:, 0], float(E), iota_e[:],
                                                    ALU.mult, ALU.add))
                link(nc.vector.scalar_tensor_tensor(key_col[:], ends_colf[:, :, 0], float(E), iota_p[:],
                                                    ALU.mult, ALU.add))
                for c in range(EC):
                    link(nc.vector.tensor_scalar(is_less[:], key_row[:], key_col[:, c:c + 1], None, ALU.is_lt,
                                                 ALU.add, accum_out=rank[:, c:c + 1]))
                    link(nc.vector.tensor_scalar(perm[:, c], iota_e[:], rank[:, c:c + 1], None, ALU.is_equal))
                    for k in range(2):
                        link(nc.vector.tensor_scalar(rep[:, k, c], ones[:], ends_colf[:, c, k:k + 1], None, ALU.mult))
                nc.vector.memset(is_less[:], 0.0).then_inc(S["made"], 1)
                dve.wait_ge(S["pe_link"], 1)
                link(nc.vector.tensor_copy(srt[:].rearrange("p k e -> p (k e)"), ps[:, 0, :]))
                link(nc.vector.tensor_copy(srt_col[:], ps[:, 1, 0:2 * EC].rearrange("p (c k) -> p c k", k=2)))
                link(nc.vector.tensor_copy(diag_bc[:], ps[:, 2, 0:P]))
                link(nc.vector.tensor_scalar(m_qk[:], ps[:, 3, 0:P], float(C) ** -0.5, None, ALU.mult))
                link(nc.vector.tensor_copy(w_vo[:], ps[:, 3, P:2 * P]))
                link(nc.vector.tensor_scalar(hot_s[:], srt[:, 0], iota_p[:, 0:1], None, ALU.is_equal))
                link(nc.vector.tensor_scalar(hot_d[:], srt[:, 1], iota_p[:, 0:1], None, ALU.is_equal))
                link(nc.vector.tensor_tensor(hot_sd[:], hot_s[:], hot_d[:], ALU.add))
                nc.vector.memset(is_less[:], 0.0).then_inc(S["made"], 1)
                for c in range(EC):
                    link(nc.vector.tensor_scalar(hot_sT[:, c], iota_e[:, 0:P], srt_col[:, c, 0:1], None, ALU.is_equal))
                    link(nc.vector.tensor_scalar(hot_dT[:, c], iota_e[:, 0:P], srt_col[:, c, 1:2], None, ALU.is_equal))
                    link(nc.vector.tensor_scalar(same[:, c], srt[:, 0], srt_col[:, c, 0:1], None, ALU.is_equal))
                link(nc.vector.memset(cut_f[:, 0:1], CUT))
                link(nc.vector.memset(cut_b[:, E - 1:E], CUT))
                link(nc.vector.tensor_tensor(is_less[:, 1:E], srt[:, 0, 1:E], srt[:, 0, 0:E - 1], ALU.not_equal))
                link(nc.vector.tensor_scalar(cut_f[:, 1:E], is_less[:, 1:E], CUT, None, ALU.mult))
                link(nc.vector.tensor_copy(cut_b[:, 0:E - 1], cut_f[:, 1:E]))
                dve.wait_ge(S["pe_link"], 2)
                link(nc.vector.tensor_tensor(picked[:], ps[:, 4, 0:EC * P].rearrange("p (c m) -> p c m", c=EC),
                                             hot_dT[:], ALU.mult))
                link(nc.vector.tensor_reduce(rank[:], picked[:], AXX, ALU.add))
                nc.vector.tensor_scalar(rank[:], rank[:], LOG_EPS, None, ALU.add).then_inc(S["made"], 1)

            @block.scalar
            def _(act):
                act.wait_ge(S["made"], 4)
                nc.scalar.activation(log_a[:], rank[:], ACT.Ln).then_inc(S["act_link"], 1)

            @block.tensor
            def _(pe):
                pe.wait_ge(S["made"], 2)
                for k in range(2):
                    for c in range(EC):
                        nc.tensor.matmul(ps[:, 0, k * E:(k + 1) * E], rep[:, k, c], perm[:, c],
                                         start=(c == 0), stop=(c == EC - 1))
                for r in range(EC):
                    for c in range(EC):
                        nc.tensor.matmul(ps[:, 1, 2 * r:2 * r + 2], perm[:, c, r * P:(r + 1) * P], ends_colf[:, c],
                                         start=(c == 0), stop=(c == EC - 1))
                nc.tensor.matmul(ps[:, 2, 0:P], ones[:], adj_diag[:], start=True, stop=True)
                nc.tensor.matmul(ps[:, 3, 0:P], wqkvT[:, 0], wqkvT[:, 1], start=True, stop=True)
                nc.tensor.matmul(ps[:, 3, P:2 * P], wqkvT[:, 2], wo_sb[:], start=True, stop=True).then_inc(
                    S["pe_link"], 1)
                pe.wait_ge(S["made"], 3)
                for c in range(EC):
                    last = nc.tensor.matmul(ps[:, 4, c * P:(c + 1) * P], hot_s[:, c * P:(c + 1) * P], adj_sb[:],
                                            start=True, stop=True)
                last.then_inc(S["pe_link"], 1)

        part.close()


        def norm_stats(b0, k, n, done):
            for j in range(k, k + n):
                nc.vector.bn_stats(stats[:, j], x[:, bass.ds(b0 + j, 1), :].rearrange("p a c -> p (a c)")).then_inc(
                    done, 1)

        def norm_aggr(k, n, done):
            for j in range(k, k + n):
                nc.vector.bn_aggr(mv[:, j], stats[:, j]).then_inc(done, 1)

        def norm_apply(b0, k, n, done):
            for j in range(k, k + n):
                nc.vector.tensor_scalar(hn[:, j], x[:, bass.ds(b0 + j, 1), :].rearrange("p a c -> p (a c)"),
                                        mv[:, j, 0:1], rstd[:, j:j + 1], ALU.subtract, ALU.mult).then_inc(done, 1)

        part, tmp = scope()
        GB = NB // 2
        NC = GB * T
        CH = NC // 512
        CB = 512 // T
        hT = tmp("hT", [P, 2, GB, T])
        u = tmp("u", [P, 2, GB, C])
        H = tmp("H", [P, 2, GB, T])
        gate = tmp("gate", [P, 2, 4, 512])
        cell = tmp("cell", [P, 2, 512])
        hid = tmp("hid", [P, 2, 512])
        tanh_c = tmp("tanh_c", [P, 2, 512])

        steps = []
        for p in range(1, SKIPS + 1):
            nb = min(GB, 512 // (T // p))
            for b0 in range(0, GB, nb):
                steps += [(p, j, j == p - 1, b0, nb, T // p) for j in range(p)]
        n_gates = [3 if st[1] == 0 else 4 for st in steps]
        gates_of = [(I, G, O) if st[1] == 0 else (I, G, F, O) for st in steps]
        before, total = {}, 0
        for k in range(len(steps)):
            for g in range(2):
                before[k, g] = total
                total += n_gates[k]
        NS = len(steps)
        parts_before, tot_parts = {}, 0
        for k in range(NS):
            for g in range(2):
                parts_before[k, g] = tot_parts
                tot_parts += 0 if steps[k][1] == 0 else 2

        def at(buf, p, j, b0, nb, w):
            return buf[:, b0:b0 + nb, j:j + p * (w - 1) + 1:p]

        def flat(buf, nb, w):
            return buf[:, 0:nb * w].rearrange("p (b w) -> p b w", b=nb)

        ld_x, ld_x0 = S["ld_x"], S["ld_x0"]
        S = sync_names(nc, ctx, "a_stats a_aggr a_var a_rstd a_hn a_hTp a_hT a_up a_u a_Hp a_H a_gatep a_gate "
                                "a_part a_cell a_tanh a_hid a_outp a_out")
        with nc.Block() as block:
            def norm_piece(m, b0, done_turns):
                if m < 8:
                    if m == 0:
                        nc.vector.wait_ge(ld_x, 16 * (TURNS - 1))
                    norm_stats(b0, 2 * m, 2, S["a_stats"])
                elif m < 12:
                    if m == 8:
                        wait_apart(nc.vector, S["a_stats"], done_turns * NB + NB)
                    norm_aggr(4 * (m - 8), 4, S["a_aggr"])
                elif 14 <= m < 22:
                    if m == 14:
                        nc.vector.wait_ge(S["a_rstd"], done_turns + 1)
                        nc.vector.wait_ge(S["a_hTp"], done_turns * 2 * CH)
                    norm_apply(b0, 2 * (m - 14), 2, S["a_hn"])

            @block.gpsimd
            def _(pool):
                with pool.Fori(0, TURNS) as i:
                    wait_apart(pool, S["a_aggr"], i * NB + NB)
                    nc.gpsimd.tensor_scalar(rstd[:], mv[:, :, 1], EPS, None, ALU.add).then_inc(S["a_var"], 1)
                    pool.wait_ge(S["a_var"], i + 1)
                    nc.gpsimd.tensor_tensor(rstd[:], rstd[:], half[:], ALU.pow).then_inc(S["a_rstd"], 1)

            @block.vector
            def _(dve):
                def turn(i, more):
                    for s in range(2):
                        for g in range(2):
                            for c in range(CH):
                                n = (s * 2 + g) * CH + c
                                dve.wait_ge(S["a_up"], i * 4 * CH + n + 1)
                                nc.vector.tensor_tensor(
                                    u[:, g, c * CB:(c + 1) * CB],
                                    ps[:, 4 * g + 2 + c].rearrange("p (b c) -> p b c", b=CB),
                                    b_g[:, s].unsqueeze(1).to_broadcast([P, CB, C]), ALU.add).then_inc(S["a_u"], 1)
                    for k, (p, j, last, b0, nb, w) in enumerate(steps):
                        for g in range(2):
                            n0 = before[k, g]
                            q = 2 * k + g
                            gi, gf, gg, go = (flat(gate[:, g, z], nb, w) for z in (I, F, G, O))
                            cc = flat(cell[:, g], nb, w)
                            if j == 0:
                                dve.wait_ge(S["a_gate"], i * total + n0 + 2)
                                nc.vector.tensor_tensor(cc, gi, gg, ALU.mult).then_inc(S["a_cell"], 1)
                            else:
                                dve.wait_ge(S["a_gate"], i * total + n0 + 2)
                                nc.vector.tensor_tensor(gi, gi, gg, ALU.mult).then_inc(S["a_part"], 1)
                                dve.wait_ge(S["a_gate"], i * total + n0 + 3)
                                nc.vector.tensor_tensor(cc, cc, gf, ALU.mult).then_inc(S["a_part"], 1)
                                dve.wait_ge(S["a_part"], i * tot_parts + parts_before[k, g] + 2)
                                nc.vector.tensor_tensor(cc, cc, gi, ALU.add).then_inc(S["a_cell"], 1)
                            if more:
                                norm_piece(q, (i + 1) * NB, i + 1)
                            dst = at(H[:, g], p, j, b0, nb, w) if last else flat(hid[:, g], nb, w)
                            dve.wait_ge(S["a_tanh"], i * 2 * NS + q + 1)
                            nc.vector.tensor_tensor(dst, go, flat(tanh_c[:, g], nb, w), ALU.mult).then_inc(
                                S["a_hid"], 1)
                    for g in range(2):
                        for c in range(CH):
                            n = g * CH + c
                            dve.wait_ge(S["a_outp"], i * 2 * CH + n + 1)
                            xs = x[:, bass.ds(i * NB + g * GB + c * CB, CB), :]
                            nc.vector.tensor_tensor(xs, xs, ps[:, 4 * g + c].rearrange("p (b c) -> p b c", b=CB),
                                                    ALU.add).then_inc(S["a_out"], 1)

                dve.wait_ge(ld_x0, 16)
                norm_stats(0, 0, NB, S["a_stats"])
                wait_apart(dve, S["a_stats"], NB)
                norm_aggr(0, NB, S["a_aggr"])
                dve.wait_ge(S["a_rstd"], 1)
                norm_apply(0, 0, NB, S["a_hn"])
                with dve.Fori(0, TURNS - 1) as i:
                    turn(i, True)
                turn(TURNS - 1, False)

            @block.scalar
            def _(act):
                with act.Fori(0, TURNS) as i:
                    for g in range(2):
                        for c in range(CH):
                            act.wait_ge(S["a_hTp"], i * 2 * CH + g * CH + c + 1)
                            nc.scalar.activation(hT[:, g, c * CB:(c + 1) * CB],
                                                 ps[:, 4 * g + c].rearrange("p (b t) -> p b t", b=CB),
                                                 ACT.Relu).then_inc(S["a_hT"], 1)
                    for s in range(2):
                        dst = (hT, H)[s]
                        for g in range(2):
                            for c in range(CH):
                                act.wait_ge(S["a_Hp"], i * 4 * CH + (s * 2 + g) * CH + c + 1)
                                nc.scalar.activation(dst[:, g, c * CB:(c + 1) * CB],
                                                     ps[:, 4 * g + c].rearrange("p (b t) -> p b t", b=CB),
                                                     ACT.Relu).then_inc(S["a_H"], 1)
                    for k, (p, j, last, b0, nb, w) in enumerate(steps):
                        for g in range(2):
                            for m, z in enumerate(gates_of[k]):
                                act.wait_ge(S["a_gatep"], i * total + before[k, g] + m + 1)
                                nc.scalar.activation(gate[:, g, z, 0:nb * w], ps[:, 4 * g + m, 0:nb * w],
                                                     ACT.Tanh if z == G else ACT.Sigmoid,
                                                     bias=b_lstm[:, 4 * (p - 1) + z:4 * (p - 1) + z + 1]).then_inc(
                                                         S["a_gate"], 1)
                            act.wait_ge(S["a_cell"], i * 2 * NS + 2 * k + g + 1)
                            nc.scalar.activation(tanh_c[:, g, 0:nb * w], cell[:, g, 0:nb * w],
                                                 ACT.Tanh).then_inc(S["a_tanh"], 1)

            @block.tensor
            def _(pe):
                def turn(i, first):
                    for g in range(2):
                        for c in range(CH):
                            if not first:
                                pe.wait_ge(S["a_out"], i * 2 * CH - 2 * CH + g * CH + c + 1)
                            pe.wait_ge(S["a_hn"], i * NB + g * GB + (c + 1) * CB)
                            for b in range(CB):
                                last = nc.tensor.transpose(ps[:, 4 * g + c, b * T:(b + 1) * T],
                                                           hn[:, g * GB + c * CB + b], ident[:])
                            last.then_inc(S["a_hTp"], 1)
                    for s in range(2):
                        for g in range(2):
                            for c in range(CH):
                                if s == 0:
                                    pe.wait_ge(S["a_hT"], i * 2 * CH + g * CH + c + 1)
                                else:
                                    pe.wait_ge(S["a_H"], i * 4 * CH + g * CH + c + 1)
                                for b in range(CB):
                                    last = nc.tensor.matmul(ps[:, 4 * g + 2 + c, b * C:(b + 1) * C],
                                                            hT[:, g, c * CB + b], w_g[:, s], start=True, stop=True)
                                last.then_inc(S["a_up"], 1)
                        for g in range(2):
                            for c in range(CH):
                                pe.wait_ge(S["a_u"], i * 4 * CH + (s * 2 + g) * CH + c + 1)
                                for b in range(CB):
                                    last = nc.tensor.matmul(ps[:, 4 * g + c, b * T:(b + 1) * T],
                                                            u[:, g, c * CB + b], adjT_sb[:], start=True, stop=True)
                                last.then_inc(S["a_Hp"], 1)
                    for k, (p, j, last_step, b0, nb, w) in enumerate(steps):
                        for g in range(2):
                            if k == 0:
                                pe.wait_ge(S["a_H"], i * 4 * CH + 2 * CH + g * CH + CH)
                            else:
                                pe.wait_ge(S["a_hid"], i * 2 * NS + 2 * (k - 1) + g + 1)
                            for m, z in enumerate(gates_of[k]):
                                dst = ps[:, 4 * g + m, 0:nb * w]
                                last = nc.tensor.matmul(dst, w_ih[:, p - 1, z], at(H[:, g], p, j, b0, nb, w),
                                                        start=True, stop=(j == 0))
                                if j > 0:
                                    last = nc.tensor.matmul(dst, w_hh[:, p - 1, z], hid[:, g, 0:nb * w],
                                                            start=False, stop=True)
                                last.then_inc(S["a_gatep"], 1)
                    for g in range(2):
                        for c in range(CH):
                            pe.wait_ge(S["a_hid"], i * 2 * NS + 2 * (NS - 1) + g + 1)
                            for b in range(CB):
                                last = nc.tensor.transpose(ps[:, 4 * g + c, b * T:(b + 1) * T],
                                                           H[:, g, c * CB + b], ident[:])
                            last.then_inc(S["a_outp"], 1)

                turn(0, True)
                with pe.Fori(1, TURNS) as i:
                    turn(i, False)

        part.close()

        part, tmp = scope()
        W1 = 4
        QB = NB // W1
        hT1 = tmp("hT1", [P, W1, QB, T])
        hmT = tmp("hmT", [P, W1, QB, T])
        prob = tmp("prob", [P, W1, QB, T])
        probT = tmp("probT", [P, W1, QB, T])
        yT = tmp("yT", [P, W1, QB, T])
        nmax = tmp("nmax", [P, NB])
        rsum = tmp("rsum", [P, NB])
        rinv = tmp("rinv", [P, NB])
        S = sync_names(nc, ctx, "b_stats b_aggr b_var b_rstd b_aff b_hn b_hTp b_hT b_qp b_q b_sp b_s b_max b_e b_pTp "
                                "b_pT b_yp b_y b_op b_inv b_o")

        def bank(g, k):
            return ps[:, 2 * g + k]

        def by4(ap, n=QB):
            return ap.rearrange("p (b t) -> p b t", b=n)

        with nc.Block() as block:
            @block.gpsimd
            def _(pool):
                with pool.Fori(0, TURNS) as i:
                    wait_apart(pool, S["b_aggr"], i * NB + NB)
                    nc.gpsimd.tensor_scalar(rstd[:], mv[:, :, 1], EPS, None, ALU.add).then_inc(S["b_var"], 1)
                    pool.wait_ge(S["b_var"], i + 1)
                    nc.gpsimd.tensor_tensor(rstd[:], rstd[:], half[:], ALU.pow).then_inc(S["b_rstd"], 1)
                    for g in range(W1):
                        wait_apart(pool, S["b_aff"], i * NB + (g + 1) * QB)
                        nc.gpsimd.tensor_scalar(hn[:, g * QB:(g + 1) * QB], hn[:, g * QB:(g + 1) * QB], 0.0, None,
                                                ALU.max).then_inc(S["b_hn"], 1)

            @block.vector
            def _(dve):
                def norm(i, g):
                    norm_stats(i * NB, g * QB, QB, S["b_stats"])
                    wait_apart(dve, S["b_stats"], i * NB + (g + 1) * QB)
                    norm_aggr(g * QB, QB, S["b_aggr"])

                def turn(i, more):
                    for g in range(W1):
                        dve.wait_ge(S["b_sp"], i * W1 + g + 1)
                        nc.vector.tensor_tensor(prob[:, g], by4(bank(g, 0)),
                                                adj_causal[:].unsqueeze(1).to_broadcast([P, QB, T]),
                                                ALU.add).then_inc(S["b_s"], 1)
                        dve.wait_ge(S["b_s"], i * W1 + g + 1)
                        nc.vector.tensor_reduce(nmax[:, g * QB:(g + 1) * QB], prob[:, g], AXX, ALU.max,
                                                negate=True).then_inc(S["b_max"], 1)
                    for g in range(W1):
                        dve.wait_ge(S["b_pTp"], i * W1 + g + 1)
                        nc.vector.tensor_copy(probT[:, g], by4(bank(g, 1))).then_inc(S["b_pT"], 1)
                        nc.vector.reciprocal(rinv[:, g * QB:(g + 1) * QB], rsum[:, g * QB:(g + 1) * QB]).then_inc(
                            S["b_inv"], 1)
                        if more:
                            norm(i + 1, g)
                    for g in range(W1):
                        dve.wait_ge(S["b_op"], i * W1 + g + 1)
                        dve.wait_ge(S["b_inv"], i * W1 + g + 1)
                        for b in range(QB):
                            xs = x[:, bass.ds(i * NB + g * QB + b, 1), :].rearrange("p a c -> p (a c)")
                            ins = nc.vector.scalar_tensor_tensor(xs, bank(g, 1)[:, b * C:(b + 1) * C],
                                                                 rinv[:, g * QB + b:g * QB + b + 1], xs,
                                                                 ALU.mult, ALU.add)
                        ins.then_inc(S["b_o"], 1)
                    if more:
                        dve.wait_ge(S["b_rstd"], i + 2)
                        norm_apply((i + 1) * NB, 0, NB, S["b_aff"])

                for g in range(W1):
                    norm(0, g)
                dve.wait_ge(S["b_rstd"], 1)
                norm_apply(0, 0, NB, S["b_aff"])
                with dve.Fori(0, TURNS - 1) as i:
                    turn(i, True)
                turn(TURNS - 1, False)

            @block.scalar
            def _(act):
                with act.Fori(0, TURNS) as i:
                    for g in range(W1):
                        act.wait_ge(S["b_hTp"], i * W1 + g + 1)
                        nc.scalar.activation(hT1[:, g], by4(bank(g, 0)), ACT.Copy).then_inc(S["b_hT"], 1)
                    for g in range(W1):
                        act.wait_ge(S["b_qp"], i * W1 + g + 1)
                        nc.scalar.activation(hmT[:, g], by4(bank(g, 1)), ACT.Copy).then_inc(S["b_q"], 1)
                    for g in range(W1):
                        act.wait_ge(S["b_max"], i * W1 + g + 1)
                        for b in range(QB):
                            n = g * QB + b
                            ins = nc.scalar.activation(prob[:, g, b], prob[:, g, b], ACT.Exp, bias=nmax[:, n:n + 1],
                                                       accum_out=rsum[:, n:n + 1])
                        ins.then_inc(S["b_e"], 1)
                    for g in range(W1):
                        act.wait_ge(S["b_yp"], i * W1 + g + 1)
                        nc.scalar.activation(yT[:, g], by4(bank(g, 0)), ACT.Copy).then_inc(S["b_y"], 1)

            @block.tensor
            def _(pe):
                def turn(i, first):
                    for g in range(W1):
                        pe.wait_ge(S["b_hn"], i * W1 + g + 1)
                        for b in range(QB):
                            ins = nc.tensor.transpose(bank(g, 0)[:, b * T:(b + 1) * T], hn[:, g * QB + b], ident[:])
                        ins.then_inc(S["b_hTp"], 1)
                    for g in range(W1):
                        pe.wait_ge(S["b_hT"], i * W1 + g + 1)
                        if not first:
                            pe.wait_ge(S["b_o"], i * W1 - W1 + g + 1)
                        nc.tensor.matmul(bank(g, 1), m_qk[:], hT1[:, g].rearrange("p b t -> p (b t)"),
                                         start=True, stop=True).then_inc(S["b_qp"], 1)
                    for g in range(W1):
                        pe.wait_ge(S["b_q"], i * W1 + g + 1)
                        for b in range(QB):
                            ins = nc.tensor.matmul(bank(g, 0)[:, b * T:(b + 1) * T], hmT[:, g, b], hT1[:, g, b],
                                                   start=True, stop=True)
                        ins.then_inc(S["b_sp"], 1)
                    for g in range(W1):
                        pe.wait_ge(S["b_e"], i * W1 + g + 1)
                        for b in range(QB):
                            ins = nc.tensor.transpose(bank(g, 1)[:, b * T:(b + 1) * T], prob[:, g, b], ident[:])
                        ins.then_inc(S["b_pTp"], 1)
                    for g in range(W1):
                        pe.wait_ge(S["b_pT"], i * W1 + g + 1)
                        for b in range(QB):
                            ins = nc.tensor.matmul(bank(g, 0)[:, b * T:(b + 1) * T], hn[:, g * QB + b],
                                                   probT[:, g, b], start=True, stop=True)
                        ins.then_inc(S["b_yp"], 1)
                    for g in range(W1):
                        pe.wait_ge(S["b_y"], i * W1 + g + 1)
                        for b in range(QB):
                            ins = nc.tensor.matmul(bank(g, 1)[:, b * C:(b + 1) * C], yT[:, g, b], w_vo[:],
                                                   start=True, stop=True)
                        ins.then_inc(S["b_op"], 1)

                turn(0, True)
                with pe.Fori(1, TURNS) as i:
                    turn(i, False)

        part.close()

        part, tmp = scope()
        z0 = tmp("z0", [P, W1, QB, T])
        z12 = tmp("z12", [P, W1, QB, 2, T])
        xb = tmp("xb", [P, NB, C])
        S = sync_names(nc, ctx, "c_stats c_aggr c_var c_rstd c_aff c_hn c_xb c_zp c_z0 c_z12 c_op c_o")
        with nc.Block() as block:
            @block.gpsimd
            def _(pool):
                def turn(i, first):
                    wait_apart(pool, S["c_aggr"], i * NB + NB)
                    nc.gpsimd.tensor_scalar(rstd[:], mv[:, :, 1], EPS, None, ALU.add).then_inc(S["c_var"], 1)
                    pool.wait_ge(S["c_var"], i + 1)
                    nc.gpsimd.tensor_tensor(rstd[:], rstd[:], half[:], ALU.pow).then_inc(S["c_rstd"], 1)
                    for g in range(W1):
                        wait_apart(pool, S["c_aff"], i * NB + (g + 1) * QB)
                        nc.gpsimd.tensor_scalar(hn[:, g * QB:(g + 1) * QB], hn[:, g * QB:(g + 1) * QB], 0.0, None,
                                                ALU.max).then_inc(S["c_hn"], 1)
                    for g in range(W1):
                        if not first:
                            pool.wait_ge(S["c_o"], i * W1 - W1 + g + 1)
                        nc.gpsimd.tensor_tensor(xb[:, g * QB:(g + 1) * QB], x[:, bass.ds(i * NB + g * QB, QB), :],
                                                bias2_bc[:].unsqueeze(1).to_broadcast([P, QB, C]),
                                                ALU.add).then_inc(S["c_xb"], 1)
                turn(0, True)
                with pool.Fori(1, TURNS) as i:
                    turn(i, False)

            @block.vector
            def _(dve):
                def norm(i, g):
                    norm_stats(i * NB, g * QB, QB, S["c_stats"])
                    wait_apart(dve, S["c_stats"], i * NB + (g + 1) * QB)
                    norm_aggr(g * QB, QB, S["c_aggr"])

                def turn(i, more):
                    for h in range(2):
                        for g in (2 * h, 2 * h + 1):
                            dve.wait_ge(S["c_zp"], i * W1 + g + 1)
                            nc.vector.tensor_tensor(z0[:, g], by4(ps[:, 4 * (g % 2)]),
                                                    diag_bc[:].unsqueeze(1).to_broadcast([P, QB, T]),
                                                    ALU.mult).then_inc(S["c_z0"], 1)
                            if more:
                                norm(i + 1, g)
                        for g in (2 * h, 2 * h + 1):
                            dve.wait_ge(S["c_op"], i * W1 + g + 1)
                            dve.wait_ge(S["c_xb"], i * W1 + g + 1)
                            nc.vector.tensor_tensor(x[:, bass.ds(i * NB + g * QB, QB), :], by4(ps[:, 4 * (g % 2) + 3]),
                                                    xb[:, g * QB:(g + 1) * QB], ALU.add).then_inc(S["c_o"], 1)
                    if more:
                        dve.wait_ge(S["c_rstd"], i + 2)
                        norm_apply((i + 1) * NB, 0, NB, S["c_aff"])

                for g in range(W1):
                    norm(0, g)
                dve.wait_ge(S["c_rstd"], 1)
                norm_apply(0, 0, NB, S["c_aff"])
                with dve.Fori(0, TURNS - 1) as i:
                    turn(i, True)
                turn(TURNS - 1, False)

            @block.scalar
            def _(act):
                with act.Fori(0, TURNS) as i:
                    for g in range(W1):
                        act.wait_ge(S["c_zp"], i * W1 + g + 1)
                        nc.scalar.activation(z12[:, g].rearrange("p b k t -> p (b k t)").rearrange(
                            "p (a n) -> p a n", a=2), ps[:, 4 * (g % 2) + 1:4 * (g % 2) + 3],
                                             ACT.Copy).then_inc(S["c_z12"], 1)

            @block.tensor
            def _(pe):
                def turn(i, first):
                    for h in range(2):
                        for g in (2 * h, 2 * h + 1):
                            k = 4 * (g % 2)
                            pe.wait_ge(S["c_hn"], i * W1 + g + 1)
                            if h > 0 or not first:
                                pe.wait_ge(S["c_z0"], i * W1 + g - 1)
                                pe.wait_ge(S["c_z12"], i * W1 + g - 1)
                            for b in range(QB):
                                nc.tensor.transpose(ps[:, k, b * T:(b + 1) * T], hn[:, g * QB + b], ident[:])
                            for b in range(QB):
                                ins = nc.tensor.matmul(ps[:, k + 1 + b // 2, (b % 2) * 2 * T:(b % 2 + 1) * 2 * T],
                                                       hn[:, g * QB + b], adj_ul[:].rearrange("p k t -> p (k t)"),
                                                       start=True, stop=True)
                            ins.then_inc(S["c_zp"], 1)
                        for g in (2 * h, 2 * h + 1):
                            k = 4 * (g % 2)
                            pe.wait_ge(S["c_z0"], i * W1 + g + 1)
                            pe.wait_ge(S["c_z12"], i * W1 + g + 1)
                            if h > 0 or not first:
                                pe.wait_ge(S["c_o"], i * W1 + g - 1)
                            for b in range(QB):
                                dst = ps[:, k + 3, b * C:(b + 1) * C]
                                nc.tensor.matmul(dst, z0[:, g, b], w2_sb[:, 0], start=True, stop=False)
                                nc.tensor.matmul(dst, z12[:, g, b, 0], w2_sb[:, 1], start=False, stop=False)
                                ins = nc.tensor.matmul(dst, z12[:, g, b, 1], w2_sb[:, 2], start=False, stop=True)
                            ins.then_inc(S["c_op"], 1)

                turn(0, True)
                with pe.Fori(1, TURNS) as i:
                    turn(i, False)

        part.close()

        part, tmp = scope()
        SB = P // HEADS
        SUPER = B // SB
        NG = SB // QB
        xq = tmp("xq", [P, 2, QB, C])
        xv = tmp("xv", [P, SB, C])
        rl = tmp("rl", [P, 2, 2, 512])
        lr = tmp("lr", [P, 2, QB, E])
        hT3 = tmp("hT3", [P, 2, QB, T])
        lg = tmp("lg", [P, EC, P])
        lgT = tmp("lgT", [P, E])
        fwd = tmp("fwd", [P, E])
        bwd = tmp("bwd", [P, E])
        expT = tmp("expT", [P, E])
        ex = tmp("ex", [P, EC, P])
        att = tmp("att", [P, EC, P])
        va = tmp("va", [P, 2, EC, QB, C])
        y3 = tmp("y3", [P, 2, QB, T])
        S = sync_names(nc, ctx, "d_stats d_aggr d_var d_rstd d_aff d_hn d_hTp d_hT d_xp d_xq d_xv d_zp d_rl d_lr d_lgp d_lg "
                                "d_lgTp d_lgT d_fb d_m d_sub d_exp d_exTp d_ex d_denp d_att d_vp d_va d_yp d_y "
                                "d_op d_o d_st")
        LGB = 7
        with nc.Block() as block:
            @block.gpsimd
            def _(pool):
                with pool.Fori(0, B // NB) as i:
                    wait_apart(pool, S["d_aggr"], i * NB + NB)
                    nc.gpsimd.tensor_scalar(rstd[:], mv[:, :, 1], EPS, None, ALU.add).then_inc(S["d_var"], 1)
                    pool.wait_ge(S["d_var"], i + 1)
                    nc.gpsimd.tensor_tensor(rstd[:], rstd[:], half[:], ALU.pow).then_inc(S["d_rstd"], 1)

            @block.sync
            def _(sp):
                with sp.Fori(0, B // QB) as i:
                    sp.wait_ge(S["d_o"], i + 1)
                    sp.dma_start(out[bass.ds(i * QB, QB)].rearrange("b t c -> t b c"),
                                 x[:, bass.ds(i * QB, QB), :]).then_inc(S["d_st"], 16)
                sp.wait_ge(S["d_st"], 16 * (B // QB))

            @block.vector
            def _(dve):
                with dve.Fori(0, SUPER) as s:
                    for n in range(0, NG, 2):
                        if n % 4 == 0:
                            i = s * (SB // NB) + n // 4
                            norm_stats(i * NB, 0, NB, S["d_stats"])
                            wait_apart(dve, S["d_stats"], i * NB + NB)
                            norm_aggr(0, NB, S["d_aggr"])
                            dve.wait_ge(S["d_rstd"], i + 1)
                            norm_apply(i * NB, 0, NB, S["d_hn"])
                        for g in range(2):
                            dve.wait_ge(S["d_xp"], s * NG + n + g + 1)
                            nc.vector.tensor_copy(xv[:, (n + g) * QB:(n + g + 1) * QB],
                                                  by4(ps[:, 3 * g + 2])).then_inc(S["d_xv"], 1)
                        for g in range(2):
                            for k in range(2):
                                dve.wait_ge(S["d_rl"], (s * NG + n + g) * 2 + k + 1)
                                nc.vector.scalar_tensor_tensor(
                                    lr[:, g, 2 * k:2 * k + 2].rearrange("p b e -> p (b e)"), ps[:, 3 * g + k], SLOPE,
                                    rl[:, g, k], ALU.mult, ALU.add).then_inc(S["d_lr"], 1)
                    dve.wait_ge(S["d_lgp"], s * NG + NG)
                    for c in range(EC):
                        nc.vector.tensor_scalar(lg[:, c], ps[:, LGB, c * P:(c + 1) * P], log_a[:, c:c + 1], None,
                                                ALU.add).then_inc(S["d_lg"], 1)
                    dve.wait_ge(S["d_lgTp"], s + 1)
                    nc.vector.tensor_copy(lgT[:], ps[:, 0, 0:E]).then_inc(S["d_lgT"], 1)
                    dve.wait_ge(S["d_lgT"], s + 1)
                    nc.vector.tensor_tensor_scan(fwd[:], cut_f[:], lgT[:], 0.0, ALU.add, ALU.max).then_inc(S["d_fb"], 1)
                    nc.vector.tensor_tensor_scan(bwd[:, ::-1], cut_b[:, ::-1], lgT[:, ::-1], 0.0, ALU.add,
                                                 ALU.max).then_inc(S["d_fb"], 1)
                    dve.wait_ge(S["d_fb"], 2 * s + 2)
                    nc.vector.tensor_tensor(fwd[:], fwd[:], bwd[:], ALU.max).then_inc(S["d_m"], 1)
                    dve.wait_ge(S["d_m"], s + 1)
                    nc.vector.tensor_tensor(bwd[:], lgT[:], fwd[:], ALU.subtract).then_inc(S["d_sub"], 1)
                    dve.wait_ge(S["d_exTp"], s + 1)
                    nc.vector.tensor_copy(ex[:].rearrange("p c n -> p (c n)"), ps[:, 1, 0:E]).then_inc(S["d_ex"], 1)
                    dve.wait_ge(S["d_denp"], s + 1)
                    nc.vector.reciprocal(att[:].rearrange("p c n -> p (c n)"), ps[:, 2, 0:E]).then_inc(S["d_ex"], 1)
                    dve.wait_ge(S["d_ex"], 2 * s + 2)
                    nc.vector.tensor_tensor(att[:], att[:], ex[:], ALU.mult).then_inc(S["d_att"], 1)
                    dve.wait_ge(S["d_att"], s + 1)
                    for n in range(NG):
                        g = n % 2
                        for c in range(EC):
                            dve.wait_ge(S["d_vp"], (s * NG + n) * EC + c + 1)
                            nc.vector.tensor_tensor(
                                va[:, g, c].rearrange("p b (h d) -> p (b h) d", h=HEADS),
                                ps[:, 3 * g + c].rearrange("p (n d) -> p n d", d=DH),
                                att[:, c, n * QB * HEADS:(n + 1) * QB * HEADS].unsqueeze(2).to_broadcast(
                                    [P, QB * HEADS, DH]), ALU.mult).then_inc(S["d_va"], 1)
                        if n > 0:
                            m = n - 1
                            dve.wait_ge(S["d_op"], s * NG + m + 1)
                            xs = x[:, bass.ds(s * SB + m * QB, QB), :]
                            nc.vector.tensor_tensor(xs, xs, by4(ps[:, 3 * (m % 2) + 2]), ALU.add).then_inc(S["d_o"], 1)
                    dve.wait_ge(S["d_op"], s * NG + NG)
                    xs = x[:, bass.ds(s * SB + (NG - 1) * QB, QB), :]
                    nc.vector.tensor_tensor(xs, xs, by4(ps[:, 3 * ((NG - 1) % 2) + 2]), ALU.add).then_inc(S["d_o"], 1)

            @block.scalar
            def _(act):
                with act.Fori(0, SUPER) as s:
                    for n in range(0, NG, 2):
                        for g in range(2):
                            act.wait_ge(S["d_hTp"], s * NG + n + g + 1)
                            nc.scalar.activation(hT3[:, g], by4(ps[:, 3 * g]), ACT.Relu).then_inc(S["d_hT"], 1)
                        for g in range(2):
                            act.wait_ge(S["d_xp"], s * NG + n + g + 1)
                            nc.scalar.activation(xq[:, g], by4(ps[:, 3 * g + 1]), ACT.Copy).then_inc(S["d_xq"], 1)
                        for g in range(2):
                            for k in range(2):
                                act.wait_ge(S["d_zp"], (s * NG + n + g) * 2 + k + 1)
                                nc.scalar.activation(rl[:, g, k], ps[:, 3 * g + k], ACT.Relu,
                                                     scale=1.0 - SLOPE).then_inc(S["d_rl"], 1)
                    act.wait_ge(S["d_sub"], s + 1)
                    nc.scalar.activation(expT[:], bwd[:], ACT.Exp).then_inc(S["d_exp"], 1)
                    for n in range(NG):
                        g = n % 2
                        act.wait_ge(S["d_yp"], s * NG + n + 1)
                        nc.scalar.activation(y3[:, g], by4(ps[:, 6]), ACT.Copy).then_inc(S["d_y"], 1)

            @block.tensor
            def _(pe):
                def turn(s, first):
                    for h in range(NG // 2):
                        ns = (2 * h, 2 * h + 1)
                        for n in ns:
                            g = n % 2
                            if h > 0:
                                pe.wait_ge(S["d_lr"], (s * NG + n - 1) * 2)
                            elif not first:
                                pe.wait_ge(S["d_o"], s * NG - 2 + g + 1)
                            pe.wait_ge(S["d_hn"], (s * NG + n + 1) * QB)
                            for b in range(QB):
                                ins = nc.tensor.transpose(ps[:, 3 * g, b * T:(b + 1) * T], hn[:, (n % 4) * QB + b],
                                                          ident[:])
                            ins.then_inc(S["d_hTp"], 1)
                        for n in ns:
                            g = n % 2
                            pe.wait_ge(S["d_hT"], s * NG + n + 1)
                            for k in range(2):
                                for b in range(QB):
                                    ins = nc.tensor.matmul(ps[:, 3 * g + 1 + k, b * C:(b + 1) * C], hT3[:, g, b],
                                                           w_lv[:, k], start=True, stop=True)
                            ins.then_inc(S["d_xp"], 1)
                        for n in ns:
                            g = n % 2
                            pe.wait_ge(S["d_xq"], s * NG + n + 1)
                            pe.wait_ge(S["d_xv"], s * NG + n + 1)
                            for k in range(2):
                                for b in range(2):
                                    ins = nc.tensor.matmul(ps[:, 3 * g + k, b * E:(b + 1) * E], xq[:, g, 2 * k + b],
                                                           hot_sd[:], start=True, stop=True)
                                ins.then_inc(S["d_zp"], 1)
                        for n in ns:
                            g = n % 2
                            pe.wait_ge(S["d_lr"], (s * NG + n + 1) * 2)
                            for b in range(QB):
                                for c in range(EC):
                                    col = c * P + (n * QB + b) * HEADS
                                    ins = nc.tensor.matmul(ps[:, LGB, col:col + HEADS],
                                                           lr[:, g, b, c * P:(c + 1) * P], a_blk[:],
                                                           start=True, stop=True)
                            ins.then_inc(S["d_lgp"], 1)
                    pe.wait_ge(S["d_lg"], s * EC + EC)
                    for c in range(EC):
                        ins = nc.tensor.transpose(ps[:, 0, c * P:(c + 1) * P], lg[:, c], ident[:])
                    ins.then_inc(S["d_lgTp"], 1)
                    pe.wait_ge(S["d_exp"], s + 1)
                    for c in range(EC):
                        ins = nc.tensor.transpose(ps[:, 1, c * P:(c + 1) * P], expT[:, c * P:(c + 1) * P], ident[:])
                    ins.then_inc(S["d_exTp"], 1)
                    pe.wait_ge(S["d_ex"], 2 * s + 1)
                    for c in range(EC):
                        for k in range(EC):
                            ins = nc.tensor.matmul(ps[:, 2, c * P:(c + 1) * P], same[:, k, c * P:(c + 1) * P], ex[:, k],
                                                   start=(k == 0), stop=(k == EC - 1))
                    ins.then_inc(S["d_denp"], 1)
                    pe.wait_ge(S["d_att"], s + 1)
                    for n in range(NG + 1):
                        if n < NG:
                            g = n % 2
                            if n >= 2:
                                pe.wait_ge(S["d_va"], (s * NG + n - 1) * EC)
                            for c in range(EC):
                                nc.tensor.matmul(ps[:, 3 * g + c], hot_d[:, c * P:(c + 1) * P],
                                                 xv[:, n * QB:(n + 1) * QB].rearrange("p b c -> p (b c)"),
                                                 start=True, stop=True).then_inc(S["d_vp"], 1)
                        if n > 0:
                            m = n - 1
                            g = m % 2
                            pe.wait_ge(S["d_va"], (s * NG + m + 1) * EC)
                            if m > 0:
                                pe.wait_ge(S["d_y"], s * NG + m)
                            for b in range(QB):
                                for c in range(EC):
                                    ins = nc.tensor.matmul(ps[:, 6, b * T:(b + 1) * T], va[:, g, c, b], hot_sT[:, c],
                                                           start=(c == 0), stop=(c == EC - 1))
                            ins.then_inc(S["d_yp"], 1)
                            pe.wait_ge(S["d_y"], s * NG + m + 1)
                            if m >= 2:
                                pe.wait_ge(S["d_o"], s * NG + m - 1)
                            for b in range(QB):
                                ins = nc.tensor.matmul(ps[:, 3 * g + 2, b * C:(b + 1) * C], y3[:, g, b], w_out[:],
                                                       start=True, stop=True)
                            ins.then_inc(S["d_op"], 1)

                turn(0, True)
                with pe.Fori(1, SUPER) as s:
                    turn(s, False)


def kernel(x, adj, L0_gnn_Wg0, L0_gnn_bg0, L0_gnn_Wg1, L0_gnn_bg1, L0_gnn_Wih, L0_gnn_Whh, L0_gnn_bih, L0_gnn_bhh,
           L1_gnn_Wqkv, L1_gnn_Wo, L2_gnn_W, L2_gnn_bias, L3_gnn_W_lin, L3_gnn_W_val, L3_gnn_a, L3_gnn_W_out,
           L3_gnn_src, L3_gnn_dst):
    import numpy as np
    import concourse.bacc as bacc
    from concourse.bass_utils import run_bass_kernel_spmd

    def lay(a):
        return np.ascontiguousarray(a)

    skips, gates, hid = L0_gnn_Wih.shape
    a_rep = np.broadcast_to(np.asarray(L3_gnn_a).reshape(-1, 1), (L3_gnn_a.size, L3_gnn_a.shape[0]))
    laid = {
        "x_in": x, "adj": adj, "adjT": np.asarray(adj).T,
        "Wg0": L0_gnn_Wg0, "bg0": np.asarray(L0_gnn_bg0)[None, :],
        "Wg1": L0_gnn_Wg1, "bg1": np.asarray(L0_gnn_bg1)[None, :],
        "WihT": np.asarray(L0_gnn_Wih).reshape(skips * gates, hid).T,
        "WhhT": np.asarray(L0_gnn_Whh).reshape(skips * gates, hid).T,
        "bihT": np.asarray(L0_gnn_bih).reshape(-1, hid).T, "bhhT": np.asarray(L0_gnn_bhh).reshape(-1, hid).T,
        "WqkvT": np.asarray(L1_gnn_Wqkv).T, "Wo": L1_gnn_Wo,
        "W2": L2_gnn_W, "bias2": np.asarray(L2_gnn_bias)[None, :],
        "WlvT": np.concatenate([np.asarray(L3_gnn_W_lin).T, np.asarray(L3_gnn_W_val).T], axis=1),
        "a_col": a_rep, "WoutT": np.asarray(L3_gnn_W_out).T,
        "src_row": np.asarray(L3_gnn_src)[None, :], "src_col": np.asarray(L3_gnn_src).reshape(-1, 128).T,
        "dst_row": np.asarray(L3_gnn_dst)[None, :], "dst_col": np.asarray(L3_gnn_dst).reshape(-1, 128).T,
    }
    nc = bacc.Bacc("TRN2", target_bir_lowering=False, num_devices=1)
    arrays, args = {}, {}
    for name, a in laid.items():
        a = lay(a)
        arrays[f"in_{name}"] = a
        args[name] = nc.dram_tensor(f"in_{name}", a.shape, mybir.dt.from_np(a.dtype), kind="ExternalInput").ap()
    out = nc.dram_tensor("out", x.shape, F32, kind="ExternalOutput").ap()
    four_layers(nc, out=out, **args)
    return run_bass_kernel_spmd(nc, [arrays], core_ids=[0]).results[0]["out"]
```

```python
from contextlib import ExitStack

import concourse.bass as bass
from concourse import mybir

F32 = mybir.dt.float32
F32R = mybir.dt.float32r
I32 = mybir.dt.int32
ALU = mybir.AluOpType
ACT = mybir.ActivationFunctionType
AXX = mybir.AxisListType.X

P = 128
EPS = 1e-5
LOG_EPS = 1e-8
NEG = -1e30
CUT = -3e38
SLOPE = 0.2
I, F, G, O = range(4)


def sync_names(nc, ctx, names):
    return {n: ctx.enter_context(nc.semaphore(n)) for n in names.split()}


def four_layers(nc, x_in, adj, adjT, Wg0, bg0, Wg1, bg1, WihT, WhhT, bihT, bhhT, WqkvT, Wo, W2, bias2,
                WlvT, a_col, WoutT, src_row, src_col, dst_row, dst_col, out):
    B = x_in.shape[0]
    T = C = P
    SKIPS = WihT.shape[1] // (4 * P)
    HEADS = a_col.shape[1]
    DH = C // HEADS
    E = src_row.shape[1]
    EC = E // P
    NB = 16
    TURNS = B // NB

    with ExitStack() as ctx:
        def sb(name, shape, dt=F32):
            return ctx.enter_context(nc.sbuf_tensor(name, shape, dt))

        passed = ctx.enter_context(nc.semaphore("passed"))

        def wait_apart(eng, sem, value):
            eng.wait_ge(sem, value)
            eng.sem_inc(passed, 1)

        def scope():
            stack = ctx.enter_context(ExitStack())
            return stack, lambda name, shape, dt=F32: stack.enter_context(nc.sbuf_tensor(name, shape, dt))

        x = sb("x", [P, B, C])
        ps = ctx.enter_context(nc.psum_tensor("ps", [P, 8, 512], F32))

        ident = sb("ident", [P, P])
        ones = sb("ones", [P, P])
        w_g = sb("w_g", [P, 2, P])
        b_g = sb("b_g", [P, 2, P])
        b_lstm = sb("b_lstm", [P, SKIPS * 4])
        adjT_sb = sb("adjT_sb", [P, P])
        m_qk = sb("m_qk", [P, P])
        w_vo = sb("w_vo", [P, P])
        adj_causal = sb("adj_causal", [P, P])
        adj_ul = sb("adj_ul", [P, 2, P])
        diag_bc = sb("diag_bc", [P, P])
        w2_sb = sb("w2_sb", [P, 3, P])
        bias2_bc = sb("bias2_bc", [P, P])
        w_lv = sb("w_lv", [P, 2, P])
        w_out = sb("w_out", [P, P])
        a_blk = sb("a_blk", [P, HEADS])
        iota_p = sb("iota_p", [P, EC])
        hot_s = sb("hot_s", [P, E])
        hot_d = sb("hot_d", [P, E], F32R)
        hot_sd = sb("hot_sd", [P, E], F32R)
        hot_sT = sb("hot_sT", [P, EC, P])
        hot_dT = sb("hot_dT", [P, EC, P])
        same = sb("same", [P, EC, E])
        cut_f = sb("cut_f", [P, E])
        cut_b = sb("cut_b", [P, E])
        log_a = sb("log_a", [P, EC])
        half = sb("half", [P, NB])

        stats = sb("stats", [P, NB, 6])
        mv = sb("mv", [P, NB, 2])
        rstd = sb("rstd", [P, NB])
        hn = sb("hn", [P, NB, C])

        part0, tmp0 = scope()
        w_hi = tmp0("w_hi", [P, 2, SKIPS, 4, P], F32R)
        w_lo = tmp0("w_lo", [P, 2, SKIPS, 4, P], F32R)
        part, tmp = scope()
        w_raw = tmp("w_raw", [P, 2, SKIPS * 4 * P])
        b_ih = tmp("b_ih", [P, SKIPS * 4])
        b_hh = tmp("b_hh", [P, SKIPS * 4])
        adj_sb = tmp("adj_sb", [P, P])
        wqkvT = tmp("wqkvT", [P, 3, P])
        wo_sb = tmp("wo_sb", [P, P])
        adj_diag = tmp("adj_diag", [P, P])
        a_sb = tmp("a_sb", [P, HEADS])
        iota_e = tmp("iota_e", [P, E])
        ends_row = tmp("ends_row", [P, 2, E], I32)
        ends_rowf = tmp("ends_rowf", [P, 2, E])
        ends_col = tmp("ends_col", [P, 2, EC], I32)
        ends_colf = tmp("ends_colf", [P, EC, 2])
        key_row = tmp("key_row", [P, E])
        key_col = tmp("key_col", [P, EC])
        is_less = tmp("is_less", [P, E])
        rank = tmp("rank", [P, EC])
        perm = tmp("perm", [P, EC, E])
        rep = tmp("rep", [P, 2, EC, P])
        srt = tmp("srt", [P, 2, E])
        srt_col = tmp("srt_col", [P, EC, 2])
        picked = tmp("picked", [P, EC, P])
        S = sync_names(nc, ctx, "ld_x0 ld_x ld_w made pool_link dve_link act_link pe_link")
        with nc.Block() as block:

            @block.sync
            def _(sp):
                sp.dma_start(x[:, 0:NB, :], x_in[0:NB].rearrange("b t c -> t b c")).then_inc(S["ld_x0"], 16)
                for dst, s in ((w_g[:, 0], Wg0), (w_g[:, 1], Wg1), (w_raw[:, 0], WihT),
                               (w_raw[:, 1], WhhT), (b_ih[:], bihT), (b_hh[:], bhhT),
                               (adj_sb[:], adj), (adjT_sb[:], adjT),
                               (wqkvT[:], WqkvT.rearrange("(k d) c -> d k c", d=P)), (wo_sb[:], Wo),
                               (w2_sb[:], W2.rearrange("k f o -> f k o")),
                               (w_lv[:].rearrange("p k c -> p (k c)"), WlvT), (w_out[:], WoutT), (a_sb[:], a_col),
                               (b_g[:, 0], bg0.to_broadcast([P, P])), (b_g[:, 1], bg1.to_broadcast([P, P])),
                               (bias2_bc[:], bias2.to_broadcast([P, P])),
                               (ends_row[:, 0], src_row.to_broadcast([P, E])),
                               (ends_row[:, 1], dst_row.to_broadcast([P, E])),
                               (ends_col[:, 0], src_col), (ends_col[:, 1], dst_col)):
                    sp.dma_start(dst, s).then_inc(S["ld_w"], 16)
                for i in range(1, TURNS):
                    sp.dma_start(x[:, i * NB:(i + 1) * NB, :],
                                 x_in[i * NB:(i + 1) * NB].rearrange("b t c -> t b c")).then_inc(S["ld_x"], 16)
            n_w = 21 * 16

            @block.gpsimd
            def _(pool):
                n = [0]

                def link(ins):
                    n[0] += 1
                    ins.then_inc(S["pool_link"], 1)
                    pool.wait_ge(S["pool_link"], n[0])

                link(nc.gpsimd.memset(ident[:], 0.0))
                link(nc.gpsimd.memset(ones[:], 1.0))
                link(nc.gpsimd.memset(half[:], -0.5))
                link(nc.gpsimd.affine_select(out=ident[:], in_=ident[:], compare_op=ALU.not_equal, fill=1.0, base=0,
                                             pattern=[[-1, P]], channel_multiplier=1))
                link(nc.gpsimd.iota(iota_e[:], pattern=[[1, E]], base=0, channel_multiplier=0,
                                    allow_small_or_imprecise_dtypes=True))
                link(nc.gpsimd.iota(iota_p[:], pattern=[[P, EC]], base=0, channel_multiplier=1,
                                    allow_small_or_imprecise_dtypes=True))
                pool.wait_ge(S["ld_w"], n_w)
                link(nc.gpsimd.affine_select(out=adj_causal[:], in_=adj_sb[:], compare_op=ALU.is_ge, fill=NEG,
                                             base=0, pattern=[[-1, P]], channel_multiplier=1))
                link(nc.gpsimd.affine_select(out=adj_ul[:, 0], in_=adjT_sb[:], compare_op=ALU.is_gt, fill=0.0,
                                             base=0, pattern=[[-1, P]], channel_multiplier=1))
                link(nc.gpsimd.affine_select(out=adj_ul[:, 1], in_=adjT_sb[:], compare_op=ALU.is_gt, fill=0.0,
                                             base=0, pattern=[[1, P]], channel_multiplier=-1))
                link(nc.gpsimd.affine_select(out=adj_diag[:], in_=adjT_sb[:], compare_op=ALU.is_equal, fill=0.0,
                                             base=0, pattern=[[1, P]], channel_multiplier=-1))
                link(nc.gpsimd.affine_select(out=a_blk[:], in_=a_sb[:], compare_op=ALU.is_ge, fill=0.0,
                                             base=0, pattern=[[-DH, HEADS]], channel_multiplier=1))
                link(nc.gpsimd.affine_select(out=a_blk[:], in_=a_blk[:], compare_op=ALU.is_ge, fill=0.0,
                                             base=DH - 1, pattern=[[DH, HEADS]], channel_multiplier=-1))
                nc.gpsimd.memset(log_a[:], 0.0).then_inc(S["made"], 1)

            @block.vector
            def _(dve):
                n = [0]

                def link(ins):
                    n[0] += 1
                    ins.then_inc(S["dve_link"], 1)
                    dve.wait_ge(S["dve_link"], n[0])

                dve.wait_ge(S["ld_w"], n_w)
                dve.wait_ge(S["made"], 1)
                link(nc.vector.tensor_tensor(b_lstm[:], b_ih[:], b_hh[:], ALU.add))
                link(nc.vector.tensor_copy(ends_rowf[:], ends_row[:]))
                link(nc.vector.tensor_copy(ends_colf[:].rearrange("p c k -> p k c"), ends_col[:]))
                link(nc.vector.scalar_tensor_tensor(key_row[:], ends_rowf[:, 0], float(E), iota_e[:],
                                                    ALU.mult, ALU.add))
                link(nc.vector.scalar_tensor_tensor(key_col[:], ends_colf[:, :, 0], float(E), iota_p[:],
                                                    ALU.mult, ALU.add))
                for c in range(EC):
                    link(nc.vector.tensor_scalar(is_less[:], key_row[:], key_col[:, c:c + 1], None, ALU.is_lt,
                                                 ALU.add, accum_out=rank[:, c:c + 1]))
                    link(nc.vector.tensor_scalar(perm[:, c], iota_e[:], rank[:, c:c + 1], None, ALU.is_equal))
                    for k in range(2):
                        link(nc.vector.tensor_scalar(rep[:, k, c], ones[:], ends_colf[:, c, k:k + 1], None, ALU.mult))
                w_all = w_raw[:].rearrange("p a n -> p (a n)")
                link(nc.vector.tensor_copy(w_hi[:].rearrange("p a s g h -> p (a s g h)"), w_all))
                link(nc.vector.tensor_tensor(w_lo[:].rearrange("p a s g h -> p (a s g h)"), w_all,
                                             w_hi[:].rearrange("p a s g h -> p (a s g h)").bitcast(F32),
                                             ALU.subtract))
                nc.vector.memset(is_less[:], 0.0).then_inc(S["made"], 1)
                dve.wait_ge(S["pe_link"], 1)
                link(nc.vector.tensor_copy(srt[:].rearrange("p k e -> p (k e)"), ps[:, 0, :]))
                link(nc.vector.tensor_copy(srt_col[:], ps[:, 1, 0:2 * EC].rearrange("p (c k) -> p c k", k=2)))
                link(nc.vector.tensor_copy(diag_bc[:], ps[:, 2, 0:P]))
                link(nc.vector.tensor_scalar(m_qk[:], ps[:, 3, 0:P], float(C) ** -0.5, None, ALU.mult))
                link(nc.vector.tensor_copy(w_vo[:], ps[:, 3, P:2 * P]))
                link(nc.vector.tensor_scalar(hot_s[:], srt[:, 0], iota_p[:, 0:1], None, ALU.is_equal))
                link(nc.vector.tensor_scalar(hot_d[:], srt[:, 1], iota_p[:, 0:1], None, ALU.is_equal))
                link(nc.vector.tensor_tensor(hot_sd[:], hot_s[:], hot_d[:].bitcast(F32), ALU.add))
                nc.vector.memset(is_less[:], 0.0).then_inc(S["made"], 1)
                for c in range(EC):
                    link(nc.vector.tensor_scalar(hot_sT[:, c], iota_e[:, 0:P], srt_col[:, c, 0:1], None, ALU.is_equal))
                    link(nc.vector.tensor_scalar(hot_dT[:, c], iota_e[:, 0:P], srt_col[:, c, 1:2], None, ALU.is_equal))
                    link(nc.vector.tensor_scalar(same[:, c], srt[:, 0], srt_col[:, c, 0:1], None, ALU.is_equal))
                link(nc.vector.memset(cut_f[:, 0:1], CUT))
                link(nc.vector.memset(cut_b[:, E - 1:E], CUT))
                link(nc.vector.tensor_tensor(is_less[:, 1:E], srt[:, 0, 1:E], srt[:, 0, 0:E - 1], ALU.not_equal))
                link(nc.vector.tensor_scalar(cut_f[:, 1:E], is_less[:, 1:E], CUT, None, ALU.mult))
                link(nc.vector.tensor_copy(cut_b[:, 0:E - 1], cut_f[:, 1:E]))
                dve.wait_ge(S["pe_link"], 2)
                link(nc.vector.tensor_tensor(picked[:], ps[:, 4, 0:EC * P].rearrange("p (c m) -> p c m", c=EC),
                                             hot_dT[:], ALU.mult))
                link(nc.vector.tensor_reduce(rank[:], picked[:], AXX, ALU.add))
                nc.vector.tensor_scalar(rank[:], rank[:], LOG_EPS, None, ALU.add).then_inc(S["made"], 1)

            @block.scalar
            def _(act):
                act.wait_ge(S["made"], 4)
                nc.scalar.activation(log_a[:], rank[:], ACT.Ln).then_inc(S["act_link"], 1)

            @block.tensor
            def _(pe):
                pe.wait_ge(S["made"], 2)
                for k in range(2):
                    for c in range(EC):
                        nc.tensor.matmul(ps[:, 0, k * E:(k + 1) * E], rep[:, k, c], perm[:, c],
                                         start=(c == 0), stop=(c == EC - 1))
                for r in range(EC):
                    for c in range(EC):
                        nc.tensor.matmul(ps[:, 1, 2 * r:2 * r + 2], perm[:, c, r * P:(r + 1) * P], ends_colf[:, c],
                                         start=(c == 0), stop=(c == EC - 1))
                nc.tensor.matmul(ps[:, 2, 0:P], ones[:], adj_diag[:], start=True, stop=True)
                nc.tensor.matmul(ps[:, 3, 0:P], wqkvT[:, 0], wqkvT[:, 1], start=True, stop=True)
                nc.tensor.matmul(ps[:, 3, P:2 * P], wqkvT[:, 2], wo_sb[:], start=True, stop=True).then_inc(
                    S["pe_link"], 1)
                pe.wait_ge(S["made"], 3)
                for c in range(EC):
                    last = nc.tensor.matmul(ps[:, 4, c * P:(c + 1) * P], hot_s[:, c * P:(c + 1) * P], adj_sb[:],
                                            start=True, stop=True)
                last.then_inc(S["pe_link"], 1)

        part.close()


        def norm_stats(b0, k, n, done, slot=0):
            for j in range(k, k + n):
                nc.vector.bn_stats(stats[:, slot + j],
                                   x[:, bass.ds(b0 + j, 1), :].rearrange("p a c -> p (a c)")).then_inc(done, 1)

        def norm_aggr(k, n, done):
            for j in range(k, k + n):
                nc.vector.bn_aggr(mv[:, j], stats[:, j]).then_inc(done, 1)

        def norm_apply(b0, k, n, done, slot=0):
            for j in range(k, k + n):
                nc.vector.tensor_scalar(hn[:, slot + j], x[:, bass.ds(b0 + j, 1), :].rearrange("p a c -> p (a c)"),
                                        mv[:, slot + j, 0:1], rstd[:, slot + j:slot + j + 1], ALU.subtract,
                                        ALU.mult).then_inc(done, 1)

        GB = NB // 2
        CH = GB * T // 512
        CB = 512 // T
        hT = tmp0("hT", [P, 2, GB, T])
        u = tmp0("u", [P, 2, GB, C])
        H = tmp0("H", [P, 2, GB, T])
        H_hi = tmp0("H_hi", [P, 2, GB, T], F32R)
        H_lo = tmp0("H_lo", [P, 2, GB, T], F32R)
        hid_hi = tmp0("hid_hi", [P, 2, 512], F32R)
        hid_lo = tmp0("hid_lo", [P, 2, 512], F32R)
        gate = tmp0("gate", [P, 2, 4, 512])
        cell = tmp0("cell", [P, 2, 512])
        hid = tmp0("hid", [P, 2, 512])
        tanh_c = tmp0("tanh_c", [P, 2, 512])

        steps = []
        for p in range(1, SKIPS + 1):
            nb = min(GB, 512 // (T // p))
            for b0 in range(0, GB, nb):
                steps += [(p, j, j == p - 1, b0, nb, T // p) for j in range(p)]
        NS = len(steps)
        gates_of = [(I, G, O) if st[1] == 0 else (I, G, F, O) for st in steps]
        gates_before = [sum(len(z) for z in gates_of[:k]) for k in range(NS + 1)]
        parts_before = [sum(2 for st in steps[:k] if st[1] > 0) for k in range(NS + 1)]
        TG, TP = gates_before[NS], parts_before[NS]

        TRANSPOSE, U0, A0, U1, A1, STEP = range(6)
        OUT = STEP + NS
        ITEMS = OUT + 1
        BEHIND = 1

        def interleave(engine, item):
            def turn(i, first, last):
                for n in range(ITEMS):
                    item(i, 0, n, not last, not first)
                    if n >= BEHIND:
                        item(i, 1, n - BEHIND, not last, not first)
                    elif not first:
                        item(i - 1, 1, n - BEHIND + ITEMS, True, True)

            turn(0, True, False)
            with engine.Fori(1, TURNS - 1) as i:
                turn(i, False, False)
            turn(TURNS - 1, False, True)
            for n in range(ITEMS - BEHIND, ITEMS):
                item(TURNS - 1, 1, n, False, True)

        def at(buf, p, j, b0, nb, w):
            return buf[:, b0:b0 + nb, j:j + p * (w - 1) + 1:p]

        inner = [not st[2] for st in steps[:-1]]

        def lo_sem(g, k):
            return sa(g, "a_lo" if inner[k] else "a_lo_end")

        def lo_count(i, k):
            kinds = [z == inner[k] for z in inner]
            return i * sum(kinds) + sum(kinds[:k + 1])

        def flat(buf, nb, w):
            return buf[:, 0:nb * w].rearrange("p (b w) -> p b w", b=nb)

        def hidden(k, g):
            p, j, last, b0, nb, w = steps[k]
            if last:
                return [at(h[:, g], p, j, b0, nb, w) for h in (H, H_hi, H_lo)]
            return [flat(h[:, g], nb, w) for h in (hid, hid_hi, hid_lo)]

        ld_x, ld_x0 = S["ld_x"], S["ld_x0"]
        A = [sync_names(nc, ctx, " ".join(f"{n}{g}" for n in
                                          "a_stats a_aggr a_var a_rstd a_hn a_hTp a_hT a_up a_u a_Hp a_H a_gatep "
                                          "a_gate a_Hlo a_part a_cell a_tanh a_hid a_h32 a_lo a_lo_end a_outp a_out".split()))
             for g in range(2)]

        def sa(g, name):
            return A[g][f"{name}{g}"]

        with nc.Block() as block:
            @block.gpsimd
            def _(pool):
                def make_rstd(i, g):
                    wait_apart(pool, sa(g, "a_aggr"), i * GB + GB)
                    r = rstd[:, g * GB:(g + 1) * GB]
                    nc.gpsimd.tensor_scalar(r, mv[:, g * GB:(g + 1) * GB, 1], EPS, None, ALU.add).then_inc(
                        sa(g, "a_var"), 1)
                    pool.wait_ge(sa(g, "a_var"), i + 1)
                    nc.gpsimd.tensor_tensor(r, r, half[:, 0:GB], ALU.pow).then_inc(sa(g, "a_rstd"), 1)

                def item(i, g, n, more, _):
                    k = n - STEP
                    if 0 <= k < NS - 1 and not steps[k][2]:
                        h32, h_hi, h_lo = hidden(k, g)
                        pool.wait_ge(sa(g, "a_h32"), i * (NS - 1) + k + 1)
                        nc.gpsimd.tensor_tensor(h_lo, h32, h_hi.bitcast(F32), ALU.subtract).then_inc(
                            sa(g, "a_lo"), 1)
                    if k == 5 and more:
                        make_rstd(i + 1, g)

                make_rstd(0, 0)
                make_rstd(0, 1)
                interleave(pool, item)

            @block.vector
            def _(dve):
                def norm_piece(i, g, k):
                    b0 = i * NB + g * GB
                    if k < 4:
                        if k == 0:
                            dve.wait_ge(ld_x, 16 * (TURNS - 1))
                        norm_stats(b0, 2 * k, 2, sa(g, "a_stats"), g * GB)
                    elif k == 4:
                        wait_apart(dve, sa(g, "a_stats"), i * GB + GB)
                        norm_aggr(g * GB, GB, sa(g, "a_aggr"))
                    elif 7 <= k < 11:
                        if k == 7:
                            dve.wait_ge(sa(g, "a_rstd"), i + 1)
                        norm_apply(b0, 2 * (k - 7), 2, sa(g, "a_hn"), g * GB)

                def item(i, g, n, more, _):
                    if n in (U0, U1):
                        s = (n == U1)
                        for c in range(CH):
                            dve.wait_ge(sa(g, "a_up"), i * 2 * CH + s * CH + c + 1)
                            nc.vector.tensor_tensor(
                                u[:, g, c * CB:(c + 1) * CB],
                                ps[:, 4 * g + 2 + c].rearrange("p (b c) -> p b c", b=CB),
                                b_g[:, int(s)].unsqueeze(1).to_broadcast([P, CB, C]), ALU.add).then_inc(
                                    sa(g, "a_u"), 1)
                    elif n == A1:
                        for c in range(CH):
                            dve.wait_ge(sa(g, "a_H"), i * 2 * CH + CH + c + 1)
                            nc.vector.scalar_tensor_tensor(
                                H_lo[:, g, c * CB:(c + 1) * CB].rearrange("p b t -> p (b t)"), ps[:, 4 * g + c], 0.0,
                                H_hi[:, g, c * CB:(c + 1) * CB].rearrange("p b t -> p (b t)").bitcast(F32),
                                ALU.max, ALU.subtract).then_inc(sa(g, "a_Hlo"), 1)
                    elif n == OUT:
                        for c in range(CH):
                            dve.wait_ge(sa(g, "a_outp"), i * CH + c + 1)
                            xs = x[:, bass.ds(i * NB + g * GB + c * CB, CB), :]
                            nc.vector.tensor_tensor(xs, xs, ps[:, 4 * g + c].rearrange("p (b c) -> p b c", b=CB),
                                                    ALU.add).then_inc(sa(g, "a_out"), 1)
                    elif n >= STEP:
                        k = n - STEP
                        p, j, last, b0, nb, w = steps[k]
                        n0 = i * TG + gates_before[k]
                        gi, gf, gg, go = (flat(gate[:, g, z], nb, w) for z in (I, F, G, O))
                        cc = flat(cell[:, g], nb, w)
                        dve.wait_ge(sa(g, "a_gate"), n0 + 2)
                        if j == 0:
                            nc.vector.tensor_tensor(cc, gi, gg, ALU.mult).then_inc(sa(g, "a_cell"), 1)
                        else:
                            nc.vector.tensor_tensor(gi, gi, gg, ALU.mult).then_inc(sa(g, "a_part"), 1)
                            dve.wait_ge(sa(g, "a_gate"), n0 + 3)
                            nc.vector.tensor_tensor(cc, cc, gf, ALU.mult).then_inc(sa(g, "a_part"), 1)
                            dve.wait_ge(sa(g, "a_part"), i * TP + parts_before[k] + 2)
                            nc.vector.tensor_tensor(cc, cc, gi, ALU.add).then_inc(sa(g, "a_cell"), 1)
                        if more:
                            norm_piece(i + 1, g, k)
                        h32, h_hi, _lo = hidden(k, g)
                        tc = flat(tanh_c[:, g], nb, w)
                        dve.wait_ge(sa(g, "a_tanh"), i * NS + k + 1)
                        if k < NS - 1:
                            nc.vector.tensor_tensor(h_hi, go, tc, ALU.mult).then_inc(sa(g, "a_hid"), 1)
                            nc.vector.tensor_tensor(h32, go, tc, ALU.mult).then_inc(sa(g, "a_h32"), 1)
                            if last:
                                dve.wait_ge(sa(g, "a_h32"), i * (NS - 1) + k + 1)
                                nc.vector.tensor_tensor(_lo, h32, h_hi.bitcast(F32), ALU.subtract).then_inc(
                                    sa(g, "a_lo_end"), 1)
                        else:
                            nc.vector.tensor_tensor(h32, go, tc, ALU.mult).then_inc(sa(g, "a_hid"), 1)

                dve.wait_ge(ld_x0, 16)
                for g in range(2):
                    norm_stats(g * GB, 0, GB, sa(g, "a_stats"), g * GB)
                for g in range(2):
                    wait_apart(dve, sa(g, "a_stats"), GB)
                    norm_aggr(g * GB, GB, sa(g, "a_aggr"))
                for g in range(2):
                    dve.wait_ge(sa(g, "a_rstd"), 1)
                    norm_apply(g * GB, 0, GB, sa(g, "a_hn"), g * GB)
                interleave(dve, item)

            @block.scalar
            def _(act):
                def item(i, g, n, *_):
                    if n == TRANSPOSE:
                        for c in range(CH):
                            act.wait_ge(sa(g, "a_hTp"), i * CH + c + 1)
                            nc.scalar.activation(hT[:, g, c * CB:(c + 1) * CB],
                                                 ps[:, 4 * g + c].rearrange("p (b t) -> p b t", b=CB),
                                                 ACT.Relu).then_inc(sa(g, "a_hT"), 1)
                    elif n in (A0, A1):
                        s = (n == A1)
                        dst = H_hi if s else hT
                        for c in range(CH):
                            act.wait_ge(sa(g, "a_Hp"), i * 2 * CH + s * CH + c + 1)
                            nc.scalar.activation(dst[:, g, c * CB:(c + 1) * CB],
                                                 ps[:, 4 * g + c].rearrange("p (b t) -> p b t", b=CB),
                                                 ACT.Relu).then_inc(sa(g, "a_H"), 1)
                    elif STEP <= n < OUT:
                        k = n - STEP
                        p, j, last, b0, nb, w = steps[k]
                        for m, z in enumerate(gates_of[k]):
                            act.wait_ge(sa(g, "a_gatep"), i * TG + gates_before[k] + m + 1)
                            nc.scalar.activation(gate[:, g, z, 0:nb * w], ps[:, 4 * g + m, 0:nb * w],
                                                 ACT.Tanh if z == G else ACT.Sigmoid,
                                                 bias=b_lstm[:, 4 * (p - 1) + z:4 * (p - 1) + z + 1]).then_inc(
                                                     sa(g, "a_gate"), 1)
                        act.wait_ge(sa(g, "a_cell"), i * NS + k + 1)
                        nc.scalar.activation(tanh_c[:, g, 0:nb * w], cell[:, g, 0:nb * w],
                                             ACT.Tanh).then_inc(sa(g, "a_tanh"), 1)

                interleave(act, item)

            @block.tensor
            def _(pe):
                def step(i, g, k):
                    p, j, _, b0, nb, w = steps[k]
                    gates = list(enumerate(gates_of[k]))

                    def term(m, z, src, v_hi, v_lo, start, stop, half):
                        dst = ps[:, 4 * g + m, 0:nb * w]
                        if half == 0:
                            nc.tensor.matmul(dst, w_hi[:, src, p - 1, z], v_hi, start=start, stop=False)
                            return nc.tensor.matmul(dst, w_lo[:, src, p - 1, z], v_hi, start=False, stop=False)
                        return nc.tensor.matmul(dst, w_hi[:, src, p - 1, z], v_lo, start=False, stop=stop)

                    v = (at(H_hi[:, g], p, j, b0, nb, w), at(H_lo[:, g], p, j, b0, nb, w))
                    src = 0
                    if k == 0:
                        pe.wait_ge(sa(g, "a_Hlo"), i * CH + CH)
                    elif j > 0:
                        pe.wait_ge(sa(g, "a_gate"), i * TG + gates_before[k])
                        for m, z in gates:
                            term(m, z, 0, *v, True, False, 0)
                            term(m, z, 0, *v, True, False, 1)
                        v = (hid_hi[:, g, 0:nb * w], hid_lo[:, g, 0:nb * w])
                        src = 1
                    if k > 0:
                        pe.wait_ge(sa(g, "a_hid"), i * NS + k)
                    for m, z in gates[:2]:
                        term(m, z, src, *v, j == 0, True, 0)
                    if k > 0:
                        pe.wait_ge(lo_sem(g, k - 1), lo_count(i, k - 1))
                    for m, z in gates[:2]:
                        term(m, z, src, *v, j == 0, True, 1).then_inc(sa(g, "a_gatep"), 1)
                    for m, z in gates[2:]:
                        term(m, z, src, *v, j == 0, True, 0)
                        term(m, z, src, *v, j == 0, True, 1).then_inc(sa(g, "a_gatep"), 1)

                def item(i, g, n, more, before):
                    if n == TRANSPOSE:
                        for c in range(CH):
                            if before:
                                pe.wait_ge(sa(g, "a_out"), i * CH - CH + c + 1)
                            pe.wait_ge(sa(g, "a_hn"), i * GB + (c + 1) * CB)
                            for b in range(CB):
                                ins = nc.tensor.transpose(ps[:, 4 * g + c, b * T:(b + 1) * T],
                                                          hn[:, g * GB + c * CB + b], ident[:])
                            ins.then_inc(sa(g, "a_hTp"), 1)
                    elif n in (U0, U1):
                        s = (n == U1)
                        for c in range(CH):
                            if s:
                                pe.wait_ge(sa(g, "a_H"), i * 2 * CH + c + 1)
                            else:
                                pe.wait_ge(sa(g, "a_hT"), i * CH + c + 1)
                            for b in range(CB):
                                ins = nc.tensor.matmul(ps[:, 4 * g + 2 + c, b * C:(b + 1) * C],
                                                       hT[:, g, c * CB + b], w_g[:, int(s)], start=True, stop=True)
                            ins.then_inc(sa(g, "a_up"), 1)
                    elif n in (A0, A1):
                        s = (n == A1)
                        for c in range(CH):
                            pe.wait_ge(sa(g, "a_u"), i * 2 * CH + s * CH + c + 1)
                            for b in range(CB):
                                ins = nc.tensor.matmul(ps[:, 4 * g + c, b * T:(b + 1) * T], u[:, g, c * CB + b],
                                                       adjT_sb[:], start=True, stop=True)
                            ins.then_inc(sa(g, "a_Hp"), 1)
                    elif n == OUT:
                        for c in range(CH):
                            pe.wait_ge(sa(g, "a_hid"), i * NS + NS)
                            for b in range(CB):
                                ins = nc.tensor.transpose(ps[:, 4 * g + c, b * T:(b + 1) * T],
                                                          H[:, g, c * CB + b], ident[:])
                            ins.then_inc(sa(g, "a_outp"), 1)
                    else:
                        step(i, g, n - STEP)

                interleave(pe, item)

        part0.close()

        part, tmp = scope()
        W1 = 4
        QB = NB // W1
        hT1 = tmp("hT1", [P, W1, QB, T])
        hmT = tmp("hmT", [P, W1, QB, T])
        val = tmp("val", [P, W1, QB, C])
        prob = tmp("prob", [P, W1, QB, T])
        probT = tmp("probT", [P, W1, QB, T])
        nmax = tmp("nmax", [P, NB])
        rsum = tmp("rsum", [P, NB])
        rinv = tmp("rinv", [P, NB])
        S = sync_names(nc, ctx, "b_stats b_aggr b_var b_rstd b_hn b_hTp b_hT b_qp b_q b_vp b_v b_sp b_s b_max b_e b_pTp "
                                "b_pT b_op b_inv b_o")
        HT, PT, QK, VAL, SCORE, OUT1, EXP, STATS, APPLY = range(9)
        BESIDE = [(HT, 0), (PT, 2), (QK, 0), (VAL, 0), (EXP, 1), (SCORE, 0), (STATS, 0), (OUT1, 2), (APPLY, 1)]

        def pipeline(engine, stage):
            def turn(i, first, last):
                for step in range(W1):
                    for what, behind in BESIDE:
                        g = step - behind
                        if g >= 0:
                            stage(i, what, g, not last, not first)
                        elif not first:
                            stage(i - 1, what, g + W1, True, True)

            turn(0, True, False)
            with engine.Fori(1, TURNS - 1) as i:
                turn(i, False, False)
            turn(TURNS - 1, False, True)
            for step in range(max(behind for _, behind in BESIDE)):
                for what, behind in BESIDE:
                    if behind > step:
                        stage(TURNS - 1, what, step - behind + W1, False, True)

        BANK = {HT: (0, 0), QK: (1, 1), VAL: (2, 2), PT: (3, 3), SCORE: (4, 5), OUT1: (6, 7)}

        def bank(what, g):
            return ps[:, BANK[what][g % 2]]

        def by4(ap, n=QB):
            return ap.rearrange("p (b t) -> p b t", b=n)

        def group_rstd(pool, s, count, g):
            r = rstd[:, g * QB:(g + 1) * QB]
            wait_apart(pool, s["aggr"], count * QB + QB)
            nc.gpsimd.tensor_scalar(r, mv[:, g * QB:(g + 1) * QB, 1], EPS, None, ALU.add).then_inc(s["var"], 1)
            pool.wait_ge(s["var"], count + 1)
            nc.gpsimd.tensor_tensor(r, r, half[:, 0:QB], ALU.pow).then_inc(s["rstd"], 1)

        NORM = {n: S["b_" + n] for n in ("stats", "aggr", "var", "rstd")}
        with nc.Block() as block:
            @block.gpsimd
            def _(pool):
                def stage(i, what, g, more, before):
                    if what == STATS and more:
                        group_rstd(pool, NORM, i * W1 + W1 + g, g)

                for g in range(W1):
                    group_rstd(pool, NORM, g, g)
                pipeline(pool, stage)

            @block.vector
            def _(dve):
                def stage(i, what, g, more, before):
                    count = i * W1 + g + 1
                    if what == SCORE:
                        dve.wait_ge(S["b_sp"], count)
                        nc.vector.tensor_tensor(prob[:, g], by4(bank(SCORE, g)),
                                                adj_causal[:].unsqueeze(1).to_broadcast([P, QB, T]),
                                                ALU.add).then_inc(S["b_s"], 1)
                        dve.wait_ge(S["b_s"], count)
                        nc.vector.tensor_reduce(nmax[:, g * QB:(g + 1) * QB], prob[:, g], AXX, ALU.max,
                                                negate=True).then_inc(S["b_max"], 1)
                    elif what == STATS and more:
                        norm_stats((i + 1) * NB, g * QB, QB, S["b_stats"])
                        wait_apart(dve, S["b_stats"], (i + 1) * NB + (g + 1) * QB)
                        norm_aggr(g * QB, QB, S["b_aggr"])
                    elif what == OUT1:
                        dve.wait_ge(S["b_e"], count)
                        nc.vector.reciprocal(rinv[:, g * QB:(g + 1) * QB], rsum[:, g * QB:(g + 1) * QB]).then_inc(
                            S["b_inv"], 1)
                        dve.wait_ge(S["b_op"], count)
                        dve.wait_ge(S["b_inv"], count)
                        for b in range(QB):
                            xs = x[:, bass.ds(i * NB + g * QB + b, 1), :].rearrange("p a c -> p (a c)")
                            ins = nc.vector.scalar_tensor_tensor(xs, bank(OUT1, g)[:, b * C:(b + 1) * C],
                                                                 rinv[:, g * QB + b:g * QB + b + 1], xs,
                                                                 ALU.mult, ALU.add)
                        ins.then_inc(S["b_o"], 1)
                    elif what == APPLY and more:
                        dve.wait_ge(S["b_hTp"], count)
                        dve.wait_ge(S["b_rstd"], count + W1)
                        norm_apply((i + 1) * NB, g * QB, QB, S["b_hn"])

                for g in range(W1):
                    norm_stats(0, g * QB, QB, S["b_stats"])
                    wait_apart(dve, S["b_stats"], (g + 1) * QB)
                    norm_aggr(g * QB, QB, S["b_aggr"])
                for g in range(W1):
                    dve.wait_ge(S["b_rstd"], g + 1)
                    norm_apply(0, g * QB, QB, S["b_hn"])
                pipeline(dve, stage)

            @block.scalar
            def _(act):
                def copy(sem, count, dst, src, done, func=ACT.Copy):
                    act.wait_ge(sem, count)
                    nc.scalar.activation(dst, by4(src), func).then_inc(done, 1)

                def stage(i, what, g, more, before):
                    count = i * W1 + g + 1
                    if what == HT:
                        copy(S["b_hTp"], count, hT1[:, g], bank(HT, g), S["b_hT"], ACT.Relu)
                    elif what == QK:
                        copy(S["b_qp"], count, hmT[:, g], bank(QK, g), S["b_q"])
                    elif what == VAL:
                        copy(S["b_vp"], count, val[:, g], bank(VAL, g), S["b_v"])
                    elif what == EXP:
                        act.wait_ge(S["b_max"], count)
                        for b in range(QB):
                            n = g * QB + b
                            ins = nc.scalar.activation(prob[:, g, b], prob[:, g, b], ACT.Exp, bias=nmax[:, n:n + 1],
                                                       accum_out=rsum[:, n:n + 1])
                        ins.then_inc(S["b_e"], 1)
                    elif what == PT:
                        copy(S["b_pTp"], count, probT[:, g], bank(PT, g), S["b_pT"])

                pipeline(act, stage)

            @block.tensor
            def _(pe):
                def four(dst, product, done):
                    for b in range(QB):
                        ins = product(dst[:, b * T:(b + 1) * T], b)
                    ins.then_inc(done, 1)

                def stage(i, what, g, more, before):
                    count = i * W1 + g + 1
                    if what == HT:
                        pe.wait_ge(S["b_hn"], count * QB)
                        four(bank(HT, g), lambda dst, b: nc.tensor.transpose(dst, hn[:, g * QB + b], ident[:]),
                             S["b_hTp"])
                    elif what == QK:
                        pe.wait_ge(S["b_hT"], count)
                        nc.tensor.matmul(bank(QK, g), m_qk[:], hT1[:, g].rearrange("p b t -> p (b t)"),
                                         start=True, stop=True).then_inc(S["b_qp"], 1)
                    elif what == VAL:
                        if before or g > 0:
                            pe.wait_ge(S["b_v"], count - 1)
                        four(bank(VAL, g), lambda dst, b: nc.tensor.matmul(dst, hT1[:, g, b], w_vo[:],
                                                                           start=True, stop=True), S["b_vp"])
                    elif what == SCORE:
                        pe.wait_ge(S["b_q"], count)
                        if before or g > 1:
                            pe.wait_ge(S["b_s"], count - 2)
                        four(bank(SCORE, g), lambda dst, b: nc.tensor.matmul(dst, hmT[:, g, b], hT1[:, g, b],
                                                                             start=True, stop=True), S["b_sp"])
                    elif what == PT:
                        pe.wait_ge(S["b_e"], count)
                        four(bank(PT, g), lambda dst, b: nc.tensor.transpose(dst, prob[:, g, b], ident[:]),
                             S["b_pTp"])
                    elif what == OUT1:
                        pe.wait_ge(S["b_pT"], count)
                        pe.wait_ge(S["b_v"], count)
                        if before or g > 1:
                            pe.wait_ge(S["b_o"], count - 2)
                        four(bank(OUT1, g), lambda dst, b: nc.tensor.matmul(dst, probT[:, g, b], val[:, g, b],
                                                                            start=True, stop=True), S["b_op"])

                pipeline(pe, stage)

        part.close()

        part, tmp = scope()
        hr = tmp("hr2", [P, NB, C])
        z0 = tmp("z0", [P, W1, QB, T])
        z12 = tmp("z12", [P, W1, QB, 2, T])
        xb = tmp("xb", [P, NB, C])
        S = sync_names(nc, ctx, "c_stats c_aggr c_var c_rstd c_hn c_hr c_xb c_zp c_z0 c_z12 c_op c_o")
        NORM2 = {n: S["c_" + n] for n in ("stats", "aggr", "var", "rstd")}

        def one_behind(engine, spread, gather):
            def turn(i, first, last):
                for g in range(W1):
                    spread(i, g, not last, not first)
                    if g > 0:
                        gather(i, g - 1, not last, not first)
                    elif not first:
                        gather(i - 1, W1 - 1, True, True)

            turn(0, True, False)
            with engine.Fori(1, TURNS - 1) as i:
                turn(i, False, False)
            turn(TURNS - 1, False, True)
            gather(TURNS - 1, W1 - 1, False, True)

        with nc.Block() as block:
            @block.gpsimd
            def _(pool):
                def relu(i, g):
                    wait_apart(pool, S["c_hn"], (i * W1 + g + 1) * QB)
                    nc.gpsimd.tensor_scalar(hr[:, g * QB:(g + 1) * QB], hn[:, g * QB:(g + 1) * QB], 0.0, None,
                                            ALU.max).then_inc(S["c_hr"], 1)

                def spread(i, g, more, before):
                    if before:
                        pool.wait_ge(S["c_o"], i * W1 - W1 + g + 1)
                    nc.gpsimd.tensor_tensor(xb[:, g * QB:(g + 1) * QB], x[:, bass.ds(i * NB + g * QB, QB), :],
                                            bias2_bc[:].unsqueeze(1).to_broadcast([P, QB, C]),
                                            ALU.add).then_inc(S["c_xb"], 1)
                    if more:
                        group_rstd(pool, NORM2, i * W1 + W1 + g, g)

                def gather(i, g, more, before):
                    if more:
                        relu(i + 1, g)

                for g in range(W1):
                    group_rstd(pool, NORM2, g, g)
                    relu(0, g)
                one_behind(pool, spread, gather)

            @block.vector
            def _(dve):
                def spread(i, g, more, before):
                    dve.wait_ge(S["c_zp"], i * W1 + g + 1)
                    nc.vector.scalar_tensor_tensor(z0[:, g], by4(ps[:, 4 * (g % 2)]), 0.0,
                                                   diag_bc[:].unsqueeze(1).to_broadcast([P, QB, T]),
                                                   ALU.max, ALU.mult).then_inc(S["c_z0"], 1)
                    if more:
                        norm_stats((i + 1) * NB, g * QB, QB, S["c_stats"])

                def gather(i, g, more, before):
                    dve.wait_ge(S["c_xb"], i * W1 + g + 1)
                    dve.wait_ge(S["c_op"], i * W1 + g + 1)
                    nc.vector.tensor_tensor(x[:, bass.ds(i * NB + g * QB, QB), :], by4(ps[:, 4 * (g % 2) + 3]),
                                            xb[:, g * QB:(g + 1) * QB], ALU.add).then_inc(S["c_o"], 1)
                    if more:
                        dve.wait_ge(S["c_rstd"], (i + 1) * W1 + g + 1)
                        norm_apply((i + 1) * NB, g * QB, QB, S["c_hn"])

                def aggr(i, g, more, before):
                    if more:
                        wait_apart(dve, S["c_stats"], (i + 1) * NB + (g + 1) * QB)
                        norm_aggr(g * QB, QB, S["c_aggr"])

                for g in range(W1):
                    norm_stats(0, g * QB, QB, S["c_stats"])
                    wait_apart(dve, S["c_stats"], (g + 1) * QB)
                    norm_aggr(g * QB, QB, S["c_aggr"])
                for g in range(W1):
                    dve.wait_ge(S["c_rstd"], g + 1)
                    norm_apply(0, g * QB, QB, S["c_hn"])

                def spread_and_aggr(i, g, more, before):
                    spread(i, g, more, before)
                    aggr(i, g, more, before)

                one_behind(dve, spread_and_aggr, gather)

            @block.scalar
            def _(act):
                with act.Fori(0, TURNS) as i:
                    for g in range(W1):
                        act.wait_ge(S["c_zp"], i * W1 + g + 1)
                        nc.scalar.activation(z12[:, g].rearrange("p b k t -> p (b k t)").rearrange(
                            "p (a n) -> p a n", a=2), ps[:, 4 * (g % 2) + 1:4 * (g % 2) + 3],
                                             ACT.Copy).then_inc(S["c_z12"], 1)

            @block.tensor
            def _(pe):
                def spread(i, g, more, before):
                    k = 4 * (g % 2)
                    pe.wait_ge(S["c_hr"], i * W1 + g + 1)
                    if before or g > 1:
                        pe.wait_ge(S["c_z0"], i * W1 + g - 1)
                        pe.wait_ge(S["c_z12"], i * W1 + g - 1)
                    for b in range(QB):
                        nc.tensor.transpose(ps[:, k, b * T:(b + 1) * T], hn[:, g * QB + b], ident[:])
                    for b in range(QB):
                        ins = nc.tensor.matmul(ps[:, k + 1 + b // 2, (b % 2) * 2 * T:(b % 2 + 1) * 2 * T],
                                               hr[:, g * QB + b], adj_ul[:].rearrange("p k t -> p (k t)"),
                                               start=True, stop=True)
                    ins.then_inc(S["c_zp"], 1)

                def gather(i, g, more, before):
                    k = 4 * (g % 2)
                    pe.wait_ge(S["c_z0"], i * W1 + g + 1)
                    pe.wait_ge(S["c_z12"], i * W1 + g + 1)
                    if before or g > 1:
                        pe.wait_ge(S["c_o"], i * W1 + g - 1)
                    for b in range(QB):
                        dst = ps[:, k + 3, b * C:(b + 1) * C]
                        nc.tensor.matmul(dst, z0[:, g, b], w2_sb[:, 0], start=True, stop=False)
                        nc.tensor.matmul(dst, z12[:, g, b, 0], w2_sb[:, 1], start=False, stop=False)
                        ins = nc.tensor.matmul(dst, z12[:, g, b, 1], w2_sb[:, 2], start=False, stop=True)
                    ins.then_inc(S["c_op"], 1)

                one_behind(pe, spread, gather)

        part.close()

        part, tmp = scope()
        NG = B // QB
        GH = QB * HEADS
        BH = B * HEADS // P
        xv = tmp("xv", [P, B, C])
        hT3 = tmp("hT3", [P, QB, T])
        xq_hi = tmp("xq_hi", [P, QB, C], F32R)
        xq_lo = tmp("xq_lo", [P, QB, C], F32R)
        rl = tmp("rl", [P, 2, 512])
        lr = tmp("lr", [P, QB, E])
        lg = tmp("lg", [P, EC, B * HEADS])
        S = sync_names(nc, ctx, "d_stats d_aggr d_var d_rstd d_hn d_hTp d_hT d_xp d_xqh d_xql d_xv d_zp d_rl d_lr "
                                "d_lgp d_lg")

        with nc.Block() as block:
            def steps_of(engine, step):
                step(0, False, True, True)
                step(1, True, True, True)
                with engine.Fori(2, NG - 2) as n:
                    step(n, True, True, True)
                for n in range(NG - 2, NG):
                    step(n, True, n + 1 < NG, n + 2 < NG)

            @block.gpsimd
            def _(pool):
                with pool.Fori(0, NG) as n:
                    wait_apart(pool, S["d_aggr"], n * QB + QB)
                    nc.gpsimd.tensor_scalar(rstd[:, 0:QB], mv[:, 0:QB, 1], EPS, None, ALU.add).then_inc(S["d_var"], 1)
                    pool.wait_ge(S["d_var"], n + 1)
                    nc.gpsimd.tensor_tensor(rstd[:, 0:QB], rstd[:, 0:QB], half[:, 0:QB], ALU.pow).then_inc(
                        S["d_rstd"], 1)

            @block.vector
            def _(dve):
                def norm_sums(n):
                    norm_stats(n * QB, 0, QB, S["d_stats"])
                    wait_apart(dve, S["d_stats"], n * QB + QB)
                    norm_aggr(0, QB, S["d_aggr"])

                def step(n, before, has1, has2):
                    dve.wait_ge(S["d_xqh"], n + 1)
                    nc.vector.tensor_tensor(xq_lo[:], by4(ps[:, 1]), xq_hi[:].bitcast(F32), ALU.subtract).then_inc(
                        S["d_xql"], 1)
                    if has2:
                        norm_sums(n + 2)
                    for k in range(2):
                        dve.wait_ge(S["d_rl"], n * 2 + k + 1)
                        nc.vector.scalar_tensor_tensor(
                            lr[:, 2 * k:2 * k + 2].rearrange("p b e -> p (b e)"), ps[:, 3 + k], SLOPE, rl[:, k],
                            ALU.mult, ALU.add).then_inc(S["d_lr"], 1)
                    if before:
                        add_log(n - 1)
                    if has2:
                        dve.wait_ge(S["d_hTp"], n + 2)
                        dve.wait_ge(S["d_rstd"], n + 3)
                        norm_apply((n + 2) * QB, 0, QB, S["d_hn"])

                def add_log(n):
                    dve.wait_ge(S["d_lgp"], n + 1)
                    nc.vector.tensor_tensor(lg[:, :, bass.ds(n * GH, GH)],
                                            ps[:, 5, 0:EC * GH].rearrange("p (c m) -> p c m", c=EC),
                                            log_a[:].unsqueeze(2).to_broadcast([P, EC, GH]), ALU.add).then_inc(
                                                S["d_lg"], 1)

                norm_sums(0)
                dve.wait_ge(S["d_rstd"], 1)
                norm_apply(0, 0, QB, S["d_hn"])
                norm_sums(1)
                dve.wait_ge(S["d_hTp"], 1)
                dve.wait_ge(S["d_rstd"], 2)
                norm_apply(QB, 0, QB, S["d_hn"])
                steps_of(dve, step)
                add_log(NG - 1)

            @block.scalar
            def _(act):
                def relu_hT(n):
                    act.wait_ge(S["d_hTp"], n + 1)
                    nc.scalar.activation(hT3[:], by4(ps[:, 0]), ACT.Relu).then_inc(S["d_hT"], 1)

                def step(n, before, has1, has2):
                    act.wait_ge(S["d_xp"], n + 1)
                    nc.scalar.activation(xq_hi[:], by4(ps[:, 1]), ACT.Copy).then_inc(S["d_xqh"], 1)
                    nc.scalar.activation(xv[:, bass.ds(n * QB, QB), :], by4(ps[:, 2]), ACT.Copy).then_inc(
                        S["d_xv"], 1)
                    if has1:
                        relu_hT(n + 1)
                    for k in range(2):
                        act.wait_ge(S["d_zp"], n * 2 + k + 1)
                        if k == 0 and before:
                            act.wait_ge(S["d_lr"], n * 2)
                        nc.scalar.activation(rl[:, k], ps[:, 3 + k], ACT.Relu, scale=1.0 - SLOPE).then_inc(
                            S["d_rl"], 1)

                relu_hT(0)
                steps_of(act, step)

            @block.tensor
            def _(pe):
                def transpose(n):
                    pe.wait_ge(S["d_hn"], n * QB + QB)
                    for b in range(QB):
                        ins = nc.tensor.transpose(ps[:, 0, b * T:(b + 1) * T], hn[:, b], ident[:])
                    ins.then_inc(S["d_hTp"], 1)

                def logits(n, before=True):
                    if before:
                        pe.wait_ge(S["d_lg"], n)
                    pe.wait_ge(S["d_lr"], n * 2 + 2)
                    for b in range(QB):
                        for c in range(EC):
                            col = c * GH + b * HEADS
                            ins = nc.tensor.matmul(ps[:, 5, col:col + HEADS], lr[:, b, c * P:(c + 1) * P], a_blk[:],
                                                   start=True, stop=True)
                    ins.then_inc(S["d_lgp"], 1)

                def step(n, before, has1, has2):
                    pe.wait_ge(S["d_hT"], n + 1)
                    if before:
                        pe.wait_ge(S["d_xv"], n)
                    for k in range(2):
                        for b in range(QB):
                            ins = nc.tensor.matmul(ps[:, 1 + k, b * C:(b + 1) * C], hT3[:, b], w_lv[:, k],
                                                   start=True, stop=True)
                    ins.then_inc(S["d_xp"], 1)
                    if before:
                        logits(n - 1, not (isinstance(n, int) and n == 1))
                    if has1:
                        transpose(n + 1)
                    pe.wait_ge(S["d_xqh"], n + 1)
                    pe.wait_ge(S["d_xql"], n + 1)
                    for k in range(2):
                        for b in range(2):
                            dst = ps[:, 3 + k, b * E:(b + 1) * E]
                            nc.tensor.matmul(dst, xq_hi[:, 2 * k + b], hot_sd[:], start=True, stop=False)
                            ins = nc.tensor.matmul(dst, xq_lo[:, 2 * k + b], hot_sd[:], start=False, stop=True)
                        ins.then_inc(S["d_zp"], 1)

                transpose(0)
                steps_of(pe, step)
                logits(NG - 1)

        fwd = tmp("fwd", [P, BH, E])
        bwd = tmp("bwd", [P, BH, E])
        expT = tmp("expT", [P, BH, E])
        ex = tmp("ex", [P, EC, B * HEADS])
        att = tmp("att", [P, EC, B * HEADS])
        xv_hi = tmp("xv_hi", [P, QB * C], F32R)
        xv_lo = tmp("xv_lo", [P, QB * C], F32R)
        va = tmp("va", [P, EC, QB, C])
        y3 = tmp("y3", [P, QB, T])
        S = sync_names(nc, ctx, "e_lgTp e_fb e_m e_sub e_exp e_exTp e_ex e_denp e_inv e_att e_xvh e_xvl e_vp e_va "
                                "e_yp e_y e_op e_o e_st")
        with nc.Block() as block:
            @block.sync
            def _(sp):
                with sp.Fori(0, NG) as n:
                    sp.wait_ge(S["e_o"], n + 1)
                    sp.dma_start(out[bass.ds(n * QB, QB)].rearrange("b t c -> t b c"),
                                 x[:, bass.ds(n * QB, QB), :]).then_inc(S["e_st"], 16)
                sp.wait_ge(S["e_st"], 16 * NG)

            @block.gpsimd
            def _(pool):
                def low_values(n):
                    pool.wait_ge(S["e_xvh"], n + 1)
                    nc.gpsimd.tensor_tensor(xv_lo[:], xv[:, bass.ds(n * QB, QB), :].rearrange("p b c -> p (b c)"),
                                            xv_hi[:].bitcast(F32), ALU.subtract).then_inc(S["e_xvl"], 1)

                with pool.Fori(0, NG) as n:
                    low_values(n)

            @block.vector
            def _(dve):
                for s in range(BH):
                    src = ps[:, s, 0:E]
                    dve.wait_ge(S["e_lgTp"], s + 1)
                    nc.vector.tensor_tensor_scan(fwd[:, s], cut_f[:], src, 0.0, ALU.add, ALU.max).then_inc(
                        S["e_fb"], 1)
                    nc.vector.tensor_tensor_scan(bwd[:, s, ::-1], cut_b[:, ::-1], src[:, ::-1], 0.0, ALU.add,
                                                 ALU.max).then_inc(S["e_fb"], 1)
                    dve.wait_ge(S["e_fb"], 2 * s + 2)
                    nc.vector.tensor_tensor(fwd[:, s], fwd[:, s], bwd[:, s], ALU.max).then_inc(S["e_m"], 1)
                    dve.wait_ge(S["e_m"], s + 1)
                    nc.vector.tensor_tensor(bwd[:, s], src, fwd[:, s], ALU.subtract).then_inc(S["e_sub"], 1)
                for c in range(EC):
                    dve.wait_ge(S["e_exTp"], BH)
                    nc.vector.tensor_copy(ex[:, c], ps[:, 4 + c]).then_inc(S["e_ex"], 1)
                for c in range(EC):
                    dve.wait_ge(S["e_denp"], c + 1)
                    nc.vector.reciprocal(att[:, c], ps[:, 6 + c]).then_inc(S["e_inv"], 1)
                for c in range(EC):
                    dve.wait_ge(S["e_inv"], c + 1)
                    nc.vector.tensor_tensor(att[:, c], att[:, c], ex[:, c], ALU.mult).then_inc(S["e_att"], 1)
                dve.wait_ge(S["e_att"], EC)

                def weigh(n):
                    for c in range(EC):
                        dve.wait_ge(S["e_vp"], n * EC + c + 1)
                        nc.vector.tensor_tensor(
                            va[:, c].rearrange("p b (h d) -> p (b h) d", h=HEADS),
                            ps[:, c].rearrange("p (n d) -> p n d", d=DH),
                            att[:, c, bass.ds(n * GH, GH)].unsqueeze(2).to_broadcast([P, GH, DH]),
                            ALU.mult).then_inc(S["e_va"], 1)

                def finish(n):
                    xs = x[:, bass.ds(n * QB, QB), :]
                    dve.wait_ge(S["e_op"], n + 1)
                    nc.vector.tensor_tensor(xs, xs, by4(ps[:, 7]), ALU.add).then_inc(S["e_o"], 1)

                weigh(0)
                with dve.Fori(0, NG - 1) as n:
                    weigh(n + 1)
                    finish(n)
                finish(NG - 1)

            @block.scalar
            def _(act):
                def high_values(n, before):
                    if before:
                        act.wait_ge(S["e_vp"], n * EC)
                        act.wait_ge(S["e_xvl"], n)
                    nc.scalar.activation(xv_hi[:], xv[:, bass.ds(n * QB, QB), :].rearrange("p b c -> p (b c)"),
                                         ACT.Copy).then_inc(S["e_xvh"], 1)

                def copy_y(n):
                    act.wait_ge(S["e_yp"], n + 1)
                    nc.scalar.activation(y3[:], by4(ps[:, 6]), ACT.Copy).then_inc(S["e_y"], 1)

                high_values(0, False)
                for s in range(BH):
                    act.wait_ge(S["e_sub"], s + 1)
                    nc.scalar.activation(expT[:, s], bwd[:, s], ACT.Exp).then_inc(S["e_exp"], 1)
                high_values(1, True)
                with act.Fori(0, NG - 2) as n:
                    copy_y(n)
                    high_values(n + 2, True)
                copy_y(NG - 2)
                copy_y(NG - 1)

            @block.tensor
            def _(pe):
                for s in range(BH):
                    for c in range(EC):
                        ins = nc.tensor.transpose(ps[:, s, c * P:(c + 1) * P],
                                                  lg[:, c, s * P:(s + 1) * P], ident[:])
                    ins.then_inc(S["e_lgTp"], 1)
                for s in range(BH):
                    pe.wait_ge(S["e_exp"], s + 1)
                    for c in range(EC):
                        ins = nc.tensor.transpose(ps[:, 4 + c, s * P:(s + 1) * P], expT[:, s, c * P:(c + 1) * P],
                                                  ident[:])
                    ins.then_inc(S["e_exTp"], 1)
                pe.wait_ge(S["e_ex"], EC)
                for c in range(EC):
                    for k in range(EC):
                        ins = nc.tensor.matmul(ps[:, 6 + c], same[:, k, c * P:(c + 1) * P], ex[:, k],
                                               start=(k == 0), stop=(k == EC - 1))
                    ins.then_inc(S["e_denp"], 1)

                def values(n):
                    pe.wait_ge(S["e_xvh"], n + 1)
                    pe.wait_ge(S["e_xvl"], n + 1)
                    for c in range(EC):
                        nc.tensor.matmul(ps[:, c], hot_d[:, c * P:(c + 1) * P], xv_hi[:], start=True, stop=False)
                        nc.tensor.matmul(ps[:, c], hot_d[:, c * P:(c + 1) * P], xv_lo[:], start=False,
                                         stop=True).then_inc(S["e_vp"], 1)

                def aggregate(n):
                    pe.wait_ge(S["e_va"], n * EC + EC)
                    for b in range(QB):
                        for c in range(EC):
                            ins = nc.tensor.matmul(ps[:, 6, b * T:(b + 1) * T], va[:, c, b], hot_sT[:, c],
                                                   start=(c == 0), stop=(c == EC - 1))
                    ins.then_inc(S["e_yp"], 1)

                def project(n, before):
                    pe.wait_ge(S["e_y"], n + 1)
                    if before:
                        pe.wait_ge(S["e_o"], n)
                    for b in range(QB):
                        ins = nc.tensor.matmul(ps[:, 7, b * C:(b + 1) * C], y3[:, b], w_out[:], start=True, stop=True)
                    ins.then_inc(S["e_op"], 1)

                values(0)
                pe.wait_ge(S["e_att"], EC)
                aggregate(0)
                values(1)
                project(0, False)
                with pe.Fori(1, NG - 1) as n:
                    aggregate(n)
                    values(n + 1)
                    project(n, True)
                aggregate(NG - 1)
                project(NG - 1, True)


def kernel(x, adj, L0_gnn_Wg0, L0_gnn_bg0, L0_gnn_Wg1, L0_gnn_bg1, L0_gnn_Wih, L0_gnn_Whh, L0_gnn_bih, L0_gnn_bhh,
           L1_gnn_Wqkv, L1_gnn_Wo, L2_gnn_W, L2_gnn_bias, L3_gnn_W_lin, L3_gnn_W_val, L3_gnn_a, L3_gnn_W_out,
           L3_gnn_src, L3_gnn_dst):
    import numpy as np
    import concourse.bacc as bacc
    from concourse.bass_utils import run_bass_kernel_spmd

    def lay(a):
        return np.ascontiguousarray(a)

    skips, gates, hid = L0_gnn_Wih.shape
    a_rep = np.broadcast_to(np.asarray(L3_gnn_a).reshape(-1, 1), (L3_gnn_a.size, L3_gnn_a.shape[0]))
    laid = {
        "x_in": x, "adj": adj, "adjT": np.asarray(adj).T,
        "Wg0": L0_gnn_Wg0, "bg0": np.asarray(L0_gnn_bg0)[None, :],
        "Wg1": L0_gnn_Wg1, "bg1": np.asarray(L0_gnn_bg1)[None, :],
        "WihT": np.asarray(L0_gnn_Wih).reshape(skips * gates, hid).T,
        "WhhT": np.asarray(L0_gnn_Whh).reshape(skips * gates, hid).T,
        "bihT": np.asarray(L0_gnn_bih).reshape(-1, hid).T, "bhhT": np.asarray(L0_gnn_bhh).reshape(-1, hid).T,
        "WqkvT": np.asarray(L1_gnn_Wqkv).T, "Wo": L1_gnn_Wo,
        "W2": L2_gnn_W, "bias2": np.asarray(L2_gnn_bias)[None, :],
        "WlvT": np.concatenate([np.asarray(L3_gnn_W_lin).T, np.asarray(L3_gnn_W_val).T], axis=1),
        "a_col": a_rep, "WoutT": np.asarray(L3_gnn_W_out).T,
        "src_row": np.asarray(L3_gnn_src)[None, :], "src_col": np.asarray(L3_gnn_src).reshape(-1, 128).T,
        "dst_row": np.asarray(L3_gnn_dst)[None, :], "dst_col": np.asarray(L3_gnn_dst).reshape(-1, 128).T,
    }
    nc = bacc.Bacc("TRN2", target_bir_lowering=False, num_devices=1)
    arrays, args = {}, {}
    for name, a in laid.items():
        a = lay(a)
        arrays[f"in_{name}"] = a
        args[name] = nc.dram_tensor(f"in_{name}", a.shape, mybir.dt.from_np(a.dtype), kind="ExternalInput").ap()
    out = nc.dram_tensor("out", x.shape, F32, kind="ExternalOutput").ap()
    four_layers(nc, out=out, **args)
    return run_bass_kernel_spmd(nc, [arrays], core_ids=[0]).results[0]["out"]
```

```python
from contextlib import ExitStack

import concourse.bass as bass
from concourse import mybir

F32 = mybir.dt.float32
F32R = mybir.dt.float32r
I32 = mybir.dt.int32
ALU = mybir.AluOpType
ACT = mybir.ActivationFunctionType
AXX = mybir.AxisListType.X

P = 128
EPS = 1e-5
LOG_EPS = 1e-8
NEG = -1e30
CUT = -3e38
SLOPE = 0.2
I, F, G, O = range(4)


def sync_names(nc, ctx, names):
    return {n: ctx.enter_context(nc.semaphore(n)) for n in names.split()}


def four_layers(nc, x_in, adj, adjT, Wg0, bg0, Wg1, bg1, WihT, WhhT, bihT, bhhT, WqkvT, Wo, W2, bias2,
                WlvT, a_col, WoutT, src_row, src_col, dst_row, dst_col, out):
    B = x_in.shape[0]
    T = C = P
    SKIPS = WihT.shape[1] // (4 * P)
    HEADS = a_col.shape[1]
    DH = C // HEADS
    E = src_row.shape[1]
    EC = E // P
    NB = 16
    TURNS = B // NB

    with ExitStack() as ctx:
        def sb(name, shape, dt=F32):
            return ctx.enter_context(nc.sbuf_tensor(name, shape, dt))

        passed = ctx.enter_context(nc.semaphore("passed"))

        def wait_apart(eng, sem, value):
            eng.wait_ge(sem, value)
            eng.sem_inc(passed, 1)

        def scope():
            stack = ctx.enter_context(ExitStack())
            return stack, lambda name, shape, dt=F32: stack.enter_context(nc.sbuf_tensor(name, shape, dt))

        x = sb("x", [P, B, C])
        ps = ctx.enter_context(nc.psum_tensor("ps", [P, 8, 512], F32))

        ident = sb("ident", [P, P])
        ones = sb("ones", [P, P])
        w_g = sb("w_g", [P, 2, P])
        cut0 = sb("cut0", [P, P])
        add1 = sb("add1", [P, P])
        b_lstm = sb("b_lstm", [P, SKIPS * 4])
        adjT_sb = sb("adjT_sb", [P, P])
        m_qk = sb("m_qk", [P, P])
        w_vo = sb("w_vo", [P, P])
        adj_causal = sb("adj_causal", [P, P])
        adj_ul = sb("adj_ul", [P, 2, P])
        diag_bc = sb("diag_bc", [P, P])
        w2_sb = sb("w2_sb", [P, 3, P])
        bias2_bc = sb("bias2_bc", [P, P])
        lv_hi = sb("lv_hi", [P, 2 * P], F32R)
        lv_lo = sb("lv_lo", [P, 2 * P], F32R)
        w_out = sb("w_out", [P, P])
        a_blk = sb("a_blk", [P, HEADS])
        iota_p = sb("iota_p", [P, EC])
        hot_s = sb("hot_s", [P, E])
        hot_d = sb("hot_d", [P, E], F32R)
        hot_sd = sb("hot_sd", [P, E], F32R)
        hot_sT = sb("hot_sT", [P, EC, P])
        hot_dT = sb("hot_dT", [P, EC, P])
        same = sb("same", [P, EC, E])
        cut_f = sb("cut_f", [P, E])
        cut_b = sb("cut_b", [P, E])
        log_a = sb("log_a", [P, EC])
        half = sb("half", [P, NB])

        stats = sb("stats", [P, NB, 6])
        mv = sb("mv", [P, NB, 2])
        rstd = sb("rstd", [P, NB])
        shift = sb("shift", [P, NB])
        hn = sb("hn", [P, NB, C])


        def norm_stats(b0, k, n, done, slot=0):
            for j in range(k, k + n):
                nc.vector.bn_stats(stats[:, slot + j],
                                   x[:, bass.ds(b0 + j, 1), :].rearrange("p a c -> p (a c)")).then_inc(done, 1)

        def norm_aggr(k, n, done):
            for j in range(k, k + n):
                nc.vector.bn_aggr(mv[:, j], stats[:, j]).then_inc(done, 1)

        def norm_apply(b0, k, n, done, slot=0):
            for j in range(k, k + n):
                nc.vector.tensor_scalar(hn[:, slot + j], x[:, bass.ds(b0 + j, 1), :].rearrange("p a c -> p (a c)"),
                                        mv[:, slot + j, 0:1], rstd[:, slot + j:slot + j + 1], ALU.subtract,
                                        ALU.mult).then_inc(done, 1)

        GB = NB // 2
        names = ("a_stats a_aggr a_var a_rstd a_nmean a_shift a_hn a_axp a_ax a_w0p a_w0 a_up a_u a_Hp a_H a_gatep "
                 "a_gate a_Hlo a_part a_cell a_tanh a_hid a_h32 a_lo a_lo_end a_outp a_out").split()
        A = [sync_names(nc, ctx, " ".join(f"{n}{g}" for n in names)) for g in range(2)]

        def sa(g, name):
            return A[g][f"{name}{g}"]

        def turn_start(i):
            return 0 if isinstance(i, int) and i == TURNS else i * NB

        def make_rstd(pool, i, g):
            wait_apart(pool, sa(g, "a_aggr"), i * GB + GB)
            r = rstd[:, g * GB:(g + 1) * GB]
            nc.gpsimd.tensor_scalar(r, mv[:, g * GB:(g + 1) * GB, 1], EPS, None, ALU.add).then_inc(sa(g, "a_var"), 1)
            pool.wait_ge(sa(g, "a_var"), i + 1)
            nc.gpsimd.tensor_tensor(r, r, half[:, 0:GB], ALU.pow).then_inc(sa(g, "a_rstd"), 1)
            sh = shift[:, g * GB:(g + 1) * GB]
            nc.gpsimd.tensor_scalar(sh, mv[:, g * GB:(g + 1) * GB, 0], -1.0, None, ALU.mult).then_inc(
                sa(g, "a_nmean"), 1)
            pool.wait_ge(sa(g, "a_rstd"), i + 1)
            pool.wait_ge(sa(g, "a_nmean"), i + 1)
            nc.gpsimd.tensor_tensor(sh, sh, r, ALU.mult).then_inc(sa(g, "a_shift"), 1)

        def relu_norm(act, i, g, k, n):
            if k == 0:
                act.wait_ge(sa(g, "a_shift"), i + 1)
            for j in range(g * GB + k, g * GB + k + n):
                nc.scalar.activation(hn[:, j], x[:, bass.ds(turn_start(i) + j, 1), :].rearrange("p a c -> p (a c)"),
                                     ACT.Relu, bias=shift[:, j:j + 1], scale=rstd[:, j:j + 1]).then_inc(
                                         sa(g, "a_hn"), 1)

        part0, tmp0 = scope()
        w_hi = tmp0("w_hi", [P, 2, SKIPS, 4, P], F32R)
        w_lo = tmp0("w_lo", [P, 2, SKIPS, 4, P], F32R)
        part, tmp = scope()
        w_raw = tmp("w_raw", [P, 2, SKIPS * 4 * P])
        w_lv = tmp("w_lv", [P, 2 * P])
        b0_col = tmp("b0_col", [P, 1])
        b1_bc = tmp("b1_bc", [P, P])
        b0_part = tmp("b0_part", [P, P])
        b_ih = tmp("b_ih", [P, SKIPS * 4])
        b_hh = tmp("b_hh", [P, SKIPS * 4])
        adj_sb = tmp("adj_sb", [P, P])
        wqkvT = tmp("wqkvT", [P, 3, P])
        wo_sb = tmp("wo_sb", [P, P])
        adj_diag = tmp("adj_diag", [P, P])
        a_sb = tmp("a_sb", [P, HEADS])
        iota_e = tmp("iota_e", [P, E])
        ends_row = tmp("ends_row", [P, 2, E], I32)
        ends_rowf = tmp("ends_rowf", [P, 2, E])
        ends_col = tmp("ends_col", [P, 2, EC], I32)
        ends_colf = tmp("ends_colf", [P, EC, 2])
        key_row = tmp("key_row", [P, E])
        key_col = tmp("key_col", [P, EC])
        is_less = tmp("is_less", [P, E])
        rank = tmp("rank", [P, EC])
        perm = tmp("perm", [P, EC, E])
        rep = tmp("rep", [P, 2, EC, P])
        srt = tmp("srt", [P, 2, E])
        srt_col = tmp("srt_col", [P, EC, 2])
        picked = tmp("picked", [P, EC, P])
        S = sync_names(nc, ctx, "ld_e ld_x0 ld_lstm ld_w ld_x1 ld_x pool_made dve_made w_high w_low pool_link dve_link "
                                "act_link pe_srt pe_w pe_b0 pe_adj")
        with nc.Block() as block:

            @block.sync
            def _(sp):
                ends = ((ends_row[:, 0], src_row.to_broadcast([P, E])), (ends_row[:, 1], dst_row.to_broadcast([P, E])),
                        (ends_col[:, 0], src_col), (ends_col[:, 1], dst_col))
                for dst, s in ends:
                    sp.dma_start(dst, s).then_inc(S["ld_e"], 16)
                sp.dma_start(x[:, 0:NB, :], x_in[0:NB].rearrange("b t c -> t b c")).then_inc(S["ld_x0"], 16)
                for dst, s in ((w_raw[:, 0], WihT), (w_raw[:, 1], WhhT), (b_ih[:], bihT), (b_hh[:], bhhT)):
                    sp.dma_start(dst, s).then_inc(S["ld_lstm"], 16)
                for dst, s in ((adj_sb[:], adj), (adjT_sb[:], adjT), (w_g[:, 0], Wg0), (w_g[:, 1], Wg1),
                               (b0_col[:], bg0), (b1_bc[:], bg1.to_broadcast([P, P])), (a_sb[:], a_col),
                               (wqkvT[:], WqkvT.rearrange("(k d) c -> d k c", d=P)), (wo_sb[:], Wo),
                               (w2_sb[:], W2.rearrange("k f o -> f k o")),
                               (w_lv[:], WlvT), (w_out[:], WoutT),
                               (bias2_bc[:], bias2.to_broadcast([P, P]))):
                    sp.dma_start(dst, s).then_inc(S["ld_w"], 16)
                for i in range(1, TURNS):
                    sp.dma_start(x[:, i * NB:(i + 1) * NB, :],
                                 x_in[i * NB:(i + 1) * NB].rearrange("b t c -> t b c")).then_inc(
                                     S["ld_x1" if i == 1 else "ld_x"], 16)
            n_e, n_lstm, n_w = 4 * 16, 4 * 16, 13 * 16
            w_all, hi_all, lo_all = ([w[:, a].rearrange(how) for a in range(2)] for w, how in (
                (w_raw, "p n -> p n"), (w_hi, "p s g h -> p (s g h)"), (w_lo, "p s g h -> p (s g h)")))

            @block.gpsimd
            def _(pool):
                n = [0]

                def link(ins):
                    n[0] += 1
                    ins.then_inc(S["pool_link"], 1)
                    pool.wait_ge(S["pool_link"], n[0])

                link(nc.gpsimd.iota(iota_e[:], pattern=[[1, E]], base=0, channel_multiplier=0,
                                    allow_small_or_imprecise_dtypes=True))
                link(nc.gpsimd.iota(iota_p[:], pattern=[[P, EC]], base=0, channel_multiplier=1,
                                    allow_small_or_imprecise_dtypes=True))
                nc.gpsimd.memset(ones[:], 1.0).then_inc(S["pool_made"], 1)
                link(nc.gpsimd.memset(ident[:], 0.0))
                link(nc.gpsimd.memset(half[:], -0.5))
                link(nc.gpsimd.affine_select(out=ident[:], in_=ident[:], compare_op=ALU.not_equal, fill=1.0, base=0,
                                             pattern=[[-1, P]], channel_multiplier=1))
                for g in range(2):
                    make_rstd(pool, 0, g)
                pool.wait_ge(S["ld_w"], n_w)
                link(nc.gpsimd.affine_select(out=adj_diag[:], in_=adjT_sb[:], compare_op=ALU.is_equal, fill=0.0,
                                             base=0, pattern=[[1, P]], channel_multiplier=-1))
                nc.gpsimd.memset(log_a[:], 0.0).then_inc(S["pool_made"], 1)
                pool.wait_ge(S["w_high"], 2)
                nc.gpsimd.tensor_tensor(lo_all[1], w_all[1], hi_all[1].bitcast(F32), ALU.subtract).then_inc(
                    S["w_low"], 1)
                link(nc.gpsimd.affine_select(out=adj_causal[:], in_=adj_sb[:], compare_op=ALU.is_ge, fill=NEG,
                                             base=0, pattern=[[-1, P]], channel_multiplier=1))
                link(nc.gpsimd.affine_select(out=adj_ul[:, 0], in_=adjT_sb[:], compare_op=ALU.is_gt, fill=0.0,
                                             base=0, pattern=[[-1, P]], channel_multiplier=1))
                link(nc.gpsimd.affine_select(out=adj_ul[:, 1], in_=adjT_sb[:], compare_op=ALU.is_gt, fill=0.0,
                                             base=0, pattern=[[1, P]], channel_multiplier=-1))
                link(nc.gpsimd.affine_select(out=a_blk[:], in_=a_sb[:], compare_op=ALU.is_ge, fill=0.0,
                                             base=0, pattern=[[-DH, HEADS]], channel_multiplier=1))
                link(nc.gpsimd.affine_select(out=a_blk[:], in_=a_blk[:], compare_op=ALU.is_ge, fill=0.0,
                                             base=DH - 1, pattern=[[DH, HEADS]], channel_multiplier=-1))

            @block.vector
            def _(dve):
                n = [0]

                def link(ins):
                    n[0] += 1
                    ins.then_inc(S["dve_link"], 1)
                    dve.wait_ge(S["dve_link"], n[0])

                dve.wait_ge(S["ld_e"], n_e)
                dve.wait_ge(S["pool_made"], 1)
                link(nc.vector.tensor_copy(ends_rowf[:], ends_row[:]))
                link(nc.vector.tensor_copy(ends_colf[:].rearrange("p c k -> p k c"), ends_col[:]))
                link(nc.vector.scalar_tensor_tensor(key_row[:], ends_rowf[:, 0], float(E), iota_e[:],
                                                    ALU.mult, ALU.add))
                link(nc.vector.scalar_tensor_tensor(key_col[:], ends_colf[:, :, 0], float(E), iota_p[:],
                                                    ALU.mult, ALU.add))
                for c in range(EC):
                    link(nc.vector.tensor_scalar(is_less[:], key_row[:], key_col[:, c:c + 1], None, ALU.is_lt,
                                                 ALU.add, accum_out=rank[:, c:c + 1]))
                    link(nc.vector.tensor_scalar(perm[:, c], iota_e[:], rank[:, c:c + 1], None, ALU.is_equal))
                    for k in range(2):
                        link(nc.vector.tensor_scalar(rep[:, k, c], ones[:], ends_colf[:, c, k:k + 1], None, ALU.mult))
                nc.vector.memset(is_less[:, 0:1], 0.0).then_inc(S["dve_made"], 1)
                dve.wait_ge(S["ld_x0"], 16)
                for g in range(2):
                    norm_stats(g * GB, 0, GB, sa(g, "a_stats"), g * GB)
                for g in range(2):
                    wait_apart(dve, sa(g, "a_stats"), GB)
                    norm_aggr(g * GB, GB, sa(g, "a_aggr"))
                dve.wait_ge(S["pe_srt"], 1)
                link(nc.vector.tensor_copy(srt[:].rearrange("p k e -> p (k e)"), ps[:, 0, :]))
                link(nc.vector.tensor_copy(srt_col[:], ps[:, 1, 0:2 * EC].rearrange("p (c k) -> p c k", k=2)))
                link(nc.vector.tensor_scalar(hot_s[:], srt[:, 0], iota_p[:, 0:1], None, ALU.is_equal))
                link(nc.vector.tensor_scalar(hot_d[:], srt[:, 1], iota_p[:, 0:1], None, ALU.is_equal))
                link(nc.vector.tensor_tensor(hot_sd[:], hot_s[:], hot_d[:].bitcast(F32), ALU.add))
                nc.vector.memset(is_less[:, 0:1], 0.0).then_inc(S["dve_made"], 1)
                for c in range(EC):
                    link(nc.vector.tensor_scalar(hot_sT[:, c], iota_e[:, 0:P], srt_col[:, c, 0:1], None, ALU.is_equal))
                    link(nc.vector.tensor_scalar(hot_dT[:, c], iota_e[:, 0:P], srt_col[:, c, 1:2], None, ALU.is_equal))
                    link(nc.vector.tensor_scalar(same[:, c], srt[:, 0], srt_col[:, c, 0:1], None, ALU.is_equal))
                link(nc.vector.memset(cut_f[:, 0:1], CUT))
                link(nc.vector.memset(cut_b[:, E - 1:E], CUT))
                link(nc.vector.tensor_tensor(is_less[:, 1:E], srt[:, 0, 1:E], srt[:, 0, 0:E - 1], ALU.not_equal))
                link(nc.vector.tensor_scalar(cut_f[:, 1:E], is_less[:, 1:E], CUT, None, ALU.mult))
                link(nc.vector.tensor_copy(cut_b[:, 0:E - 1], cut_f[:, 1:E]))
                dve.wait_ge(S["ld_lstm"], n_lstm)
                link(nc.vector.tensor_tensor(b_lstm[:], b_ih[:], b_hh[:], ALU.add))
                dve.wait_ge(S["w_high"], 1)
                link(nc.vector.tensor_tensor(lo_all[0], w_all[0], hi_all[0].bitcast(F32), ALU.subtract))
                dve.wait_ge(S["w_high"], 3)
                link(nc.vector.tensor_tensor(lv_lo[:], w_lv[:], lv_hi[:].bitcast(F32), ALU.subtract))
                dve.wait_ge(S["pe_w"], 1)
                link(nc.vector.tensor_scalar(b0_part[:], ps[:, 5, 0:P], b0_col[:, 0:1], None, ALU.mult))
                nc.vector.memset(is_less[:, 0:1], 0.0).then_inc(S["dve_made"], 1)
                link(nc.vector.tensor_scalar(cut0[:], b0_part[:], -1.0, None, ALU.mult))
                link(nc.vector.tensor_copy(diag_bc[:], ps[:, 2, 0:P]))
                link(nc.vector.tensor_scalar(m_qk[:], ps[:, 3, 0:P], float(C) ** -0.5, None, ALU.mult))
                link(nc.vector.tensor_copy(w_vo[:], ps[:, 3, P:2 * P]))
                dve.wait_ge(S["pe_adj"], 1)
                link(nc.vector.tensor_tensor(picked[:], ps[:, 4, 0:EC * P].rearrange("p (c m) -> p c m", c=EC),
                                             hot_dT[:], ALU.mult))
                link(nc.vector.tensor_reduce(rank[:], picked[:], AXX, ALU.add))
                nc.vector.tensor_scalar(rank[:], rank[:], LOG_EPS, None, ALU.add).then_inc(S["dve_made"], 1)
                dve.wait_ge(S["pe_b0"], 1)
                link(nc.vector.tensor_tensor(add1[:], ps[:, 6, 0:P], b1_bc[:], ALU.add))

            @block.scalar
            def _(act):
                for g in range(2):
                    relu_norm(act, 0, g, 0, GB)
                act.wait_ge(S["ld_lstm"], n_lstm)
                for k in range(2):
                    nc.scalar.activation(hi_all[k], w_all[k], ACT.Copy).then_inc(S["w_high"], 1)
                act.wait_ge(S["ld_w"], n_w)
                nc.scalar.activation(lv_hi[:], w_lv[:], ACT.Copy).then_inc(S["w_high"], 1)
                act.wait_ge(S["dve_made"], 4)
                act.wait_ge(S["pool_made"], 2)
                nc.scalar.activation(log_a[:], rank[:], ACT.Ln).then_inc(S["act_link"], 1)

            @block.tensor
            def _(pe):
                pe.wait_ge(S["dve_made"], 1)
                for k in range(2):
                    for c in range(EC):
                        nc.tensor.matmul(ps[:, 0, k * E:(k + 1) * E], rep[:, k, c], perm[:, c],
                                         start=(c == 0), stop=(c == EC - 1))
                for r in range(EC):
                    for c in range(EC):
                        ins = nc.tensor.matmul(ps[:, 1, 2 * r:2 * r + 2], perm[:, c, r * P:(r + 1) * P],
                                               ends_colf[:, c], start=(c == 0), stop=(c == EC - 1))
                ins.then_inc(S["pe_srt"], 1)
                pe.wait_ge(S["ld_w"], n_w)
                pe.wait_ge(S["pool_made"], 2)
                nc.tensor.matmul(ps[:, 2, 0:P], ones[:], adj_diag[:], start=True, stop=True)
                nc.tensor.matmul(ps[:, 5, 0:P], ones[:], adjT_sb[:], start=True, stop=True)
                nc.tensor.matmul(ps[:, 3, 0:P], wqkvT[:, 0], wqkvT[:, 1], start=True, stop=True)
                nc.tensor.matmul(ps[:, 3, P:2 * P], wqkvT[:, 2], wo_sb[:], start=True, stop=True).then_inc(
                    S["pe_w"], 1)
                pe.wait_ge(S["dve_made"], 2)
                for c in range(EC):
                    ins = nc.tensor.matmul(ps[:, 4, c * P:(c + 1) * P], hot_s[:, c * P:(c + 1) * P], adj_sb[:],
                                           start=True, stop=True)
                ins.then_inc(S["pe_adj"], 1)
                pe.wait_ge(S["dve_made"], 3)
                nc.tensor.matmul(ps[:, 6, 0:P], b0_part[:], w_g[:, 1], start=True, stop=True).then_inc(S["pe_b0"], 1)

        part.close()

        CH = GB * T // 512
        CB = 512 // T
        hT = tmp0("hT", [P, 2, GB, T])
        u = tmp0("u", [P, 2, GB, C])
        H = tmp0("H", [P, 2, GB, T])
        H_hi = tmp0("H_hi", [P, 2, GB, T], F32R)
        H_lo = tmp0("H_lo", [P, 2, GB, T], F32R)
        hid_hi = tmp0("hid_hi", [P, 2, 512], F32R)
        hid_lo = tmp0("hid_lo", [P, 2, 512], F32R)
        gate = tmp0("gate", [P, 2, 4, 512])
        cell = tmp0("cell", [P, 2, 512])
        hid = tmp0("hid", [P, 2, 512])
        tanh_c = tmp0("tanh_c", [P, 2, 512])

        steps = []
        for p in range(1, SKIPS + 1):
            nb = min(GB, 512 // (T // p))
            for b0 in range(0, GB, nb):
                steps += [(p, j, j == p - 1, b0, nb, T // p) for j in range(p)]
        NS = len(steps)
        gates_of = [(I, G, O) if st[1] == 0 else (I, G, F, O) for st in steps]
        gates_before = [sum(len(z) for z in gates_of[:k]) for k in range(NS + 1)]
        parts_before = [sum(2 for st in steps[:k] if st[1] > 0) for k in range(NS + 1)]
        TG, TP = gates_before[NS], parts_before[NS]

        A0, OUT, W0, U1, A1, STEP = range(6)
        ITEMS = STEP + NS
        STATS_AT = {U1: (0, 3), A1: (3, 3), STEP: (6, 2)}
        AGGR_AT = STEP + 1
        APPLY_AT = {STEP + 3: (0, 1), STEP + 4: (1, 2), STEP + 5: (3, 2), STEP + 6: (5, 1), STEP + 8: (6, 1),
                    STEP + 9: (7, 1)}

        def interleave(engine, parts):
            def turn(i, first, last):
                for n in range(ITEMS):
                    for do, g, behind in parts:
                        if n >= behind:
                            do(i, g, n - behind, not last, not first)
                        elif not first:
                            do(i - 1, g, n - behind + ITEMS, True, True)

            turn(0, True, False)
            with engine.Fori(1, TURNS - 1) as i:
                turn(i, False, False)
            turn(TURNS - 1, False, True)
            for n in range(OUT + 1 + max(behind for _, _, behind in parts)):
                for do, g, behind in parts:
                    if n < behind:
                        do(TURNS - 1, g, n - behind + ITEMS, False, True)
                    elif n - behind == OUT:
                        do(TURNS, g, OUT, False, True)

        def gate_bank(g, k, m):
            return ps[:, 4 * g + (gates_before[k] + m) % 4]

        def at(buf, p, j, b0, nb, w):
            return buf[:, b0:b0 + nb, j:j + p * (w - 1) + 1:p]

        apart = [k > 0 and steps[k][0] == steps[k - 1][0] and steps[k][1] == 0 for k in range(NS)]
        inner = [not st[2] or apart[k + 1] for k, st in enumerate(steps[:-1])]

        def lo_sem(g, k):
            return sa(g, "a_lo" if inner[k] else "a_lo_end")

        def lo_count(i, k):
            kinds = [z == inner[k] for z in inner]
            return i * sum(kinds) + sum(kinds[:k + 1])

        def flat(buf, nb, w):
            return buf[:, 0:nb * w].rearrange("p (b w) -> p b w", b=nb)

        def hidden(k, g):
            p, j, last, b0, nb, w = steps[k]
            if last:
                return [at(h[:, g], p, j, b0, nb, w) for h in (H, H_hi, H_lo)]
            return [flat(h[:, g], nb, w) for h in (hid, hid_hi, hid_lo)]

        ld_x1, ld_x = (S["ld_x1"], 16), (S["ld_x"], 16 * (TURNS - 2))
        with nc.Block() as block:
            @block.gpsimd
            def _(pool):
                def item(i, g, n, more, _):
                    k = n - STEP
                    if 0 <= k < NS - 1 and inner[k]:
                        h32, h_hi, h_lo = hidden(k, g)
                        pool.wait_ge(sa(g, "a_h32"), i * (NS - 1) + k + 1)
                        nc.gpsimd.tensor_tensor(h_lo, h32, h_hi.bitcast(F32), ALU.subtract).then_inc(
                            sa(g, "a_lo"), 1)
                    if n == AGGR_AT:
                        make_rstd(pool, i + 1, g)

                interleave(pool, [(item, 0, 0), (item, 1, 1)])

            @block.vector
            def _(dve):
                def norm_piece(i, g, n):
                    if n in STATS_AT:
                        if (g, n) == (0, min(STATS_AT)):
                            dve.wait_ge(*(ld_x1 if isinstance(i, int) and i == 1 else ld_x))
                        norm_stats(turn_start(i) + g * GB, *STATS_AT[n], sa(g, "a_stats"), g * GB)
                    elif n == AGGR_AT:
                        wait_apart(dve, sa(g, "a_stats"), i * GB + GB)
                        norm_aggr(g * GB, GB, sa(g, "a_aggr"))

                def item(i, g, n, more, before):
                    if n == W0:
                        for c in range(CH):
                            dve.wait_ge(sa(g, "a_w0p"), i * CH + c + 1)
                            nc.vector.tensor_tensor(
                                hT[:, g, c * CB:(c + 1) * CB], ps[:, 4 * g + 2 + c].rearrange("p (b t) -> p b t", b=CB),
                                cut0[:].unsqueeze(1).to_broadcast([P, CB, T]), ALU.max).then_inc(sa(g, "a_w0"), 1)
                    elif n == U1:
                        for c in range(CH):
                            dve.wait_ge(sa(g, "a_up"), i * CH + c + 1)
                            nc.vector.tensor_tensor(
                                u[:, g, c * CB:(c + 1) * CB], ps[:, 4 * g + 2 + c].rearrange("p (b c) -> p b c", b=CB),
                                add1[:].unsqueeze(1).to_broadcast([P, CB, C]), ALU.add).then_inc(sa(g, "a_u"), 1)
                        norm_piece(i + 1, g, n)
                    elif n == A1:
                        for c in range(CH):
                            dve.wait_ge(sa(g, "a_H"), i * CH + c + 1)
                            nc.vector.scalar_tensor_tensor(
                                H_lo[:, g, c * CB:(c + 1) * CB].rearrange("p b t -> p (b t)"), ps[:, 4 * g + c], 0.0,
                                H_hi[:, g, c * CB:(c + 1) * CB].rearrange("p b t -> p (b t)").bitcast(F32),
                                ALU.max, ALU.subtract).then_inc(sa(g, "a_Hlo"), 1)
                        norm_piece(i + 1, g, n)
                    elif n == OUT and before:
                        for c in range(CH):
                            dve.wait_ge(sa(g, "a_outp"), i * CH - CH + c + 1)
                            xs = x[:, bass.ds(i * NB - NB + g * GB + c * CB, CB), :]
                            nc.vector.tensor_tensor(xs, xs, ps[:, 4 * g + 2 + c].rearrange("p (b c) -> p b c", b=CB),
                                                    ALU.add).then_inc(sa(g, "a_out"), 1)
                    elif n >= STEP:
                        k = n - STEP
                        p, j, last, b0, nb, w = steps[k]
                        n0 = i * TG + gates_before[k]
                        gi, gf, gg, go = (flat(gate[:, g, z], nb, w) for z in (I, F, G, O))
                        cc = flat(cell[:, g], nb, w)
                        dve.wait_ge(sa(g, "a_gate"), n0 + 2)
                        if j == 0:
                            nc.vector.tensor_tensor(cc, gi, gg, ALU.mult).then_inc(sa(g, "a_cell"), 1)
                        else:
                            nc.vector.tensor_tensor(gi, gi, gg, ALU.mult).then_inc(sa(g, "a_part"), 1)
                            dve.wait_ge(sa(g, "a_gate"), n0 + 3)
                            nc.vector.tensor_tensor(cc, cc, gf, ALU.mult).then_inc(sa(g, "a_part"), 1)
                            dve.wait_ge(sa(g, "a_part"), i * TP + parts_before[k] + 2)
                            nc.vector.tensor_tensor(cc, cc, gi, ALU.add).then_inc(sa(g, "a_cell"), 1)
                        norm_piece(i + 1, g, n)
                        h32, h_hi, _lo = hidden(k, g)
                        tc = flat(tanh_c[:, g], nb, w)
                        dve.wait_ge(sa(g, "a_tanh"), i * NS + k + 1)
                        if k < NS - 1:
                            nc.vector.tensor_tensor(h_hi, go, tc, ALU.mult).then_inc(sa(g, "a_hid"), 1)
                            nc.vector.tensor_tensor(h32, go, tc, ALU.mult).then_inc(sa(g, "a_h32"), 1)
                            if not inner[k]:
                                dve.wait_ge(sa(g, "a_h32"), i * (NS - 1) + k + 1)
                                nc.vector.tensor_tensor(_lo, h32, h_hi.bitcast(F32), ALU.subtract).then_inc(
                                    sa(g, "a_lo_end"), 1)
                        else:
                            nc.vector.tensor_tensor(h32, go, tc, ALU.mult).then_inc(sa(g, "a_hid"), 1)

                interleave(dve, [(item, 0, 0), (item, 1, 1)])

            @block.scalar
            def _(act):
                def item(i, g, n, more, _):
                    if n == A0:
                        for c in range(CH):
                            act.wait_ge(sa(g, "a_axp"), i * CH + c + 1)
                            nc.scalar.activation(u[:, g, c * CB:(c + 1) * CB],
                                                 ps[:, 4 * g + c].rearrange("p (b t) -> p b t", b=CB),
                                                 ACT.Copy).then_inc(sa(g, "a_ax"), 1)
                    elif n == A1:
                        for c in range(CH):
                            act.wait_ge(sa(g, "a_Hp"), i * CH + c + 1)
                            nc.scalar.activation(H_hi[:, g, c * CB:(c + 1) * CB],
                                                 ps[:, 4 * g + c].rearrange("p (b t) -> p b t", b=CB),
                                                 ACT.Relu).then_inc(sa(g, "a_H"), 1)

                def gates(i, g, n, *_):
                    k = n - STEP
                    if k >= 0:
                        p, j, last, b0, nb, w = steps[k]
                        for m, z in enumerate(gates_of[k]):
                            act.wait_ge(sa(g, "a_gatep"), i * TG + gates_before[k] + m + 1)
                            if apart[k] and z == O:
                                act.wait_ge(sa(g, "a_h32"), i * (NS - 1) + k)
                            nc.scalar.activation(gate[:, g, z, 0:nb * w], gate_bank(g, k, m)[:, 0:nb * w],
                                                 ACT.Tanh if z == G else ACT.Sigmoid,
                                                 bias=b_lstm[:, 4 * (p - 1) + z:4 * (p - 1) + z + 1]).then_inc(
                                                     sa(g, "a_gate"), 1)

                def cell_tanh(i, g, n, more, _):
                    k = n - STEP
                    if k >= 0:
                        nb, w = steps[k][4:]
                        act.wait_ge(sa(g, "a_cell"), i * NS + k + 1)
                        nc.scalar.activation(tanh_c[:, g, 0:nb * w], cell[:, g, 0:nb * w],
                                             ACT.Tanh).then_inc(sa(g, "a_tanh"), 1)
                        if n in APPLY_AT:
                            relu_norm(act, i + 1, g, *APPLY_AT[n])

                interleave(act, [(item, 0, 0), (gates, 0, 0), (cell_tanh, 0, 0),
                                 (item, 1, 1), (gates, 1, 1), (cell_tanh, 1, 1)])

            @block.tensor
            def _(pe):
                def term(g, k, m, z, src, v_hi, v_lo, start, stop, half):
                    p, _, _, _, nb, w = steps[k]
                    dst = gate_bank(g, k, m)[:, 0:nb * w]
                    if half == 0:
                        nc.tensor.matmul(dst, w_hi[:, src, p - 1, z], v_hi, start=start, stop=False)
                        return nc.tensor.matmul(dst, w_lo[:, src, p - 1, z], v_hi, start=False, stop=False)
                    return nc.tensor.matmul(dst, w_hi[:, src, p - 1, z], v_lo, start=False, stop=stop)

                def input_share(i, g, n, *_):
                    k = n - STEP
                    if k >= 0 and steps[k][1] > 0:
                        p, j, _, b0, nb, w = steps[k]
                        for m, z in enumerate(gates_of[k]):
                            pe.wait_ge(sa(g, "a_gate"), i * TG + gates_before[k] + m - 3)
                            for part in (0, 1):
                                term(g, k, m, z, 0, at(H_hi[:, g], p, j, b0, nb, w), at(H_lo[:, g], p, j, b0, nb, w),
                                     True, False, part)

                def step(i, g, k):
                    p, j, last, b0, nb, w = steps[k]
                    gates = list(enumerate(gates_of[k]))
                    if k == 0:
                        pe.wait_ge(sa(g, "a_Hlo"), i * CH + CH)
                    if j == 0:
                        v = (at(H_hi[:, g], p, j, b0, nb, w), at(H_lo[:, g], p, j, b0, nb, w))
                        src = 0
                    else:
                        v = (hid_hi[:, g, 0:nb * w], hid_lo[:, g, 0:nb * w])
                        src = 1
                    if k > 0 and not apart[k]:
                        pe.wait_ge(sa(g, "a_hid"), i * NS + k)
                    for m, z in gates[:2]:
                        if apart[k] and gates_before[k] + m >= 4:
                            pe.wait_ge(sa(g, "a_gate"), i * TG + gates_before[k] + m - 3)
                        term(g, k, m, z, src, *v, j == 0, True, 0)
                    if k > 0 and not apart[k]:
                        pe.wait_ge(lo_sem(g, k - 1), lo_count(i, k - 1))
                        if apart[k - 1]:
                            pe.wait_ge(lo_sem(g, k - 2), lo_count(i, k - 2))
                    for m, z in gates[:2]:
                        term(g, k, m, z, src, *v, j == 0, True, 1).then_inc(sa(g, "a_gatep"), 1)
                    for m, z in gates[2:]:
                        if apart[k]:
                            pe.wait_ge(sa(g, "a_gate"), i * TG + gates_before[k] + m - 3)
                        term(g, k, m, z, src, *v, j == 0, True, 0)
                        term(g, k, m, z, src, *v, j == 0, True, 1).then_inc(sa(g, "a_gatep"), 1)

                def item(i, g, n, more, before):
                    if n == A0:
                        if before:
                            pe.wait_ge(sa(g, "a_gate"), i * TG)
                        for c in range(CH):
                            pe.wait_ge(sa(g, "a_hn"), i * GB + (c + 1) * CB)
                            for b in range(CB):
                                ins = nc.tensor.matmul(ps[:, 4 * g + c, b * T:(b + 1) * T],
                                                       hn[:, g * GB + c * CB + b], adjT_sb[:], start=True, stop=True)
                            ins.then_inc(sa(g, "a_axp"), 1)
                    elif n == OUT:
                        if before:
                            pe.wait_ge(sa(g, "a_hid"), i * NS)
                            for c in range(CH):
                                for b in range(CB):
                                    ins = nc.tensor.transpose(ps[:, 4 * g + 2 + c, b * T:(b + 1) * T],
                                                              H[:, g, c * CB + b], ident[:])
                                ins.then_inc(sa(g, "a_outp"), 1)
                    elif n == W0:
                        for c in range(CH):
                            pe.wait_ge(sa(g, "a_ax"), i * CH + c + 1)
                            if before:
                                pe.wait_ge(sa(g, "a_out"), i * CH - CH + c + 1)
                            nc.tensor.matmul(ps[:, 4 * g + 2 + c], w_g[:, 0],
                                             u[:, g, c * CB:(c + 1) * CB].rearrange("p b t -> p (b t)"),
                                             start=True, stop=True).then_inc(sa(g, "a_w0p"), 1)
                    elif n == U1:
                        for c in range(CH):
                            pe.wait_ge(sa(g, "a_w0"), i * CH + c + 1)
                            for b in range(CB):
                                ins = nc.tensor.matmul(ps[:, 4 * g + 2 + c, b * C:(b + 1) * C],
                                                       hT[:, g, c * CB + b], w_g[:, 1], start=True, stop=True)
                            ins.then_inc(sa(g, "a_up"), 1)
                    elif n == A1:
                        for c in range(CH):
                            pe.wait_ge(sa(g, "a_u"), i * CH + c + 1)
                            for b in range(CB):
                                ins = nc.tensor.matmul(ps[:, 4 * g + c, b * T:(b + 1) * T], u[:, g, c * CB + b],
                                                       adjT_sb[:], start=True, stop=True)
                            ins.then_inc(sa(g, "a_Hp"), 1)
                    else:
                        step(i, g, n - STEP)

                interleave(pe, [(input_share, 0, 0), (input_share, 1, 1), (item, 0, 0), (item, 1, 1)])

        part0.close()

        part, tmp = scope()
        W1 = 4
        QB = NB // W1
        hT1 = tmp("hT1", [P, W1, QB, T])
        hmT = tmp("hmT", [P, W1, QB, T])
        val = tmp("val", [P, W1, QB, C])
        prob = tmp("prob", [P, W1, QB, T])
        probT = tmp("probT", [P, W1, QB, T])
        nmax = tmp("nmax", [P, NB])
        rsum = tmp("rsum", [P, NB])
        rinv = tmp("rinv", [P, NB])
        S = sync_names(nc, ctx, "b_stats b_aggr b_var b_rstd b_hn b_hTp b_hT b_qp b_q b_vp b_v b_sp b_s b_max b_e "
                                "b_pTp b_pT b_op b_inv b_o")
        HT, PT, QK, VAL, SCORE, OUT1, EXP, STATS, APPLY = range(9)
        BESIDE = [(HT, 0), (PT, 2), (QK, 0), (VAL, 0), (EXP, 1), (SCORE, 0), (STATS, 0), (OUT1, 2), (APPLY, 1)]

        def pipeline(engine, stage):
            def turn(i, first, last):
                for step in range(W1):
                    for what, behind in BESIDE:
                        g = step - behind
                        if g >= 0:
                            stage(i, what, g, not last, not first)
                        elif not first:
                            stage(i - 1, what, g + W1, True, True)

            turn(0, True, False)
            with engine.Fori(1, TURNS - 1) as i:
                turn(i, False, False)
            turn(TURNS - 1, False, True)
            for step in range(max(behind for _, behind in BESIDE)):
                for what, behind in BESIDE:
                    if behind > step:
                        stage(TURNS - 1, what, step - behind + W1, False, True)

        BANK = {HT: (0, 0), QK: (1, 1), VAL: (2, 2), PT: (3, 3), SCORE: (4, 5), OUT1: (6, 7)}

        def bank(what, g):
            return ps[:, BANK[what][g % 2]]

        def by4(ap, n=QB):
            return ap.rearrange("p (b t) -> p b t", b=n)

        def group_rstd(pool, s, count, g):
            r = rstd[:, g * QB:(g + 1) * QB]
            wait_apart(pool, s["aggr"], count * QB + QB)
            nc.gpsimd.tensor_scalar(r, mv[:, g * QB:(g + 1) * QB, 1], EPS, None, ALU.add).then_inc(s["var"], 1)
            pool.wait_ge(s["var"], count + 1)
            nc.gpsimd.tensor_tensor(r, r, half[:, 0:QB], ALU.pow).then_inc(s["rstd"], 1)

        NORM = {n: S["b_" + n] for n in ("stats", "aggr", "var", "rstd")}
        with nc.Block() as block:
            @block.gpsimd
            def _(pool):
                def stage(i, what, g, more, before):
                    if what == STATS:
                        group_rstd(pool, NORM, i * W1 + g, g)

                pipeline(pool, stage)

            @block.vector
            def _(dve):
                def stage(i, what, g, more, before):
                    count = i * W1 + g + 1
                    if what == SCORE:
                        dve.wait_ge(S["b_sp"], count)
                        nc.vector.tensor_tensor(prob[:, g], by4(bank(SCORE, g)),
                                                adj_causal[:].unsqueeze(1).to_broadcast([P, QB, T]),
                                                ALU.add).then_inc(S["b_s"], 1)
                        dve.wait_ge(S["b_s"], count)
                        nc.vector.tensor_reduce(nmax[:, g * QB:(g + 1) * QB], prob[:, g], AXX, ALU.max,
                                                negate=True).then_inc(S["b_max"], 1)
                    elif what == STATS:
                        norm_stats(turn_start(i + 1), g * QB, QB, S["b_stats"])
                        wait_apart(dve, S["b_stats"], i * NB + (g + 1) * QB)
                        norm_aggr(g * QB, QB, S["b_aggr"])
                    elif what == OUT1:
                        dve.wait_ge(S["b_e"], count)
                        nc.vector.reciprocal(rinv[:, g * QB:(g + 1) * QB], rsum[:, g * QB:(g + 1) * QB]).then_inc(
                            S["b_inv"], 1)
                        dve.wait_ge(S["b_op"], count)
                        dve.wait_ge(S["b_inv"], count)
                        for b in range(QB):
                            xs = x[:, bass.ds(i * NB + g * QB + b, 1), :].rearrange("p a c -> p (a c)")
                            ins = nc.vector.scalar_tensor_tensor(xs, bank(OUT1, g)[:, b * C:(b + 1) * C],
                                                                 rinv[:, g * QB + b:g * QB + b + 1], xs,
                                                                 ALU.mult, ALU.add)
                        ins.then_inc(S["b_o"], 1)
                    elif what == APPLY:
                        dve.wait_ge(S["b_hTp"], count)
                        dve.wait_ge(S["b_rstd"], count)
                        norm_apply(turn_start(i + 1), g * QB, QB, S["b_hn"])

                pipeline(dve, stage)

            @block.scalar
            def _(act):
                def copy(sem, count, dst, src, done, func=ACT.Copy):
                    act.wait_ge(sem, count)
                    nc.scalar.activation(dst, by4(src), func).then_inc(done, 1)

                def stage(i, what, g, more, before):
                    count = i * W1 + g + 1
                    if what == HT:
                        copy(S["b_hTp"], count, hT1[:, g], bank(HT, g), S["b_hT"], ACT.Relu)
                    elif what == QK:
                        copy(S["b_qp"], count, hmT[:, g], bank(QK, g), S["b_q"])
                    elif what == VAL:
                        copy(S["b_vp"], count, val[:, g], bank(VAL, g), S["b_v"])
                    elif what == EXP:
                        act.wait_ge(S["b_max"], count)
                        for b in range(QB):
                            n = g * QB + b
                            ins = nc.scalar.activation(prob[:, g, b], prob[:, g, b], ACT.Exp, bias=nmax[:, n:n + 1],
                                                       accum_out=rsum[:, n:n + 1])
                        ins.then_inc(S["b_e"], 1)
                    elif what == PT:
                        copy(S["b_pTp"], count, probT[:, g], bank(PT, g), S["b_pT"])

                pipeline(act, stage)

            @block.tensor
            def _(pe):
                def four(dst, product, done):
                    for b in range(QB):
                        ins = product(dst[:, b * T:(b + 1) * T], b)
                    ins.then_inc(done, 1)

                def stage(i, what, g, more, before):
                    count = i * W1 + g + 1
                    if what == HT:
                        if before:
                            pe.wait_ge(S["b_hn"], (count - W1) * QB)
                        four(bank(HT, g), lambda dst, b: nc.tensor.transpose(dst, hn[:, g * QB + b], ident[:]),
                             S["b_hTp"])
                    elif what == QK:
                        pe.wait_ge(S["b_hT"], count)
                        nc.tensor.matmul(bank(QK, g), m_qk[:], hT1[:, g].rearrange("p b t -> p (b t)"),
                                         start=True, stop=True).then_inc(S["b_qp"], 1)
                    elif what == VAL:
                        if before or g > 0:
                            pe.wait_ge(S["b_v"], count - 1)
                        four(bank(VAL, g), lambda dst, b: nc.tensor.matmul(dst, hT1[:, g, b], w_vo[:],
                                                                           start=True, stop=True), S["b_vp"])
                    elif what == SCORE:
                        pe.wait_ge(S["b_q"], count)
                        if before or g > 1:
                            pe.wait_ge(S["b_s"], count - 2)
                        four(bank(SCORE, g), lambda dst, b: nc.tensor.matmul(dst, hmT[:, g, b], hT1[:, g, b],
                                                                             start=True, stop=True), S["b_sp"])
                    elif what == PT:
                        pe.wait_ge(S["b_e"], count)
                        four(bank(PT, g), lambda dst, b: nc.tensor.transpose(dst, prob[:, g, b], ident[:]),
                             S["b_pTp"])
                    elif what == OUT1:
                        pe.wait_ge(S["b_pT"], count)
                        pe.wait_ge(S["b_v"], count)
                        if before or g > 1:
                            pe.wait_ge(S["b_o"], count - 2)
                        four(bank(OUT1, g), lambda dst, b: nc.tensor.matmul(dst, probT[:, g, b], val[:, g, b],
                                                                            start=True, stop=True), S["b_op"])

                pipeline(pe, stage)

        part.close()

        part, tmp = scope()
        hr = tmp("hr2", [P, NB, C])
        z0 = tmp("z0", [P, W1, QB, T])
        z12 = tmp("z12", [P, W1, QB, 2, T])
        xb = tmp("xb", [P, NB, C])
        S = sync_names(nc, ctx, "c_stats c_aggr c_var c_rstd c_hn c_hr c_xb c_zp c_z0 c_z12 c_op c_o")
        NORM2 = {n: S["c_" + n] for n in ("stats", "aggr", "var", "rstd")}

        def one_behind(engine, spread, gather):
            def turn(i, first, last):
                for g in range(W1):
                    spread(i, g, not last, not first)
                    if g > 0:
                        gather(i, g - 1, not last, not first)
                    elif not first:
                        gather(i - 1, W1 - 1, True, True)

            turn(0, True, False)
            with engine.Fori(1, TURNS - 1) as i:
                turn(i, False, False)
            turn(TURNS - 1, False, True)
            gather(TURNS - 1, W1 - 1, False, True)

        with nc.Block() as block:
            @block.gpsimd
            def _(pool):
                def relu(i, g):
                    if not (isinstance(i, int) and i == 0):
                        wait_apart(pool, S["c_hn"], (i * W1 - W1 + g + 1) * QB)
                    nc.gpsimd.tensor_scalar(hr[:, g * QB:(g + 1) * QB], hn[:, g * QB:(g + 1) * QB], 0.0, None,
                                            ALU.max).then_inc(S["c_hr"], 1)

                def spread(i, g, more, before):
                    if before:
                        pool.wait_ge(S["c_o"], i * W1 - W1 + g + 1)
                    nc.gpsimd.tensor_tensor(xb[:, g * QB:(g + 1) * QB], x[:, bass.ds(i * NB + g * QB, QB), :],
                                            bias2_bc[:].unsqueeze(1).to_broadcast([P, QB, C]),
                                            ALU.add).then_inc(S["c_xb"], 1)
                    if more:
                        group_rstd(pool, NORM2, i * W1 + g, g)

                def gather(i, g, more, before):
                    if more:
                        relu(i + 1, g)

                for g in range(W1):
                    relu(0, g)
                one_behind(pool, spread, gather)

            @block.vector
            def _(dve):
                def spread(i, g, more, before):
                    dve.wait_ge(S["c_zp"], i * W1 + g + 1)
                    nc.vector.scalar_tensor_tensor(z0[:, g], by4(ps[:, 4 * (g % 2)]), 0.0,
                                                   diag_bc[:].unsqueeze(1).to_broadcast([P, QB, T]),
                                                   ALU.max, ALU.mult).then_inc(S["c_z0"], 1)
                    if more:
                        norm_stats((i + 1) * NB, g * QB, QB, S["c_stats"])

                def gather(i, g, more, before):
                    dve.wait_ge(S["c_xb"], i * W1 + g + 1)
                    dve.wait_ge(S["c_op"], i * W1 + g + 1)
                    nc.vector.tensor_tensor(x[:, bass.ds(i * NB + g * QB, QB), :], by4(ps[:, 4 * (g % 2) + 3]),
                                            xb[:, g * QB:(g + 1) * QB], ALU.add).then_inc(S["c_o"], 1)
                    if more:
                        dve.wait_ge(S["c_rstd"], i * W1 + g + 1)
                        norm_apply((i + 1) * NB, g * QB, QB, S["c_hn"])

                def aggr(i, g, more, before):
                    if more:
                        wait_apart(dve, S["c_stats"], i * NB + (g + 1) * QB)
                        norm_aggr(g * QB, QB, S["c_aggr"])

                def spread_and_aggr(i, g, more, before):
                    spread(i, g, more, before)
                    aggr(i, g, more, before)

                one_behind(dve, spread_and_aggr, gather)

            @block.scalar
            def _(act):
                with act.Fori(0, TURNS) as i:
                    for g in range(W1):
                        act.wait_ge(S["c_zp"], i * W1 + g + 1)
                        nc.scalar.activation(z12[:, g].rearrange("p b k t -> p (b k t)").rearrange(
                            "p (a n) -> p a n", a=2), ps[:, 4 * (g % 2) + 1:4 * (g % 2) + 3],
                                             ACT.Copy).then_inc(S["c_z12"], 1)

            @block.tensor
            def _(pe):
                def spread(i, g, more, before):
                    k = 4 * (g % 2)
                    pe.wait_ge(S["c_hr"], i * W1 + g + 1)
                    if before or g > 1:
                        pe.wait_ge(S["c_z0"], i * W1 + g - 1)
                        pe.wait_ge(S["c_z12"], i * W1 + g - 1)
                    for b in range(QB):
                        nc.tensor.transpose(ps[:, k, b * T:(b + 1) * T], hn[:, g * QB + b], ident[:])
                    for b in range(QB):
                        ins = nc.tensor.matmul(ps[:, k + 1 + b // 2, (b % 2) * 2 * T:(b % 2 + 1) * 2 * T],
                                               hr[:, g * QB + b], adj_ul[:].rearrange("p k t -> p (k t)"),
                                               start=True, stop=True)
                    ins.then_inc(S["c_zp"], 1)

                def gather(i, g, more, before):
                    k = 4 * (g % 2)
                    pe.wait_ge(S["c_z0"], i * W1 + g + 1)
                    pe.wait_ge(S["c_z12"], i * W1 + g + 1)
                    if before or g > 1:
                        pe.wait_ge(S["c_o"], i * W1 + g - 1)
                    for b in range(QB):
                        dst = ps[:, k + 3, b * C:(b + 1) * C]
                        nc.tensor.matmul(dst, z0[:, g, b], w2_sb[:, 0], start=True, stop=False)
                        nc.tensor.matmul(dst, z12[:, g, b, 0], w2_sb[:, 1], start=False, stop=False)
                        ins = nc.tensor.matmul(dst, z12[:, g, b, 1], w2_sb[:, 2], start=False, stop=True)
                    ins.then_inc(S["c_op"], 1)

                one_behind(pe, spread, gather)

        part.close()

        part, tmp = scope()
        NG = B // QB
        HB = QB // 2
        NV = 1
        GH = QB * HEADS
        BH = B * HEADS // P
        xv = tmp("xv", [P, B, C])
        hT_hi = tmp("hT_hi", [P, QB, T], F32R)
        hT_lo = tmp("hT_lo", [P, QB, T], F32R)
        rl = tmp("rl", [P, 2, 512])
        xq_hi = tmp("xq_hi", [P, QB, C], F32R)
        xq_lo = tmp("xq_lo", [P, QB, C], F32R)
        lr = tmp("lr", [P, QB, E])
        lg = tmp("lg", [P, EC, B * HEADS])
        S = sync_names(nc, ctx, "d_stats d_aggr d_var d_rstd d_nmean d_shift d_hns d_hnv d_hTp d_hTh d_hTl d_xp "
                                "d_xqh d_xql d_xv d_zp d_rl d_lr d_lgp d_lg")

        def part_of_x(k):
            return ps[:, 1:3].rearrange("p a (b k c) -> p a b k c", b=2, k=2)[:, :, :, k]

        def by22(buf):
            return buf[:].rearrange("p (a b) c -> p a b c", a=2)

        with nc.Block() as block:
            def steps_of(engine, step):
                step(0, False, 3)
                step(1, True, 3)
                with engine.Fori(2, NG - 3) as n:
                    step(n, True, 3)
                for n in range(NG - 3, NG):
                    step(n, True, NG - 1 - n)

            @block.gpsimd
            def _(pool):
                def scale_and_shift(n, before):
                    wait_apart(pool, S["d_aggr"], n * QB + QB)
                    if before:
                        wait_apart(pool, S["d_hns"], n * (QB - NV))
                        wait_apart(pool, S["d_hnv"], n * NV)
                    nc.gpsimd.tensor_scalar(rstd[:, 0:QB], mv[:, 0:QB, 1], EPS, None, ALU.add).then_inc(S["d_var"], 1)
                    nc.gpsimd.tensor_scalar(shift[:, 0:QB], mv[:, 0:QB, 0], -1.0, None, ALU.mult).then_inc(
                        S["d_nmean"], 1)
                    pool.wait_ge(S["d_var"], n + 1)
                    nc.gpsimd.tensor_tensor(rstd[:, 0:QB], rstd[:, 0:QB], half[:, 0:QB], ALU.pow).then_inc(
                        S["d_rstd"], 1)
                    pool.wait_ge(S["d_nmean"], n + 1)
                    pool.wait_ge(S["d_rstd"], n + 1)
                    nc.gpsimd.tensor_tensor(shift[:, 0:QB], shift[:, 0:QB], rstd[:, 0:QB], ALU.mult).then_inc(
                        S["d_shift"], 1)

                scale_and_shift(0, False)
                with pool.Fori(1, NG) as n:
                    scale_and_shift(n, True)

            @block.vector
            def _(dve):
                def norm_sums(n, before=True, between=None):
                    norm_stats(n * QB, 0, QB, S["d_stats"])
                    if between:
                        between()
                    wait_apart(dve, S["d_stats"], n * QB + QB)
                    if before:
                        wait_apart(dve, S["d_shift"], n)
                    norm_aggr(0, QB, S["d_aggr"])

                def normalise(n, before=True):
                    dve.wait_ge(S["d_shift"], n + 1)
                    if before:
                        dve.wait_ge(S["d_hTp"], n)
                    for j in range(NV):
                        nc.vector.tensor_scalar(hn[:, j], x[:, bass.ds(n * QB + j, 1), :].rearrange("p a c -> p (a c)"),
                                                rstd[:, j:j + 1], shift[:, j:j + 1], ALU.mult, ALU.add).then_inc(
                                                    S["d_hnv"], 1)

                def low_hT(n):
                    dve.wait_ge(S["d_hTh"], n + 1)
                    nc.vector.scalar_tensor_tensor(hT_lo[:], by4(ps[:, 0]), 0.0, hT_hi[:].bitcast(F32),
                                                   ALU.max, ALU.subtract).then_inc(S["d_hTl"], 1)

                def step(n, before, more):
                    dve.wait_ge(S["d_xqh"], n + 1)
                    nc.vector.tensor_tensor(by22(xq_lo), part_of_x(0), by22(xq_hi).bitcast(F32),
                                            ALU.subtract).then_inc(S["d_xql"], 1)
                    if more > 0:
                        low_hT(n + 1)
                    if more > 1:
                        normalise(n + 2)
                    if more == 3:
                        norm_sums(n + 3, between=(lambda: add_log(n - 1)) if before else None)
                    elif before:
                        add_log(n - 1)
                    for k in range(2):
                        dve.wait_ge(S["d_rl"], n * 2 + k + 1)
                        nc.vector.scalar_tensor_tensor(
                            lr[:, 2 * k:2 * k + 2].rearrange("p b e -> p (b e)"), ps[:, 3 + k], SLOPE, rl[:, k],
                            ALU.mult, ALU.add).then_inc(S["d_lr"], 1)
                def add_log(n):
                    dve.wait_ge(S["d_lgp"], n + 1)
                    nc.vector.tensor_tensor(lg[:, :, bass.ds(n * GH, GH)],
                                            ps[:, 5, 0:EC * GH].rearrange("p (c m) -> p c m", c=EC),
                                            log_a[:].unsqueeze(2).to_broadcast([P, EC, GH]), ALU.add).then_inc(
                                                S["d_lg"], 1)

                norm_sums(0, before=False)
                normalise(0, False)
                norm_sums(1)
                low_hT(0)
                normalise(1)
                norm_sums(2)
                steps_of(dve, step)
                add_log(NG - 1)

            @block.scalar
            def _(act):
                def relu_norm(n, before=True):
                    act.wait_ge(S["d_shift"], n + 1)
                    if before:
                        act.wait_ge(S["d_hTp"], n)
                    for j in range(NV, QB):
                        nc.scalar.activation(hn[:, j], x[:, bass.ds(n * QB + j, 1), :].rearrange("p a c -> p (a c)"),
                                             ACT.Relu, bias=shift[:, j:j + 1], scale=rstd[:, j:j + 1]).then_inc(
                                                 S["d_hns"], 1)

                def high_hT(n):
                    act.wait_ge(S["d_hTp"], n + 1)
                    nc.scalar.activation(hT_hi[:], by4(ps[:, 0]), ACT.Relu).then_inc(S["d_hTh"], 1)

                def step(n, before, more):
                    act.wait_ge(S["d_xp"], n + 1)
                    nc.scalar.activation(by22(xq_hi), part_of_x(0), ACT.Copy).then_inc(S["d_xqh"], 1)
                    if more > 0:
                        high_hT(n + 1)
                    if more > 1:
                        relu_norm(n + 2)
                    act.wait_ge(S["d_xql"], n + 1)
                    nc.scalar.activation(xv[:, bass.ds(n * QB, QB), :].rearrange("p (k b) c -> p k b c", k=2),
                                         part_of_x(1), ACT.Copy).then_inc(S["d_xv"], 1)
                    for k in range(2):
                        act.wait_ge(S["d_zp"], n * 2 + k + 1)
                        if k == 0 and before:
                            act.wait_ge(S["d_lr"], n * 2)
                        nc.scalar.activation(rl[:, k], ps[:, 3 + k], ACT.Relu, scale=1.0 - SLOPE).then_inc(
                            S["d_rl"], 1)

                relu_norm(0, False)
                high_hT(0)
                relu_norm(1)
                steps_of(act, step)

            @block.tensor
            def _(pe):
                def transpose(n):
                    pe.wait_ge(S["d_hnv"], (n + 1) * NV)
                    pe.wait_ge(S["d_hns"], (n + 1) * (QB - NV))
                    for b in range(QB):
                        ins = nc.tensor.transpose(ps[:, 0, b * T:(b + 1) * T], hn[:, b], ident[:])
                    ins.then_inc(S["d_hTp"], 1)

                def logits(n, before=True):
                    if before:
                        pe.wait_ge(S["d_lg"], n)
                    pe.wait_ge(S["d_lr"], n * 2 + 2)
                    for b in range(QB):
                        for c in range(EC):
                            col = c * GH + b * HEADS
                            ins = nc.tensor.matmul(ps[:, 5, col:col + HEADS], lr[:, b, c * P:(c + 1) * P], a_blk[:],
                                                   start=True, stop=True)
                    ins.then_inc(S["d_lgp"], 1)

                def step(n, before, more):
                    pe.wait_ge(S["d_hTh"], n + 1)
                    pe.wait_ge(S["d_hTl"], n + 1)
                    if before:
                        pe.wait_ge(S["d_xv"], n)
                    for b in range(QB):
                        dst = ps[:, 1 + b // 2, (b % 2) * 2 * C:(b % 2 + 1) * 2 * C]
                        nc.tensor.matmul(dst, hT_hi[:, b], lv_hi[:], start=True, stop=False)
                        nc.tensor.matmul(dst, hT_hi[:, b], lv_lo[:], start=False, stop=False)
                        ins = nc.tensor.matmul(dst, hT_lo[:, b], lv_hi[:], start=False, stop=True)
                    ins.then_inc(S["d_xp"], 1)
                    if more > 0:
                        transpose(n + 1)
                    if before:
                        logits(n - 1, not (isinstance(n, int) and n == 1))
                    pe.wait_ge(S["d_xqh"], n + 1)
                    pe.wait_ge(S["d_xql"], n + 1)
                    for k in range(2):
                        for b in range(2):
                            dst = ps[:, 3 + k, b * E:(b + 1) * E]
                            nc.tensor.matmul(dst, xq_hi[:, 2 * k + b], hot_sd[:], start=True, stop=False)
                            ins = nc.tensor.matmul(dst, xq_lo[:, 2 * k + b], hot_sd[:], start=False, stop=True)
                        ins.then_inc(S["d_zp"], 1)

                transpose(0)
                steps_of(pe, step)
                logits(NG - 1)

        fwd = tmp("fwd", [P, BH, E])
        bwd = tmp("bwd", [P, BH, E])
        expT = tmp("expT", [P, BH, E])
        ex = tmp("ex", [P, EC, B * HEADS])
        att = tmp("att", [P, EC, B * HEADS])
        xv_hi = tmp("xv_hi", [P, QB * C], F32R)
        xv_lo = tmp("xv_lo", [P, QB * C], F32R)
        va = tmp("va", [P, EC, QB, C])
        y3 = tmp("y3", [P, QB, T])
        S = sync_names(nc, ctx, "e_lgTp e_fb e_m e_sub e_exp e_exTp e_ex e_denp e_inv e_att e_xvh e_xvl e_vp e_va "
                                "e_yp e_y e_op e_o e_st")
        with nc.Block() as block:
            @block.sync
            def _(sp):
                with sp.Fori(0, NG) as n:
                    sp.wait_ge(S["e_o"], n + 1)
                    sp.dma_start(out[bass.ds(n * QB, QB)].rearrange("b t c -> t b c"),
                                 x[:, bass.ds(n * QB, QB), :]).then_inc(S["e_st"], 16)
                sp.wait_ge(S["e_st"], 16 * NG)

            @block.gpsimd
            def _(pool):
                def low_values(n):
                    pool.wait_ge(S["e_xvh"], n + 1)
                    nc.gpsimd.tensor_tensor(xv_lo[:], xv[:, bass.ds(n * QB, QB), :].rearrange("p b c -> p (b c)"),
                                            xv_hi[:].bitcast(F32), ALU.subtract).then_inc(S["e_xvl"], 1)

                with pool.Fori(0, NG) as n:
                    low_values(n)

            @block.vector
            def _(dve):
                for s in range(BH):
                    src = ps[:, s, 0:E]
                    dve.wait_ge(S["e_lgTp"], s + 1)
                    nc.vector.tensor_tensor_scan(fwd[:, s], cut_f[:], src, 0.0, ALU.add, ALU.max).then_inc(
                        S["e_fb"], 1)
                    nc.vector.tensor_tensor_scan(bwd[:, s, ::-1], cut_b[:, ::-1], src[:, ::-1], 0.0, ALU.add,
                                                 ALU.max).then_inc(S["e_fb"], 1)
                    dve.wait_ge(S["e_fb"], 2 * s + 2)
                    nc.vector.tensor_tensor(fwd[:, s], fwd[:, s], bwd[:, s], ALU.max).then_inc(S["e_m"], 1)
                    dve.wait_ge(S["e_m"], s + 1)
                    nc.vector.tensor_tensor(bwd[:, s], src, fwd[:, s], ALU.subtract).then_inc(S["e_sub"], 1)
                for c in range(EC):
                    dve.wait_ge(S["e_exTp"], BH)
                    nc.vector.tensor_copy(ex[:, c], ps[:, 4 + c]).then_inc(S["e_ex"], 1)
                dve.wait_ge(S["e_denp"], 1)

                def attention(n):
                    cols = bass.ds(n * GH, GH)
                    nc.vector.reciprocal(att[:, :, cols], ps[:, 2:2 + EC, cols]).then_inc(S["e_inv"], 1)
                    dve.wait_ge(S["e_inv"], n + 1)
                    nc.vector.tensor_tensor(att[:, :, cols], att[:, :, cols], ex[:, :, cols], ALU.mult).then_inc(
                        S["e_att"], 1)

                def weigh(n):
                    dve.wait_ge(S["e_att"], n + 1)
                    for k in range(2):
                        for c in range(EC):
                            if k == 0:
                                dve.wait_ge(S["e_vp"], n * EC + c + 1)
                            nc.vector.tensor_tensor(
                                va[:, c, k * HB:(k + 1) * HB].rearrange("p b (h d) -> p (b h) d", h=HEADS),
                                ps[:, c, k * HB * C:(k + 1) * HB * C].rearrange("p (n d) -> p n d", d=DH),
                                att[:, c, bass.ds(n * GH + k * HB * HEADS, HB * HEADS)].unsqueeze(2).to_broadcast(
                                    [P, HB * HEADS, DH]),
                                ALU.mult).then_inc(S["e_va"], 1)

                def finish(n):
                    xs = x[:, bass.ds(n * QB, QB), :]
                    dve.wait_ge(S["e_op"], n + 1)
                    nc.vector.tensor_tensor(xs, xs, by4(ps[:, 7]), ALU.add).then_inc(S["e_o"], 1)

                attention(0)
                weigh(0)
                with dve.Fori(0, NG - 1) as n:
                    attention(n + 1)
                    weigh(n + 1)
                    finish(n)
                finish(NG - 1)

            @block.scalar
            def _(act):
                def high_values(n, before):
                    if before:
                        act.wait_ge(S["e_vp"], n * EC)
                        act.wait_ge(S["e_xvl"], n)
                    nc.scalar.activation(xv_hi[:], xv[:, bass.ds(n * QB, QB), :].rearrange("p b c -> p (b c)"),
                                         ACT.Copy).then_inc(S["e_xvh"], 1)

                def copy_y(n):
                    act.wait_ge(S["e_yp"], n + 1)
                    nc.scalar.activation(y3[:], by4(ps[:, 6]), ACT.Copy).then_inc(S["e_y"], 1)

                high_values(0, False)
                for s in range(BH):
                    act.wait_ge(S["e_sub"], s + 1)
                    nc.scalar.activation(expT[:, s], bwd[:, s], ACT.Exp).then_inc(S["e_exp"], 1)
                high_values(1, True)
                with act.Fori(0, NG - 2) as n:
                    copy_y(n)
                    high_values(n + 2, True)
                copy_y(NG - 2)
                copy_y(NG - 1)

            @block.tensor
            def _(pe):
                for s in range(BH):
                    for c in range(EC):
                        ins = nc.tensor.transpose(ps[:, s, c * P:(c + 1) * P],
                                                  lg[:, c, s * P:(s + 1) * P], ident[:])
                    ins.then_inc(S["e_lgTp"], 1)
                for s in range(BH):
                    pe.wait_ge(S["e_exp"], s + 1)
                    for c in range(EC):
                        ins = nc.tensor.transpose(ps[:, 4 + c, s * P:(s + 1) * P], expT[:, s, c * P:(c + 1) * P],
                                                  ident[:])
                    ins.then_inc(S["e_exTp"], 1)
                pe.wait_ge(S["e_ex"], EC)
                for c in range(EC):
                    for k in range(EC):
                        ins = nc.tensor.matmul(ps[:, 2 + c], same[:, k, c * P:(c + 1) * P], ex[:, k],
                                               start=(k == 0), stop=(k == EC - 1))
                ins.then_inc(S["e_denp"], 1)

                def values(n):
                    pe.wait_ge(S["e_xvh"], n + 1)
                    pe.wait_ge(S["e_xvl"], n + 1)
                    for c in range(EC):
                        nc.tensor.matmul(ps[:, c], hot_d[:, c * P:(c + 1) * P], xv_hi[:], start=True, stop=False)
                        nc.tensor.matmul(ps[:, c], hot_d[:, c * P:(c + 1) * P], xv_lo[:], start=False,
                                         stop=True).then_inc(S["e_vp"], 1)

                def aggregate(n):
                    for b in range(QB):
                        if b % HB == 0:
                            pe.wait_ge(S["e_va"], (2 * n + b // HB + 1) * EC)
                        for c in range(EC):
                            ins = nc.tensor.matmul(ps[:, 6, b * T:(b + 1) * T], va[:, c, b], hot_sT[:, c],
                                                   start=(c == 0), stop=(c == EC - 1))
                    ins.then_inc(S["e_yp"], 1)

                def project(n, before):
                    pe.wait_ge(S["e_y"], n + 1)
                    if before:
                        pe.wait_ge(S["e_o"], n)
                    for b in range(QB):
                        ins = nc.tensor.matmul(ps[:, 7, b * C:(b + 1) * C], y3[:, b], w_out[:], start=True, stop=True)
                    ins.then_inc(S["e_op"], 1)

                values(0)
                aggregate(0)
                values(1)
                project(0, False)
                with pe.Fori(1, NG - 1) as n:
                    aggregate(n)
                    values(n + 1)
                    project(n, True)
                aggregate(NG - 1)
                project(NG - 1, True)


def kernel(x, adj, L0_gnn_Wg0, L0_gnn_bg0, L0_gnn_Wg1, L0_gnn_bg1, L0_gnn_Wih, L0_gnn_Whh, L0_gnn_bih, L0_gnn_bhh,
           L1_gnn_Wqkv, L1_gnn_Wo, L2_gnn_W, L2_gnn_bias, L3_gnn_W_lin, L3_gnn_W_val, L3_gnn_a, L3_gnn_W_out,
           L3_gnn_src, L3_gnn_dst):
    import numpy as np
    import concourse.bacc as bacc
    from concourse.bass_utils import run_bass_kernel_spmd

    def lay(a):
        return np.ascontiguousarray(a)

    skips, gates, hid = L0_gnn_Wih.shape
    a_rep = np.broadcast_to(np.asarray(L3_gnn_a).reshape(-1, 1), (L3_gnn_a.size, L3_gnn_a.shape[0]))
    laid = {
        "x_in": x, "adj": adj, "adjT": np.asarray(adj).T,
        "Wg0": L0_gnn_Wg0, "bg0": np.asarray(L0_gnn_bg0)[:, None],
        "Wg1": L0_gnn_Wg1, "bg1": np.asarray(L0_gnn_bg1)[None, :],
        "WihT": np.asarray(L0_gnn_Wih).reshape(skips * gates, hid).T,
        "WhhT": np.asarray(L0_gnn_Whh).reshape(skips * gates, hid).T,
        "bihT": np.asarray(L0_gnn_bih).reshape(-1, hid).T, "bhhT": np.asarray(L0_gnn_bhh).reshape(-1, hid).T,
        "WqkvT": np.asarray(L1_gnn_Wqkv).T, "Wo": L1_gnn_Wo,
        "W2": L2_gnn_W, "bias2": np.asarray(L2_gnn_bias)[None, :],
        "WlvT": np.concatenate([np.asarray(L3_gnn_W_lin).T, np.asarray(L3_gnn_W_val).T], axis=1),
        "a_col": a_rep, "WoutT": np.asarray(L3_gnn_W_out).T,
        "src_row": np.asarray(L3_gnn_src)[None, :], "src_col": np.asarray(L3_gnn_src).reshape(-1, 128).T,
        "dst_row": np.asarray(L3_gnn_dst)[None, :], "dst_col": np.asarray(L3_gnn_dst).reshape(-1, 128).T,
    }
    nc = bacc.Bacc("TRN2", target_bir_lowering=False, num_devices=1)
    arrays, args = {}, {}
    for name, a in laid.items():
        a = lay(a)
        arrays[f"in_{name}"] = a
        args[name] = nc.dram_tensor(f"in_{name}", a.shape, mybir.dt.from_np(a.dtype), kind="ExternalInput").ap()
    out = nc.dram_tensor("out", x.shape, F32, kind="ExternalOutput").ap()
    four_layers(nc, out=out, **args)
    return run_bass_kernel_spmd(nc, [arrays], core_ids=[0]).results[0]["out"]
```
